# Optimizing a Trainium2 kernel written in Bass

```python
import numpy as np
import jax
import jax.numpy as jnp

def _softmax(x, axis=-1):
    return jax.nn.softmax(x, axis=axis)

def _gelu(x):
    return jax.nn.gelu(x, approximate=True)

def _silu(x):
    return jax.nn.silu(x)

def _sigmoid(x):
    return jax.nn.sigmoid(x)

def _layernorm(x, axis=-1, eps=1e-05):
    m = jnp.mean(x, axis=axis, keepdims=True)
    v = jnp.var(x, axis=axis, keepdims=True)
    return (x - m) / jnp.sqrt(v + eps)

def _scatter_add(tgt, idx, src, axis=0):
    return tgt.at[idx].add(src)

def _segment_sum(src, seg, n):
    return jax.ops.segment_sum(src, seg, n)
kernel_name = 'mk_adaln_attn_ffn_d1_seqx_r4_9855e8'

def setup_inputs(seed: int=0):
    np.random.seed(seed)
    _w = jnp.asarray

    def _rec_inputs():
        import jax
        import jax.numpy as jnp
        _rk = jax.random.key(seed)
        x = -0.000125 + 0.9999 * jax.random.normal(jax.random.fold_in(_rk, 1), (2, 1024, 256), jnp.float32)
        _lenS = 1024 - jax.random.randint(jax.random.fold_in(_rk, 7), (2,), 0, max(1, 1024 // 4) + 1, jnp.int32)
        _lenS2 = 1024 - jax.random.randint(jax.random.fold_in(_rk, 8), (2,), 0, max(1, 1024 // 4) + 1, jnp.int32)
        cond_1024 = -0.00493535 + 1.00056 * jax.random.normal(jax.random.fold_in(_rk, 11), (2, 256), jnp.float32)
        return (x, cond_1024)
    x, cond_1024 = _rec_inputs()

    def _L0_cond_setup():
        import jax, jax.numpy as jnp
        import numpy as np
        import math
        N, T, D, H = (64, 128, 256, 256)
        key = jax.random.key(seed)
        k1, k2, k3, k4 = jax.random.split(key, 4)
        x = jax.random.normal(k1, (N, T, D), dtype=jnp.float32)
        h0 = jax.random.normal(k2, (N, H), dtype=jnp.float32)
        Wx = jax.random.normal(k3, (D, 4 * H), dtype=jnp.float32) / math.sqrt(D)
        Wh = jax.random.normal(k4, (H, 4 * H), dtype=jnp.float32) / math.sqrt(H)
        b = jnp.zeros((4 * H,), dtype=jnp.float32)
        return {'x': x, 'h0': h0, 'Wx': Wx, 'Wh': Wh, 'b': b}
    _L0_cond_all = _L0_cond_setup()
    _L0_cond_in = {k: v for k, v in _L0_cond_all.items() if k in ('Wx', 'Wh', 'b')}
    del _L0_cond_all

    def _L0_attn_setup():
        import jax, jax.numpy as jnp
        import numpy as np
        from jax import lax
        D_MODEL = 256
        D_STATE = 16
        D_CONV = 4
        EXPAND = 2
        D_INNER = D_MODEL * EXPAND
        B_SZ = 2
        T_LEN = 512
        EPS = 1e-06

        def _rmsnorm(x, w):
            rms = jnp.sqrt(jnp.mean(x * x, axis=-1, keepdims=True) + EPS)
            return x / rms * w

        def _causal_depthwise_conv(x, conv_w, conv_b):
            xp = jnp.pad(x, ((0, 0), (0, 0), (D_CONV - 1, 0)))
            y = lax.conv_general_dilated(xp, conv_w, window_strides=(1,), padding='VALID', dimension_numbers=('NCH', 'OIH', 'NCH'), feature_group_count=D_INNER)
            return y + conv_b[None, :, None]

        def _mamba_forward(x, norm_w, W_in, conv_w, conv_b, W_x, w_dt, b_dt, A_log, D_param, W_out):
            residual = x
            xn = _rmsnorm(x, norm_w)
            xz = xn @ W_in
            x_proj, z = jnp.split(xz, 2, axis=-1)
            xc = _causal_depthwise_conv(jnp.swapaxes(x_proj, 1, 2), conv_w, conv_b)
            xc = jnp.swapaxes(xc, 1, 2)
            xc = jax.nn.silu(xc)
            ssm_params = xc @ W_x
            dt_raw = ssm_params[..., 0:1]
            Bp = ssm_params[..., 1:1 + D_STATE]
            Cp = ssm_params[..., 1 + D_STATE:]
            dt = jax.nn.softplus(dt_raw * w_dt + b_dt)
            A = -jnp.exp(A_log)
            A_bar = jnp.exp(dt[..., None] * A)
            Bx = dt[..., None] * Bp[:, :, None, :] * xc[..., None]
            A_t = jnp.swapaxes(A_bar, 0, 1)
            Bx_t = jnp.swapaxes(Bx, 0, 1)
            C_t = jnp.swapaxes(Cp, 0, 1)

            def step(h, inp):
                a, bx, c = inp
                h = a * h + bx
                y = jnp.sum(h * c[:, None, :], axis=-1)
                return (h, y)
            h0 = jnp.zeros((x.shape[0], D_INNER, D_STATE), dtype=x.dtype)
            _, ys = lax.scan(step, h0, (A_t, Bx_t, C_t))
            y = jnp.swapaxes(ys, 0, 1)
            y = y + xc * D_param
            y = y * jax.nn.silu(z)
            return y @ W_out + residual
        key = jax.random.key(seed)
        ks = jax.random.split(key, 10)
        x = jax.random.normal(ks[0], (B_SZ, T_LEN, D_MODEL), dtype=jnp.float32)
        norm_w = jnp.ones((D_MODEL,), dtype=jnp.float32)
        W_in = jax.random.normal(ks[1], (D_MODEL, 2 * D_INNER), dtype=jnp.float32) * D_MODEL ** (-0.5)
        conv_w = jax.random.normal(ks[2], (D_INNER, 1, D_CONV), dtype=jnp.float32) * D_CONV ** (-0.5)
        conv_b = jnp.zeros((D_INNER,), dtype=jnp.float32)
        W_x = jax.random.normal(ks[3], (D_INNER, 2 * D_STATE + 1), dtype=jnp.float32) * D_INNER ** (-0.5)
        w_dt = jax.random.normal(ks[4], (D_INNER,), dtype=jnp.float32)
        b_dt = jax.random.uniform(ks[5], (D_INNER,), dtype=jnp.float32, minval=-0.001, maxval=0.001)
        A_log = jnp.log(jnp.arange(1, D_STATE + 1, dtype=jnp.float32))[None, :] * jnp.ones((D_INNER, 1), dtype=jnp.float32)
        D_param = jnp.ones((D_INNER,), dtype=jnp.float32)
        W_out = jax.random.normal(ks[6], (D_INNER, D_MODEL), dtype=jnp.float32) * D_INNER ** (-0.5)
        return {'x': x, 'norm_w': norm_w, 'W_in': W_in, 'conv_w': conv_w, 'conv_b': conv_b, 'W_x': W_x, 'w_dt': w_dt, 'b_dt': b_dt, 'A_log': A_log, 'D_param': D_param, 'W_out': W_out}
    _L0_attn_all = _L0_attn_setup()
    _L0_attn_in = {k: v for k, v in _L0_attn_all.items() if k in ('norm_w', 'W_in', 'conv_w', 'conv_b', 'W_x', 'w_dt', 'b_dt', 'A_log', 'D_param', 'W_out')}
    del _L0_attn_all

    def _L0_cond2_setup():
        import math
        import jax, jax.numpy as jnp
        import numpy as np
        EPS = 1e-07
        MAX_TANH_ARG = 1.0 - 1e-05

        def _norm(x):
            return jnp.sqrt(jnp.sum(x * x, axis=-1, keepdims=True)).clip(EPS)

        def logmap0(x):
            n = _norm(x)
            return jnp.arctanh(jnp.clip(n, EPS, MAX_TANH_ARG)) * x / n

        def expmap0(v):
            n = _norm(v)
            return jnp.tanh(n) * v / n

        def mobius_add(x, y):
            x2 = jnp.sum(x * x, -1, keepdims=True)
            y2 = jnp.sum(y * y, -1, keepdims=True)
            xy = jnp.sum(x * y, -1, keepdims=True)
            num = (1 + 2 * xy + y2) * x + (1 - x2) * y
            den = (1 + 2 * xy + x2 * y2).clip(EPS)
            return num / den

        def plin(x, w, b):
            return expmap0(logmap0(x) @ w + b)

        def layer_norm(x, eps=1e-06):
            m = x.mean(-1, keepdims=True)
            v = ((x - m) ** 2).mean(-1, keepdims=True)
            return (x - m) / jnp.sqrt(v + eps)

        def _beta(a, b):
            return math.exp(math.lgamma(a) + math.lgamma(b) - math.lgamma(a + b))
        D, H, FF = (256, 16, 1024)
        HD = D // H
        BETA_N = _beta(D / 2, 0.5)
        BETA_H = _beta(HD / 2, 0.5)

        def _to_heads(p):
            B, S, _ = p.shape
            t = logmap0(p).reshape(B, S, H, HD) * (BETA_H / BETA_N)
            return expmap0(jnp.transpose(t, (0, 2, 1, 3)))

        def _from_heads(ph):
            B, _, S, _ = ph.shape
            t = logmap0(ph) * (BETA_N / BETA_H)
            t = jnp.transpose(t, (0, 2, 1, 3)).reshape(B, S, D)
            return expmap0(t)
        key = jax.random.key(seed)
        ks = jax.random.split(key, 20)
        B, S = (4, 256)
        x = expmap0(0.02 * jax.random.normal(ks[0], (B, S, D), jnp.float32))
        t_emb = jax.random.normal(ks[1], (B, 1, D), jnp.float32)
        g = lambda k, sh: 0.02 * jax.random.normal(k, sh, jnp.float32)
        return {'x': x, 't_emb': t_emb, 'w_q': g(ks[2], (D, D)), 'b_q': jnp.zeros((D,), jnp.float32), 'w_k': g(ks[3], (D, D)), 'b_k': jnp.zeros((D,), jnp.float32), 'w_v': g(ks[4], (D, D)), 'b_v': jnp.zeros((D,), jnp.float32), 'w_o': g(ks[5], (D, D)), 'b_o': jnp.zeros((D,), jnp.float32), 'w_f1': g(ks[6], (D, FF)), 'b_f1': jnp.zeros((FF,), jnp.float32), 'w_f2': g(ks[7], (FF, D)), 'b_f2': jnp.zeros((D,), jnp.float32), 'w_ada': g(ks[8], (D, 6 * D)), 'b_ada': jnp.zeros((6 * D,), jnp.float32)}
    _L0_cond2_all = _L0_cond2_setup()
    _L0_cond2_in = {k: v for k, v in _L0_cond2_all.items() if k in ('w_q', 'b_q', 'w_k', 'b_k', 'w_v', 'b_v', 'w_o', 'b_o', 'w_f1', 'b_f1', 'w_f2', 'b_f2', 'w_ada', 'b_ada')}
    del _L0_cond2_all

    def _L0_ffn_setup():
        import jax, jax.numpy as jnp
        import numpy as np
        D_IN, D_HID = (256, 1024)

        def _ternary(key, shape):
            return jax.random.randint(key, shape, -1, 2).astype(jnp.float32)

        def _tlin(x, w, s):
            return jnp.einsum('bsi,oi->bso', x, w) * s
        key = jax.random.key(seed)
        ks = jax.random.split(key, 12)
        inv = lambda fan: 1.0 / np.sqrt(fan).astype(np.float32)
        return {'x': jax.random.normal(ks[0], (4, 512, D_IN), dtype=jnp.float32), 'w1_w': _ternary(ks[1], (D_HID, D_IN)), 'w1_s': jax.random.uniform(ks[2], (D_HID,), dtype=jnp.float32) * inv(D_IN), 'w2_w': _ternary(ks[3], (D_HID, D_IN)), 'w2_s': jax.random.uniform(ks[4], (D_HID,), dtype=jnp.float32) * inv(D_IN), 'h1_w': _ternary(ks[5], (D_HID, D_HID)), 'h1_s': jax.random.uniform(ks[6], (D_HID,), dtype=jnp.float32) * inv(D_HID), 'h2_w': _ternary(ks[7], (D_HID, D_HID)), 'h2_s': jax.random.uniform(ks[8], (D_HID,), dtype=jnp.float32) * inv(D_HID), 'w3_w': _ternary(ks[9], (D_IN, D_HID)), 'w3_s': jax.random.uniform(ks[10], (D_IN,), dtype=jnp.float32) * inv(D_HID)}
    _L0_ffn_all = _L0_ffn_setup()
    _L0_ffn_in = {k: v for k, v in _L0_ffn_all.items() if k in ('w1_w', 'w1_s', 'w2_w', 'w2_s', 'h1_w', 'h1_s', 'h2_w', 'h2_s', 'w3_w', 'w3_s')}
    del _L0_ffn_all
    return {'x': x, 'cond_1024': cond_1024, 'L0_cond_Wx': _L0_cond_in['Wx'], 'L0_cond_Wh': _L0_cond_in['Wh'], 'L0_cond_b': _L0_cond_in['b'], 'L0_attn_norm_w': _L0_attn_in['norm_w'], 'L0_attn_W_in': _L0_attn_in['W_in'], 'L0_attn_conv_w': _L0_attn_in['conv_w'], 'L0_attn_conv_b': _L0_attn_in['conv_b'], 'L0_attn_W_x': _L0_attn_in['W_x'], 'L0_attn_w_dt': _L0_attn_in['w_dt'], 'L0_attn_b_dt': _L0_attn_in['b_dt'], 'L0_attn_A_log': _L0_attn_in['A_log'], 'L0_attn_D_param': _L0_attn_in['D_param'], 'L0_attn_W_out': _L0_attn_in['W_out'], 'L0_cond2_w_q': _L0_cond2_in['w_q'], 'L0_cond2_b_q': _L0_cond2_in['b_q'], 'L0_cond2_w_k': _L0_cond2_in['w_k'], 'L0_cond2_b_k': _L0_cond2_in['b_k'], 'L0_cond2_w_v': _L0_cond2_in['w_v'], 'L0_cond2_b_v': _L0_cond2_in['b_v'], 'L0_cond2_w_o': _L0_cond2_in['w_o'], 'L0_cond2_b_o': _L0_cond2_in['b_o'], 'L0_cond2_w_f1': _L0_cond2_in['w_f1'], 'L0_cond2_b_f1': _L0_cond2_in['b_f1'], 'L0_cond2_w_f2': _L0_cond2_in['w_f2'], 'L0_cond2_b_f2': _L0_cond2_in['b_f2'], 'L0_cond2_w_ada': _L0_cond2_in['w_ada'], 'L0_cond2_b_ada': _L0_cond2_in['b_ada'], 'L0_ffn_w1_w': _L0_ffn_in['w1_w'], 'L0_ffn_w1_s': _L0_ffn_in['w1_s'], 'L0_ffn_w2_w': _L0_ffn_in['w2_w'], 'L0_ffn_w2_s': _L0_ffn_in['w2_s'], 'L0_ffn_h1_w': _L0_ffn_in['h1_w'], 'L0_ffn_h1_s': _L0_ffn_in['h1_s'], 'L0_ffn_h2_w': _L0_ffn_in['h2_w'], 'L0_ffn_h2_s': _L0_ffn_in['h2_s'], 'L0_ffn_w3_w': _L0_ffn_in['w3_w'], 'L0_ffn_w3_s': _L0_ffn_in['w3_s']}

def reference(x, cond_1024, L0_cond_Wx, L0_cond_Wh, L0_cond_b, L0_attn_norm_w, L0_attn_W_in, L0_attn_conv_w, L0_attn_conv_b, L0_attn_W_x, L0_attn_w_dt, L0_attn_b_dt, L0_attn_A_log, L0_attn_D_param, L0_attn_W_out, L0_cond2_w_q, L0_cond2_b_q, L0_cond2_w_k, L0_cond2_b_k, L0_cond2_w_v, L0_cond2_b_v, L0_cond2_w_o, L0_cond2_b_o, L0_cond2_w_f1, L0_cond2_b_f1, L0_cond2_w_f2, L0_cond2_b_f2, L0_cond2_w_ada, L0_cond2_b_ada, L0_ffn_w1_w, L0_ffn_w1_s, L0_ffn_w2_w, L0_ffn_w2_s, L0_ffn_h1_w, L0_ffn_h1_s, L0_ffn_h2_w, L0_ffn_h2_s, L0_ffn_w3_w, L0_ffn_w3_s):
    import jax
    import jax.numpy as jnp

    def _L0_cond_ref(x, h0, Wx, Wh, b):
        import jax, jax.numpy as jnp
        import numpy as np
        import math
        N, T, D, H = (64, 128, 256, 256)
        Hdim = h0.shape[1]
        xW = jnp.einsum('ntd,dg->ntg', x, Wx) + b

        def step(carry, xw_t):
            prev_h, prev_c = carry
            a = xw_t + prev_h @ Wh
            i = jax.nn.sigmoid(a[:, :Hdim])
            f = jax.nn.sigmoid(a[:, Hdim:2 * Hdim])
            o = jax.nn.sigmoid(a[:, 2 * Hdim:3 * Hdim])
            g = jnp.tanh(a[:, 3 * Hdim:])
            next_c = f * prev_c + i * g
            next_h = o * jnp.tanh(next_c)
            return ((next_h, next_c), next_h)
        c0 = jnp.zeros_like(h0)
        _, hs = jax.lax.scan(step, (h0, c0), jnp.swapaxes(xW, 0, 1))
        return jnp.swapaxes(hs, 0, 1)

    def _L0_attn_ref(x, norm_w, W_in, conv_w, conv_b, W_x, w_dt, b_dt, A_log, D_param, W_out):
        import jax, jax.numpy as jnp
        import numpy as np
        from jax import lax
        D_MODEL = 256
        D_STATE = 16
        D_CONV = 4
        EXPAND = 2
        D_INNER = D_MODEL * EXPAND
        B_SZ = 2
        T_LEN = 512
        EPS = 1e-06

        def _rmsnorm(x, w):
            rms = jnp.sqrt(jnp.mean(x * x, axis=-1, keepdims=True) + EPS)
            return x / rms * w

        def _causal_depthwise_conv(x, conv_w, conv_b):
            xp = jnp.pad(x, ((0, 0), (0, 0), (D_CONV - 1, 0)))
            y = lax.conv_general_dilated(xp, conv_w, window_strides=(1,), padding='VALID', dimension_numbers=('NCH', 'OIH', 'NCH'), feature_group_count=D_INNER)
            return y + conv_b[None, :, None]

        def _mamba_forward(x, norm_w, W_in, conv_w, conv_b, W_x, w_dt, b_dt, A_log, D_param, W_out):
            residual = x
            xn = _rmsnorm(x, norm_w)
            xz = xn @ W_in
            x_proj, z = jnp.split(xz, 2, axis=-1)
            xc = _causal_depthwise_conv(jnp.swapaxes(x_proj, 1, 2), conv_w, conv_b)
            xc = jnp.swapaxes(xc, 1, 2)
            xc = jax.nn.silu(xc)
            ssm_params = xc @ W_x
            dt_raw = ssm_params[..., 0:1]
            Bp = ssm_params[..., 1:1 + D_STATE]
            Cp = ssm_params[..., 1 + D_STATE:]
            dt = jax.nn.softplus(dt_raw * w_dt + b_dt)
            A = -jnp.exp(A_log)
            A_bar = jnp.exp(dt[..., None] * A)
            Bx = dt[..., None] * Bp[:, :, None, :] * xc[..., None]
            A_t = jnp.swapaxes(A_bar, 0, 1)
            Bx_t = jnp.swapaxes(Bx, 0, 1)
            C_t = jnp.swapaxes(Cp, 0, 1)

            def step(h, inp):
                a, bx, c = inp
                h = a * h + bx
                y = jnp.sum(h * c[:, None, :], axis=-1)
                return (h, y)
            h0 = jnp.zeros((x.shape[0], D_INNER, D_STATE), dtype=x.dtype)
            _, ys = lax.scan(step, h0, (A_t, Bx_t, C_t))
            y = jnp.swapaxes(ys, 0, 1)
            y = y + xc * D_param
            y = y * jax.nn.silu(z)
            return y @ W_out + residual
        return _mamba_forward(x, norm_w, W_in, conv_w, conv_b, W_x, w_dt, b_dt, A_log, D_param, W_out)

    def _L0_cond2_ref(x, t_emb, w_q, b_q, w_k, b_k, w_v, b_v, w_o, b_o, w_f1, b_f1, w_f2, b_f2, w_ada, b_ada):
        import math
        import jax, jax.numpy as jnp
        import numpy as np
        EPS = 1e-07
        MAX_TANH_ARG = 1.0 - 1e-05

        def _norm(x):
            return jnp.sqrt(jnp.sum(x * x, axis=-1, keepdims=True)).clip(EPS)

        def logmap0(x):
            n = _norm(x)
            return jnp.arctanh(jnp.clip(n, EPS, MAX_TANH_ARG)) * x / n

        def expmap0(v):
            n = _norm(v)
            return jnp.tanh(n) * v / n

        def mobius_add(x, y):
            x2 = jnp.sum(x * x, -1, keepdims=True)
            y2 = jnp.sum(y * y, -1, keepdims=True)
            xy = jnp.sum(x * y, -1, keepdims=True)
            num = (1 + 2 * xy + y2) * x + (1 - x2) * y
            den = (1 + 2 * xy + x2 * y2).clip(EPS)
            return num / den

        def plin(x, w, b):
            return expmap0(logmap0(x) @ w + b)

        def layer_norm(x, eps=1e-06):
            m = x.mean(-1, keepdims=True)
            v = ((x - m) ** 2).mean(-1, keepdims=True)
            return (x - m) / jnp.sqrt(v + eps)

        def _beta(a, b):
            return math.exp(math.lgamma(a) + math.lgamma(b) - math.lgamma(a + b))
        D, H, FF = (256, 16, 1024)
        HD = D // H
        BETA_N = _beta(D / 2, 0.5)
        BETA_H = _beta(HD / 2, 0.5)

        def _to_heads(p):
            B, S, _ = p.shape
            t = logmap0(p).reshape(B, S, H, HD) * (BETA_H / BETA_N)
            return expmap0(jnp.transpose(t, (0, 2, 1, 3)))

        def _from_heads(ph):
            B, _, S, _ = ph.shape
            t = logmap0(ph) * (BETA_N / BETA_H)
            t = jnp.transpose(t, (0, 2, 1, 3)).reshape(B, S, D)
            return expmap0(t)
        ada = t_emb @ w_ada + b_ada
        sh_msa, sc_msa, g_msa, sh_mlp, sc_mlp, g_mlp = jnp.split(ada, 6, axis=-1)
        residual = x
        xn = layer_norm(logmap0(x))
        xm = expmap0(xn * (1 + sc_msa) + sh_msa)
        q = _to_heads(plin(xm, w_q, b_q))
        k = _to_heads(plin(xm, w_k, b_k))
        v = _to_heads(plin(xm, w_v, b_v))
        qt, kt, vt = (logmap0(q), logmap0(k), logmap0(v))
        scores = jnp.einsum('bhqd,bhkd->bhqk', qt, kt) / math.sqrt(HD)
        attn = jax.nn.softmax(scores, axis=-1)
        out_h = expmap0(jnp.einsum('bhqk,bhkd->bhqd', attn, vt))
        attn_out = plin(_from_heads(out_h), w_o, b_o)
        attn_t = g_msa * logmap0(attn_out)
        x = mobius_add(residual, expmap0(attn_t))
        residual = x
        xn = layer_norm(logmap0(x))
        xm = expmap0(xn * (1 + sc_mlp) + sh_mlp)
        ff = plin(plin(xm, w_f1, b_f1), w_f2, b_f2)
        ff_t = g_mlp * logmap0(ff)
        return mobius_add(residual, expmap0(ff_t))

    def _L0_ffn_ref(x, w1_w, w1_s, w2_w, w2_s, h1_w, h1_s, h2_w, h2_s, w3_w, w3_s):
        import jax, jax.numpy as jnp
        import numpy as np
        D_IN, D_HID = (256, 1024)

        def _ternary(key, shape):
            return jax.random.randint(key, shape, -1, 2).astype(jnp.float32)

        def _tlin(x, w, s):
            return jnp.einsum('bsi,oi->bso', x, w) * s
        h = jax.nn.silu(_tlin(x, w1_w, w1_s)) * _tlin(x, w2_w, w2_s)
        h = jax.nn.gelu(_tlin(h, h1_w, h1_s), approximate=False)
        h = jax.nn.gelu(_tlin(h, h2_w, h2_s), approximate=False)
        return _tlin(h, w3_w, w3_s)
    x = x + _L0_attn_ref(_L0_cond_ref(x, cond_1024, L0_cond_Wx, L0_cond_Wh, L0_cond_b), L0_attn_norm_w, L0_attn_W_in, L0_attn_conv_w, L0_attn_conv_b, L0_attn_W_x, L0_attn_w_dt, L0_attn_b_dt, L0_attn_A_log, L0_attn_D_param, L0_attn_W_out)
    x = x + _L0_ffn_ref(_L0_cond2_ref(x, cond_1024[:, None, :], L0_cond2_w_q, L0_cond2_b_q, L0_cond2_w_k, L0_cond2_b_k, L0_cond2_w_v, L0_cond2_b_v, L0_cond2_w_o, L0_cond2_b_o, L0_cond2_w_f1, L0_cond2_b_f1, L0_cond2_w_f2, L0_cond2_b_f2, L0_cond2_w_ada, L0_cond2_b_ada), L0_ffn_w1_w, L0_ffn_w1_s, L0_ffn_w2_w, L0_ffn_w2_s, L0_ffn_h1_w, L0_ffn_h1_s, L0_ffn_h2_w, L0_ffn_h2_s, L0_ffn_w3_w, L0_ffn_w3_s)
    return x

_drawn_inputs = setup_inputs


def setup_inputs(seed=0):
    import zlib

    import numpy as np

    out = dict(_drawn_inputs(seed))
    spreads = {'L0_cond_b': (0.0, 0.1),
     'L0_attn_norm_w': (1.0, 0.2),
     'L0_attn_conv_b': (0.0, 0.1),
     'L0_attn_D_param': (1.0, 0.2),
     'L0_cond2_b_q': (0.0, 0.1),
     'L0_cond2_b_k': (0.0, 0.1),
     'L0_cond2_b_v': (0.0, 0.1),
     'L0_cond2_b_o': (0.0, 0.1),
     'L0_cond2_b_f1': (0.0, 0.1),
     'L0_cond2_b_f2': (0.0, 0.1),
     'L0_cond2_b_ada': (0.0, 0.1)}
    factors = {}
    for name, (base, spread) in spreads.items():
        noise = np.random.default_rng([zlib.crc32(name.encode()), seed]).standard_normal(out[name].shape)
        drawn = base * np.exp(spread * noise) if base else spread * noise
        out[name] = jnp.asarray(drawn.astype(out[name].dtype))
    for name, factor in factors.items():
        out[name] = (out[name] * factor).astype(out[name].dtype)
    return out
```

```python
import math
from contextlib import ExitStack

import numpy as np

import concourse.bass as bass
from concourse import mybir

F32 = mybir.dt.float32
F16 = mybir.dt.float16
I32 = mybir.dt.int32
ALU = mybir.AluOpType
ACT = mybir.ActivationFunctionType
AX = mybir.AxisListType

P = 128
B, T, D = 2, 1024, 256
N = B * T
KD = D // P
NT = N // P
BANK = 512
G8 = 4 * D // P
HC = KD * B
HEXP = 14
DI, DS, DCONV = 512, 16, 4
CI = DI // P


class Semaphores:

    def __init__(self, nc):
        self.nc, self.cleared, self.last, self.now = nc, [], [], []

    def new(self, name):
        guard = self.nc.semaphore(name)
        sem = guard.__enter__()
        self.now.append((guard, sem))
        return sem

    def next_stage(self):
        for guard, _ in self.cleared:
            guard.__exit__(None, None, None)
        self.cleared, self.last, self.now = self.last, self.now, []

    def clear_last(self, sp):
        for _, sem in self.last:
            sp.sem_clear(sem)


class Scope:

    def __init__(self, nc, stack, sems=None):
        self.nc, self.stack, self.sems = nc, stack, sems
        if sems:
            sems.next_stage()

    def sb(self, name, shape, dtype=F32, side="left"):
        return self.stack.enter_context(self.nc.sbuf_tensor(name, shape, dtype, side=side))

    def ps(self, name, shape, dtype=F32):
        return self.stack.enter_context(self.nc.psum_tensor(name, shape, dtype))

    def sem(self, name):
        return self.sems.new(name)


def lstm_inputs(nc, sems, A, xw, wq, gate_scale, ident):
    with ExitStack() as stack:
        s = Scope(nc, stack, sems)
        xT = s.sb("xT", [P, KD, N])
        wx = s.sb("wx", [P, KD, 4 * D])
        wh = s.sb("wh", [P, KD, 4 * D])
        ws = s.sb("ws", [P, KD, 4 * D])
        bias = s.sb("bias", [P, G8])
        bias_k = s.sb("bias_k", [P, G8])
        h0 = s.sb("h0", [P, KD, B])
        pmax = s.sb("pmax", [P, 1])
        wmax = s.sb("wmax", [P, 1])
        wmax_c = s.sb("wmax_c", [P, 1])
        pow2 = s.sb("pow2", [P, 1], I32)
        sc = s.sb("sc", [P, 2])
        kk = s.sb("kk", [P, 2])
        ps = s.ps("ps_in", [P, 8, BANK])
        loaded, wh_loaded = s.sem("a_loaded"), s.sem("a_wh_loaded")
        pmax_ready, wmax_ready, chain = s.sem("a_pmax"), s.sem("a_wmax"), s.sem("a_chain")
        scales_ready = s.sem("a_scales")
        bank_full, bank_free = s.sem("a_full"), s.sem("a_free")
        h0_product, scaled, split, evac = s.sem("a_h0"), s.sem("a_scaled"), s.sem("a_split"), s.sem("a_evac")
        TB = T // BANK
        HALF = (0, 1, 2, 3, 6, 7)
        with nc.Block() as block:

            @block.sync
            def _(sp):
                sems.clear_last(sp)
                sp.dma_start(wh[:, :, :], A["Wh"].rearrange("(k p) n -> p k n", p=P)).then_inc(wh_loaded, 16)
                sp.dma_start(wx[:, :, :], A["Wx"].rearrange("(k p) n -> p k n", p=P)).then_inc(loaded, 16)
                sp.dma_start(xT[:, :, :], A["xT"].rearrange("(k p) n -> p k n", p=P)).then_inc(loaded, 16)
                sp.dma_start(bias[:, :], A["b"]).then_inc(loaded, 16)
                sp.dma_start(h0[:, :, :], A["condT"].rearrange("(k p) b -> p k b", p=P)).then_inc(loaded, 16)
                sp.dma_start(ident[:, :], A["ident"]).then_inc(loaded, 16)

            @block.gpsimd
            def _(pool):
                pool.wait_ge(pmax_ready, 1)
                nc.gpsimd.partition_all_reduce(wmax[:, :], pmax[:, :], P,
                                               bass.bass_isa.ReduceOp.max).then_inc(wmax_ready, 1)

            @block.tensor
            def _(pe):
                pe.wait_ge(loaded, 16 * 5)
                with pe.Fori(0, TB) as tb:
                    for b in range(B):
                        for g in range(G8):
                            i = b * G8 + g
                            pe.wait_ge(bank_free, tb * (B * G8) + (i + 1))
                            for k in range(KD):
                                last = nc.tensor.matmul(ps[:, i % 8, :], wx[:, k, g * P:(g + 1) * P],
                                                        xT[:, k, bass.ds(tb * BANK + b * T, BANK)],
                                                        start=k == 0, stop=k == KD - 1)
                            last.then_inc(bank_full, 1)
                pe.wait_ge(wh_loaded, 16)
                pe.wait_ge(bank_free, TB * B * G8 + 1)
                for g in range(G8):
                    for k in range(KD):
                        last = nc.tensor.matmul(ps[:, 0, g * B:(g + 1) * B], wh[:, k, g * P:(g + 1) * P],
                                                h0[:, k, :], start=k == 0, stop=k == KD - 1)
                last.then_inc(h0_product, 1)

            @block.scalar
            def _(act):
                act.preload_act_table(ACT.Identity)
                act.sem_inc(bank_free, 8)
                act.wait_ge(scales_ready, 1)
                with act.Fori(0, TB) as tb:
                    for b in range(B):
                        for g in range(G8):
                            i = b * G8 + g
                            act.wait_ge(bank_full, tb * (B * G8) + (i + 1))
                            half = int(g in HALF)
                            nc.scalar.activation(xw[:, bass.ds(tb * BANK, BANK), g * B + b], ps[:, i % 8, :],
                                                 ACT.Identity, bias=bias_k[:, g:g + 1],
                                                 scale=kk[:, half:half + 1]).then_inc(bank_free, 1)

            @block.vector
            def _(dve):
                dve.wait_ge(wh_loaded, 16)
                nc.vector.tensor_scalar(ws[:, :, :], wh[:, :, :], -1.0, None, ALU.mult).then_inc(chain, 1)
                dve.wait_ge(chain, 1)
                nc.vector.tensor_tensor(ws[:, :, :], ws[:, :, :], wh[:, :, :], ALU.max).then_inc(chain, 1)
                dve.wait_ge(chain, 2)
                nc.vector.tensor_reduce(pmax[:, :], ws[:, :, :].rearrange("p k n -> p (k n)"),
                                        AX.X, ALU.max).then_inc(pmax_ready, 1)
                dve.wait_ge(wmax_ready, 1)
                nc.vector.tensor_scalar(wmax_c[:, :], wmax[:, :], 2.0 ** -40, 2.0 ** 100,
                                        ALU.max, ALU.min).then_inc(chain, 1)
                dve.wait_ge(chain, 3)
                nc.vector.tensor_scalar(pow2[:, :], wmax_c[:, :].bitcast(I32), 0x7F800000, None,
                                        ALU.bitwise_and).then_inc(chain, 1)
                dve.wait_ge(chain, 4)
                for col, e in ((0, 267), (1, 266)):
                    nc.vector.tensor_scalar(sc[:, col:col + 1].bitcast(I32), pow2[:, :], -1.0, float(e << 23),
                                            ALU.mult, ALU.add).then_inc(chain, 1)
                for col, e in ((0, 267 + HEXP), (1, 266 + HEXP)):
                    nc.vector.tensor_scalar(kk[:, col:col + 1].bitcast(I32), pow2[:, :], -1.0, float(e << 23),
                                            ALU.mult, ALU.add).then_inc(chain, 1)
                nc.vector.tensor_scalar(gate_scale[:, :].bitcast(I32), pow2[:, :], 1.0, -float((13 + HEXP) << 23),
                                        ALU.mult, ALU.add).then_inc(chain, 1)
                dve.wait_ge(chain, 9)
                dve.wait_ge(loaded, 16 * 5)
                nc.vector.tensor_scalar(bias_k[:, 0:4], bias[:, 0:4], kk[:, 1:2], None, ALU.mult).then_inc(chain, 1)
                nc.vector.tensor_scalar(bias_k[:, 4:6], bias[:, 4:6], kk[:, 0:1], None, ALU.mult).then_inc(chain, 1)
                nc.vector.tensor_scalar(bias_k[:, 6:8], bias[:, 6:8], kk[:, 1:2], None, ALU.mult).then_inc(chain, 1)
                dve.wait_ge(chain, 12)
                dve.sem_inc(scales_ready, 1)
                for lo, hi, half in ((0, 4, 1), (4, 6, 0), (6, 8, 1)):
                    nc.vector.tensor_scalar(ws[:, :, lo * P:hi * P], wh[:, :, lo * P:hi * P],
                                            sc[:, half:half + 1], None, ALU.mult).then_inc(scaled, 1)
                dve.wait_ge(scaled, 3)
                nc.vector.tensor_copy(wq[:, 0, :, :], ws[:, :, :]).then_inc(split, 1)
                dve.wait_ge(split, 1)
                nc.vector.tensor_tensor(wq[:, 1, :, :], ws[:, :, :], wq[:, 0, :, :], ALU.subtract).then_inc(split, 1)
                dve.wait_ge(h0_product, 1)
                dve.wait_ge(bank_free, 8 + TB * B * G8)
                for lo, hi, half in ((0, 4, 1), (4, 6, 0), (6, 8, 1)):
                    c = slice(lo * B, hi * B)
                    nc.vector.scalar_tensor_tensor(xw[:, 0, c], ps[:, 0, c], kk[:, half:half + 1], xw[:, 0, c],
                                                   ALU.mult, ALU.add).then_inc(evac, 1)
                dve.wait_ge(evac, 3)


def lstm(nc, sems, xw, wq, gate_scale, ident, hist):
    IFG, O = 6 * B, 2 * B
    with ExitStack() as stack:
        s = Scope(nc, stack, sems)
        gates = s.sb("gates", [P, 2, IFG + HC])
        pre = s.sb("pre", [P, IFG])
        pre_o = s.sb("pre_o", [P, O])
        og = s.sb("og", [P, O])
        og1 = s.sb("og1", [P, O])
        prod = s.sb("prod", [P, 2 * HC])
        tc = s.sb("tc", [P, HC])
        h16 = s.sb("h16", [P, 2, KD, 2, B], F16)
        ps_g = s.ps("ps_g", [P, 2, BANK])
        ps_o = s.ps("ps_o", [P, 2, BANK])
        start = s.sem("l_start")
        ifg_sum, o_sum = s.sem("l_ifg_sum"), s.sem("l_o_sum")
        ifg_pre, o_pre = s.sem("l_ifg_pre"), s.sem("l_o_pre")
        ifg_gate, o_gate, o_scaled = s.sem("l_ifg_gate"), s.sem("l_o_gate"), s.sem("l_o_scaled")
        p_ready, cell, tanh_c = s.sem("l_p"), s.sem("l_cell"), s.sem("l_tanh_c")
        h_parts, h_ready = s.sem("l_h_parts"), s.sem("l_h")
        with nc.Block() as block:

            @block.sync
            def _(sp):
                sems.clear_last(sp)

            @block.tensor
            def _(pe):
                with pe.Fori(0, T - 1, 2) as t0:
                    for u in range(2):
                        t = t0 + u
                        nc.tensor.matmul(ps_g[:, u, 0:IFG], ident[:, :], xw[:, bass.ds(t, 1), 0:IFG],
                                         start=True, stop=False, skip_group_check=True)
                        nc.tensor.matmul(ps_o[:, u, 0:O], ident[:, :], xw[:, bass.ds(t, 1), IFG:IFG + O],
                                         start=True, stop=False, skip_group_check=True)
                        pe.wait_ge(h_ready, t + 1)
                        for g in range(G8):
                            bank, at, width, done = ((ps_g, g * B, IFG, ifg_sum) if g < 6
                                                     else (ps_o, (g - 6) * B, O, o_sum))
                            out = bank[:, u, 0:2 * width].rearrange("p (h c) -> p h c", h=2)[:, :, at:at + B]
                            for k in range(KD):
                                for w in range(2):
                                    last = nc.tensor.matmul(out, wq[:, w, k, g * P:(g + 1) * P], h16[:, u, k, :, :],
                                                            start=False, stop=k == KD - 1 and w == 1,
                                                            skip_group_check=True)
                            if g in (5, 7):
                                last.then_inc(done, 1)

            @block.scalar
            def _(act):
                act.preload_act_table(ACT.Tanh)
                with act.Fori(0, T - 1, 2) as t0:
                    for u in range(2):
                        t = t0 + u
                        act.wait_ge(ifg_pre, t + 1)
                        nc.scalar.activation(gates[:, u, 0:IFG], pre[:, :], ACT.Tanh,
                                             scale=gate_scale[:, :]).then_inc(ifg_gate, 1)
                        act.wait_ge(o_pre, t + 1)
                        nc.scalar.activation(og[:, :], pre_o[:, :], ACT.Tanh, scale=gate_scale[:, :]).then_inc(o_gate, 1)
                        act.wait_ge(cell, t + 1)
                        nc.scalar.activation(tc[:, :], gates[:, 1 - u, IFG:IFG + HC], ACT.Tanh,
                                             scale=0.5).then_inc(tanh_c, 1)

            @block.vector
            def _(dve):
                nc.vector.memset(gates[:, 0, IFG:IFG + HC], 0.0).then_inc(start, 1)
                nc.vector.memset(h16[:, 0, :, :, :], 0.0).then_inc(h_ready, 1)
                dve.wait_ge(start, 1)
                with dve.Fori(0, T - 1, 2) as t0:
                    for u in range(2):
                        t = t0 + u
                        dve.wait_ge(ifg_sum, t + 1)
                        nc.vector.tensor_reduce(pre[:, :], ps_g[:, u, 0:2 * IFG].rearrange("p (h c) -> p c h", h=2),
                                                AX.X, ALU.add).then_inc(ifg_pre, 1)
                        dve.wait_ge(o_sum, t + 1)
                        nc.vector.tensor_reduce(pre_o[:, :], ps_o[:, u, 0:2 * O].rearrange("p (h c) -> p c h", h=2),
                                                AX.X, ALU.add).then_inc(o_pre, 1)
                        dve.wait_ge(ifg_gate, t + 1)
                        nc.vector.scalar_tensor_tensor(prod[:, :], gates[:, u, 0:2 * HC], 1.0,
                                                       gates[:, u, IFG - HC:IFG + HC],
                                                       ALU.add, ALU.mult).then_inc(p_ready, 1)
                        dve.wait_ge(p_ready, t + 1)
                        nc.vector.scalar_tensor_tensor(gates[:, 1 - u, IFG:IFG + HC], prod[:, HC:2 * HC], 0.5,
                                                       prod[:, 0:HC], ALU.mult, ALU.add).then_inc(cell, 1)
                        dve.wait_ge(o_gate, t + 1)
                        nc.vector.tensor_scalar(og1[:, :], og[:, :], 2.0 ** (HEXP - 1), 2.0 ** (HEXP - 1),
                                                ALU.mult, ALU.add).then_inc(o_scaled, 1)
                        dve.wait_ge(o_scaled, t + 1)
                        dve.wait_ge(tanh_c, t + 1)
                        hc = hist[:, bass.ds(t, 1), :, :].rearrange("p t k b -> p (t k) b")
                        o_kb = og1[:, :].rearrange("p (k b) -> p k b", k=KD)
                        tc_kb = tc[:, :].rearrange("p (k b) -> p k b", k=KD)
                        nc.vector.tensor_tensor(hc, o_kb, tc_kb, ALU.mult).then_inc(h_parts, 1)
                        nc.vector.tensor_tensor(h16[:, 1 - u, :, 0, :], o_kb, tc_kb, ALU.mult).then_inc(h_parts, 1)
                        dve.wait_ge(h_parts, 2 * t + 2)
                        nc.vector.tensor_tensor(h16[:, 1 - u, :, 1, :], hc, h16[:, 1 - u, :, 0, :],
                                                ALU.subtract).then_inc(h_ready, 1)


def mamba_inputs(nc, sems, A, ident, hist, x1, dt, xc, par, consts):
    w_in, conv_w, conv_b, w_dt, b_dt, w_x, norm_w, ones = consts
    L = BANK
    with ExitStack() as stack:
        s = Scope(nc, stack, sems)
        xs = s.sb("xs", [P, NT, D])
        sq = s.sb("sq", [P, KD, L])
        lnm = s.sb("lnm", [P, L])
        rstd = s.sb("rstd", [P, L])
        back = s.sb("back", [P, P])
        xp = s.sb("xp", [P, B, CI, DCONV - 1 + L])
        acc = s.sb("acc", [P, CI, L])
        th = s.sb("th", [P, CI, L])
        v = s.sb("v", [P, CI, L])
        ps = s.ps("ps_m", [P, 8, BANK])
        names = ("xs_in const taps res res_used sq ms ln rstd xn xproj xp_in a0 a1 a2 acc halo th xc prm par dtb v abs e l dt"
                 .split())
        S = {n: s.sem("m_" + n) for n in names}
        NB = N // L
        with nc.Block() as block:

            @block.sync
            def _(sp):
                sems.clear_last(sp)
                sp.dma_start(xs[:, :, :], A["x"].rearrange("(i p) d -> p i d", p=P)).then_inc(S["xs_in"], 16)

            @block.tensor
            def _(pe):
                pe.wait_ge(S["const"], 3)
                for i in range(NT):
                    b, t0 = i // (NT // B), i % (NT // B) * P
                    if i >= 8:
                        pe.wait_ge(S["res_used"], i - 7)
                    for k in range(KD):
                        last = nc.tensor.matmul(ps[:, i % 8, k * P:(k + 1) * P], hist[:, t0:t0 + P, k, b], back[:, :],
                                                start=True, stop=True)
                    last.then_inc(S["res"], 1)
                pe.wait_ge(S["res_used"], NT)
                with pe.Fori(0, NB // B) as q:
                    for b in range(B):
                        i = q * B + b
                        pe.wait_ge(S["sq"], i + 1)
                        for k in range(KD):
                            last = nc.tensor.matmul(ps[:, 0, :], ones[:, :], sq[:, k, :], start=k == 0, stop=k == KD - 1)
                        last.then_inc(S["ms"], 1)
                        pe.wait_ge(S["xn"], (i + 1) * KD)
                        for c in range(CI):
                            for k in range(KD):
                                last = nc.tensor.matmul(ps[:, 4 + c, :], w_in[:, k, c * P:(c + 1) * P],
                                                        hist[:, bass.ds(q * L, L), k, b], start=k == 0, stop=k == KD - 1)
                            last.then_inc(S["xproj"], 1)
                        pe.wait_ge(S["xc"], i + 1)
                        for c in range(CI):
                            last = nc.tensor.matmul(ps[0:2 * DS + 1, 1, :], w_x[:, c, :],
                                                    xc[:, c, bass.ds(q * L + b * T, L)], start=c == 0, stop=c == CI - 1)
                        last.then_inc(S["prm"], 1)
                        pe.wait_ge(S["par"], i + 1)
                        nc.tensor.matmul(ps[:, 2, :], ones[0:1, :], par[0:1, bass.ds(q * L + b * T, L)],
                                         start=True, stop=True).then_inc(S["dtb"], 1)

            @block.scalar
            def _(act):
                act.wait_ge(S["res_used"], NT)
                with act.Fori(0, NB // B) as q:
                    for b in range(B):
                        i = q * B + b
                        nc.scalar.activation(sq[:, :, :], hist[:, bass.ds(q * L, L), :, b].rearrange("p t k -> p k t"),
                                             ACT.Square).then_inc(S["sq"], 1)
                        act.wait_ge(S["ms"], i + 1)
                        nc.scalar.activation(lnm[:, :], ps[:, 0, :], ACT.Ln, bias=1e-6,
                                             scale=2.0 ** (-2 * HEXP) / D).then_inc(S["ln"], 1)
                        act.wait_ge(S["ln"], i + 1)
                        nc.scalar.activation(rstd[:, :], lnm[:, :], ACT.Exp, scale=-0.5).then_inc(S["rstd"], 1)
                        act.wait_ge(S["halo"], i + 1)
                        for c in range(CI):
                            act.wait_ge(S["xproj"], i * CI + (c + 1))
                            nc.scalar.activation(xp[:, b, c, DCONV - 1:], ps[:, 4 + c, :], ACT.Copy).then_inc(S["xp_in"], 1)
                        act.wait_ge(S["acc"], (i + 1) * CI)
                        nc.scalar.activation(th[:, :, :], acc[:, :, :], ACT.Tanh).then_inc(S["th"], 1)
                        act.wait_ge(S["prm"], i + 1)
                        nc.scalar.activation(par[:, bass.ds(q * L + b * T, L)], ps[0:2 * DS + 1, 1, :],
                                             ACT.Copy).then_inc(S["par"], 1)
                        act.wait_ge(S["dtb"], i + 1)
                        for c in range(CI):
                            nc.scalar.activation(v[:, c, :], ps[:, 2, :], ACT.Identity, scale=w_dt[:, c:c + 1],
                                                 bias=b_dt[:, c:c + 1]).then_inc(S["v"], 1)
                        act.wait_ge(S["abs"], i + 1)
                        nc.scalar.activation(th[:, :, :], acc[:, :, :], ACT.Exp, scale=-1.0).then_inc(S["e"], 1)
                        act.wait_ge(S["e"], i + 1)
                        nc.scalar.activation(th[:, :, :], th[:, :, :], ACT.Ln, bias=1.0).then_inc(S["l"], 1)

            @block.vector
            def _(dve):
                nc.vector.tensor_scalar(back[:, :], ident[:, :], 2.0 ** -HEXP, None, ALU.mult).then_inc(S["const"], 1)
                nc.vector.memset(ones[:, :], 1.0).then_inc(S["const"], 1)
                nc.vector.memset(xp[:, :, :, 0:DCONV - 1], 0.0).then_inc(S["const"], 1)
                nc.vector.tensor_scalar(norm_w[:, :], norm_w[:, :], 2.0 ** -HEXP, None, ALU.mult).then_inc(S["taps"], 1)
                nc.vector.tensor_scalar(conv_w[:, :, :], conv_w[:, :, :], 0.5, None, ALU.mult).then_inc(S["taps"], 1)
                nc.vector.tensor_scalar(conv_b[:, :], conv_b[:, :], 0.5, None, ALU.mult).then_inc(S["taps"], 1)
                dve.wait_ge(S["const"], 3)
                dve.wait_ge(S["taps"], 3)
                dve.sem_inc(S["halo"], 2)
                dve.wait_ge(S["xs_in"], 16)
                for i in range(NT):
                    dve.wait_ge(S["res"], i + 1)
                    nc.vector.tensor_tensor(x1[:, i, :], ps[:, i % 8, 0:D], xs[:, i, :], ALU.add).then_inc(S["res_used"], 1)
                with dve.Fori(0, NB // B) as q:
                    for b in range(B):
                        i = q * B + b
                        dve.wait_ge(S["rstd"], i + 1)
                        for k in range(KD):
                            h = hist[:, bass.ds(q * L, L), k, b]
                            nc.vector.scalar_tensor_tensor(h, h, norm_w[:, k:k + 1], rstd[:, :],
                                                           ALU.mult, ALU.mult).then_inc(S["xn"], 1)
                        for c in range(CI):
                            dve.wait_ge(S["xp_in"], i * CI + (c + 1))
                            nc.vector.tensor_scalar(acc[:, c, :], xp[:, b, c, 0:L], conv_w[:, c, 0:1], conv_b[:, c:c + 1],
                                                    ALU.mult, ALU.add).then_inc(S["a0"], 1)
                        for j, (before, mine) in enumerate((("a0", "a1"), ("a1", "a2"), ("a2", "acc")), 1):
                            for c in range(CI):
                                dve.wait_ge(S[before], i * CI + (c + 1))
                                nc.vector.scalar_tensor_tensor(acc[:, c, :], xp[:, b, c, j:j + L], conv_w[:, c, j:j + 1],
                                                               acc[:, c, :], ALU.mult, ALU.add).then_inc(S[mine], 1)
                        nc.vector.tensor_copy(xp[:, b, :, 0:DCONV - 1], xp[:, b, :, L:]).then_inc(S["halo"], 1)
                        dve.wait_ge(S["th"], i + 1)
                        cols = bass.ds(q * L + b * T, L)
                        nc.vector.scalar_tensor_tensor(xc[:, :, cols], th[:, :, :], 1.0, acc[:, :, :],
                                                       ALU.add, ALU.mult).then_inc(S["xc"], 1)
                        dve.wait_ge(S["v"], (i + 1) * CI)
                        dve.wait_ge(S["xc"], i + 1)
                        nc.vector.scalar_tensor_tensor(acc[:, :, :], v[:, :, :], -1.0, v[:, :, :],
                                                       ALU.mult, ALU.max).then_inc(S["abs"], 1)
                        dve.wait_ge(S["l"], i + 1)
                        nc.vector.scalar_tensor_tensor(dt[:, :, cols], v[:, :, :], 0.0, th[:, :, :],
                                                       ALU.max, ALU.add).then_inc(S["dt"], 1)
                        dve.wait_ge(S["dt"], i + 1)


def mamba_scan(nc, sems, ident, dt, xc, par, a_neg, d_par, ones):
    L, NR = BANK, 4
    with ExitStack() as stack:
        s = Scope(nc, stack, sems)
        rows = s.sb("rows", [1, 2, 2, NR, L])
        uu = s.sb("uu", [P, CI, L])
        xd = s.sb("xd", [P, CI, L])
        ab = s.sb("ab", [P, CI, L])
        bx = s.sb("bx", [P, CI, L])
        hh = s.sb("hh", [P, CI, L])
        cb = s.sb("cb", [P, 2, L])
        hc = s.sb("hc", [P, CI, L])
        state = s.sb("state", [P, B, CI, DS])
        ps_y = s.ps("ps_y", [P, CI, BANK])
        ps_b = s.ps("ps_b", [P, 2, BANK])
        ps_c = s.ps("ps_c", [P, 2, BANK])
        names = ("st u u_free xd bb cc b_used cb cb_free ab ab_free bx h h_used hc hc_free y y_out y_free".split())
        S = {n: s.sem("s_" + n) for n in names}
        rows_in = [s.sem("s_rows0"), s.sem("s_rows1")]
        NQ = T // L
        with nc.Block() as block:

            @block.sync
            def _(sp):
                sems.clear_last(sp)
                with sp.Fori(0, NQ) as q:
                    for b in range(B):
                        i = q * B + b
                        for r in range(DS // NR):
                            sp.wait_ge(S["cc"], i * DS + (r + 1) * NR)
                            for bc in range(2):
                                n = 1 + bc * DS + r * NR
                                sp.dma_start(rows[0:1, r % 2, bc, :, :],
                                             par[n:n + NR, bass.ds(q * L + b * T, L)]).then_inc(rows_in[r % 2], 16)

            @block.tensor
            def _(pe):
                pe.sem_inc(S["cc"], 2 * NR)
                with pe.Fori(0, NQ) as q:
                    for b in range(B):
                        i = q * B + b
                        pe.wait_ge(S["y_free"], (i + 1) * CI)
                        pe.wait_ge(S["xd"], (i + 1) * CI)
                        for c in range(CI):
                            nc.tensor.matmul(ps_y[:, c, :], ident[:, :], xd[:, c, :], start=True, stop=False,
                                             skip_group_check=True)
                        with pe.Fori(0, DS - 2 * NR + 1, 2 * NR) as n0:
                            for jj in range(2 * NR):
                                m = i * DS + n0 + jj
                                j = jj % 2
                                if jj % NR == 0:
                                    pe.wait_ge(rows_in[jj // NR], (m + (2 * NR - jj)) * (32 // (2 * NR)))
                                pe.wait_ge(S["b_used"], m * CI + CI)
                                nc.tensor.matmul(ps_b[:, j, :], ones[0:1, :], rows[0:1, jj // NR, 0, jj % NR, :],
                                                 start=True, stop=True).then_inc(S["bb"], 1)
                                pe.wait_ge(S["cb"], m + 1)
                                nc.tensor.matmul(ps_c[:, j, :], ones[0:1, :], rows[0:1, jj // NR, 1, jj % NR, :],
                                                 start=True, stop=True).then_inc(S["cc"], 1)
                                for c in range(CI):
                                    pe.wait_ge(S["hc"], m * CI + (c + 1))
                                    nc.tensor.matmul(ps_y[:, c, :], ident[:, :], hc[:, c, :], start=False, stop=True,
                                                     skip_group_check=True).then_inc(S["hc_free"], 1)
                        pe.sem_inc(S["y"], 1)

            @block.scalar
            def _(act):
                act.preload_act_table(ACT.Exp)
                act.sem_inc(S["cb"], 2)
                act.sem_inc(S["y_free"], CI)
                with act.Fori(0, NQ) as q:
                    for b in range(B):
                        i = q * B + b
                        cols = bass.ds(q * L + b * T, L)
                        act.wait_ge(S["y_free"], (i + 1) * CI)
                        for c in range(CI):
                            nc.scalar.activation(xd[:, c, :], xc[:, c, cols], ACT.Copy,
                                                 scale=d_par[:, c:c + 1]).then_inc(S["xd"], 1)
                        with act.Fori(0, DS - 1, 2) as n0:
                            for j in range(2):
                                m = i * DS + n0 + j
                                act.wait_ge(S["cc"], m + (2 * NR + 1))
                                act.wait_ge(S["cb_free"], m * CI + CI)
                                nc.scalar.activation(cb[:, j, :], ps_c[:, j, :], ACT.Copy).then_inc(S["cb"], 1)
                                for c in range(CI):
                                    act.wait_ge(S["ab_free"], m * CI + (c + 1))
                                    nc.scalar.activation(ab[:, c, :], dt[:, c, cols], ACT.Exp,
                                                         scale=a_neg[:, c, bass.ds(n0 + j, 1)]).then_inc(S["ab"], 1)
                        act.wait_ge(S["y"], i + 1)
                        act.wait_ge(S["hc_free"], (i + 2) * DS * CI - (DS * CI - CI) + 0)
                        for c in range(CI):
                            nc.scalar.activation(dt[:, c, cols], ps_y[:, c, :], ACT.Copy).then_inc(S["y_free"], 1)

            @block.vector
            def _(dve):
                nc.vector.memset(state[:, :, :, :], 0.0).then_inc(S["st"], 1)
                dve.wait_ge(S["st"], 1)
                dve.sem_inc(S["b_used"], 2 * CI)
                dve.sem_inc(S["ab_free"], CI)
                with dve.Fori(0, NQ) as q:
                    for b in range(B):
                        i = q * B + b
                        cols = bass.ds(q * L + b * T, L)
                        nc.vector.tensor_tensor(uu[:, :, :], dt[:, :, cols], xc[:, :, cols], ALU.mult).then_inc(S["u"], 1)
                        with dve.Fori(0, DS - 1, 2) as n0:
                            for j in range(2):
                                m = i * DS + n0 + j
                                dve.wait_ge(S["u"], i + 1)
                                dve.wait_ge(S["bb"], m + 1)
                                for c in range(CI):
                                    nc.vector.tensor_tensor(bx[:, c, :], uu[:, c, :], ps_b[:, j, :],
                                                            ALU.mult).then_inc(S["b_used"], 1)
                                for c in range(CI):
                                    dve.wait_ge(S["b_used"], m * CI + (2 * CI + c + 1))
                                    dve.wait_ge(S["ab"], m * CI + (c + 1))
                                    dve.wait_ge(S["h_used"], m * CI + (c + 1))
                                    nc.vector.tensor_tensor_scan(hh[:, c, :], ab[:, c, :], bx[:, c, :],
                                                                 state[:, b, c, bass.ds(n0 + j, 1)],
                                                                 ALU.mult, ALU.add).then_inc(S["ab_free"], 1)
                                for c in range(CI):
                                    dve.wait_ge(S["ab_free"], m * CI + (CI + c + 1))
                                    nc.vector.tensor_scalar(state[:, b, c, bass.ds(n0 + j, 1)], hh[:, c, L - 1:L],
                                                            1.0, None, ALU.mult).then_inc(S["h"], 1)
                        dve.wait_ge(S["h"], (i + 1) * DS * CI)

            @block.gpsimd
            def _(pool):
                pool.sem_inc(S["h_used"], CI)
                pool.sem_inc(S["cb_free"], 2 * CI)
                pool.sem_inc(S["hc_free"], CI)
                with pool.Fori(0, NQ) as q:
                    for b in range(B):
                        i = q * B + b
                        with pool.Fori(0, DS - 1, 2) as n0:
                            for j in range(2):
                                m = i * DS + n0 + j
                                pool.wait_ge(S["cb"], m + 3)
                                for c in range(CI):
                                    pool.wait_ge(S["h"], m * CI + (c + 1))
                                    pool.wait_ge(S["hc_free"], m * CI + (c + 1))
                                    nc.gpsimd.tensor_tensor(hc[:, c, :], hh[:, c, :], cb[:, j, :],
                                                            ALU.mult).then_inc(S["hc"], 1)
                                    pool.wait_ge(S["hc"], m * CI + (c + 1))
                                    pool.sem_inc(S["h_used"], 1)
                                    pool.sem_inc(S["cb_free"], 1)


def mamba_output(nc, sems, hist, x1, yy, xc, w_in, w_out):
    L = BANK
    with ExitStack() as stack:
        s = Scope(nc, stack, sems)
        th = s.sb("th_z", [P, CI, L])
        yz = s.sb("yz", [P, CI, L])
        ps_z = s.ps("ps_z", [P, CI, BANK])
        ps_o = s.ps("ps_out", [P, L // P, BANK])
        S = {n: s.sem("o_" + n) for n in "z th z2 yz z_free out out_used".split()}
        NQ = T // L
        with nc.Block() as block:

            @block.sync
            def _(sp):
                sems.clear_last(sp)

            @block.tensor
            def _(pe):
                with pe.Fori(0, NQ) as q:
                    for b in range(B):
                        i = q * B + b
                        pe.wait_ge(S["z2"], i + 1)
                        for c in range(CI):
                            for k in range(KD):
                                last = nc.tensor.matmul(ps_z[:, c, :], w_in[:, k, DI + c * P:DI + (c + 1) * P],
                                                        hist[:, bass.ds(q * L, L), k, b], start=k == 0, stop=k == KD - 1)
                        last.then_inc(S["z"], 1)
                        pe.wait_ge(S["yz"], i + 1)
                        pe.wait_ge(S["out_used"], (i + 1) * (L // P))
                        for m in range(L // P):
                            for c in range(CI):
                                last = nc.tensor.matmul(ps_o[:, m, 0:D], yz[:, c, m * P:(m + 1) * P], w_out[:, c, :],
                                                        start=c == 0, stop=c == CI - 1)
                            last.then_inc(S["out"], 1)

            @block.scalar
            def _(act):
                act.preload_act_table(ACT.Tanh)
                with act.Fori(0, NQ) as q:
                    for b in range(B):
                        i = q * B + b
                        act.wait_ge(S["z"], i + 1)
                        act.wait_ge(S["z2"], i + 1)
                        nc.scalar.activation(th[:, :, :], ps_z[:, :, :], ACT.Tanh, scale=0.5).then_inc(S["th"], 1)

            @block.vector
            def _(dve):
                dve.sem_inc(S["z2"], 1)
                dve.sem_inc(S["out_used"], L // P)
                with dve.Fori(0, NQ) as q:
                    for b in range(B):
                        i = q * B + b
                        cols = bass.ds(q * L + b * T, L)
                        dve.wait_ge(S["th"], i + 1)
                        nc.vector.scalar_tensor_tensor(th[:, :, :], th[:, :, :], 1.0, ps_z[:, :, :],
                                                       ALU.add, ALU.mult).then_inc(S["z2"], 1)
                        dve.wait_ge(S["z2"], i + 2)
                        nc.vector.scalar_tensor_tensor(yz[:, :, :], yy[:, :, cols], 0.5, th[:, :, :],
                                                       ALU.mult, ALU.mult).then_inc(S["yz"], 1)
                        for m in range(L // P):
                            dve.wait_ge(S["out"], i * (L // P) + (m + 1))
                            tile = x1[:, bass.ds(q * (L // P) + (b * (T // P) + m), 1), :]
                            nc.vector.tensor_tensor(tile, tile, ps_o[:, m, 0:D], ALU.add).then_inc(S["out_used"], 1)


def mamba(nc, sems, A, ident, hist, x1):
    with ExitStack() as stack:
        s = Scope(nc, stack, sems)
        w_in = s.sb("w_in", [P, KD, 2 * DI])
        conv_w = s.sb("conv_w", [P, CI, DCONV])
        conv_b = s.sb("conv_b", [P, CI])
        w_dt = s.sb("w_dt", [P, CI])
        b_dt = s.sb("b_dt", [P, CI])
        w_x = s.sb("w_x", [P, CI, 2 * DS + 1])
        norm_w = s.sb("norm_w", [P, KD])
        ones = s.sb("ones", [P, P])
        a_neg = s.sb("a_neg", [P, CI, DS])
        d_par = s.sb("d_par", [P, CI])
        w_out = s.sb("w_out", [P, CI, D])
        dt = s.sb("dt", [P, CI, N])
        xc = s.sb("xc", [P, CI, N])
        par = s.sb("par", [2 * DS + 1, N])
        loaded, made = s.sem("w_loaded"), s.sem("w_made")
        with nc.Block() as block:

            @block.sync
            def _(sp):
                sems.clear_last(sp)
                n = 0
                for dst, src in ((w_in[:, :, :], A["w_in"].rearrange("(k p) n -> p k n", p=P)),
                                 (conv_w[:, :, :], A["conv_w"]), (conv_b[:, :], A["conv_b"]),
                                 (w_dt[:, :], A["w_dt"]), (b_dt[:, :], A["b_dt"]),
                                 (w_x[:, :, :], A["w_x"].rearrange("(c p) n -> p c n", p=P)),
                                 (norm_w[:, :], A["norm_w"]), (a_neg[:, :, :], A["a_log"]), (d_par[:, :], A["d_par"]),
                                 (w_out[:, :, :], A["w_out"].rearrange("(c p) n -> p c n", p=P))):
                    sp.dma_start(dst, src).then_inc(loaded, 16)
                    n += 16
                sp.wait_ge(loaded, n)

            @block.scalar
            def _(act):
                act.wait_ge(loaded, 16 * 10)
                nc.scalar.activation(a_neg[:, :, :], a_neg[:, :, :], ACT.Exp).then_inc(made, 1)
                act.wait_ge(made, 1)
                nc.scalar.activation(a_neg[:, :, :], a_neg[:, :, :], ACT.Copy, scale=-1.0).then_inc(made, 1)
                act.wait_ge(made, 2)

        mamba_inputs(nc, sems, A, ident, hist, x1, dt, xc, par, (w_in, conv_w, conv_b, w_dt, b_dt, w_x, norm_w, ones))
        mamba_scan(nc, sems, ident, dt, xc, par, a_neg, d_par, ones)
        mamba_output(nc, sems, hist, x1, dt, xc, w_in, w_out)


EPS = 1e-7
MAXT = float(np.float32(1.0 - 1e-5))
ATANH = math.atanh(MAXT)
LN_A = math.log(ATANH)
TINY = 1e-18
H, HD, FF = 16, 16, 1024


def _beta(a, b):
    return math.exp(math.lgamma(a) + math.lgamma(b) - math.lgamma(a + b))


R_HEADS = _beta(HD / 2, 0.5) / _beta(D / 2, 0.5)
QSC = 256.0
TPB = NT // B


def row(ap, *shape):
    return ap.unsqueeze(len(ap.shape)).broadcast_to(list(ap.shape) + [shape[-1]])


def ada_rows(nc, sems, A, ada):
    W6 = 6 * D
    with ExitStack() as stack:
        s = Scope(nc, stack, sems)
        w = s.sb("w_ada", [P, KD, W6])
        cond = s.sb("cond", [P, KD, B])
        cond_b = s.sb("cond_b", [P, KD, B, P])
        bias = s.sb("bias_ada", [1, W6])
        one = s.sb("one_ada", [1, P])
        ps = s.ps("ps_ada", [P, B * W6 // BANK, BANK])
        loaded, made, full, out = s.sem("d_loaded"), s.sem("d_made"), s.sem("d_full"), s.sem("d_out")
        with nc.Block() as block:

            @block.sync
            def _(sp):
                sems.clear_last(sp)
                sp.dma_start(cond[:, :, :], A["condT"].rearrange("(k p) b -> p k b", p=P)).then_inc(loaded, 16)
                sp.dma_start(bias[:, :], A["b_ada"]).then_inc(loaded, 16)
                sp.dma_start(w[:, :, :], A["w_ada"].rearrange("(k p) n -> p k n", p=P)).then_inc(loaded, 16)

            @block.tensor
            def _(pe):
                pe.wait_ge(loaded, 48)
                pe.wait_ge(made, 2)
                for b in range(B):
                    for c in range(W6 // BANK):
                        cols = slice(c * BANK, (c + 1) * BANK)
                        out_ps = ps[:, b * (W6 // BANK) + c, :]
                        for k in range(KD):
                            nc.tensor.matmul(out_ps, cond_b[:, k, b, :], w[:, k, cols], start=k == 0, stop=False)
                        nc.tensor.matmul(out_ps, one[0:1, :], bias[0:1, cols], start=False, stop=True).then_inc(full, 1)

            @block.vector
            def _(dve):
                nc.vector.memset(one[:, :], 1.0).then_inc(made, 1)
                dve.wait_ge(loaded, 48)
                nc.vector.tensor_copy(cond_b[:, :, :, :], row(cond[:, :, :], P)).then_inc(made, 1)
                for b in range(B):
                    for c in range(W6 // BANK):
                        n = b * (W6 // BANK) + c
                        dve.wait_ge(full, n + 1)
                        for lo in range(c * BANK, (c + 1) * BANK, D):
                            plus = 1.0 if lo // D in (1, 4) else 0.0
                            at = lo - c * BANK
                            nc.vector.tensor_scalar(ada[:, b, lo // D, :], ps[:, n, at:at + D], plus, None,
                                                    ALU.add).then_inc(out, 1)
                dve.wait_ge(out, B * 6)


def norm_modulate(nc, sems, tag, x, ada, shift, ident, vT):
    with ExitStack() as stack:
        s = Scope(nc, stack, sems)
        big = s.sb(tag + "big", [P, NT, D])
        v = s.sb(tag + "v", [P, NT, D])
        col = {n: s.sb(tag + n, [P, NT]) for n in "sum mean n2 var n m lp lm rn s s2v f r".split()}
        ps = s.ps(tag + "ps", [P, 8, BANK])
        link_v, link_a = s.sem(tag + "link_v"), s.sem(tag + "link_a")
        S = {n: s.sem(tag + n) for n in "sq1 n2 sq2 norm m logs s2v f v sq3 n2v r ready t used".split()}
        with nc.Block() as block:

            @block.sync
            def _(sp):
                sems.clear_last(sp)

            @block.scalar
            def _(act):
                count = [0]

                def link(ins):
                    count[0] += 1
                    ins.then_inc(link_a, 1)
                    act.wait_ge(link_a, count[0])

                nc.scalar.activation(big[:, :, :], x[:, :, :], ACT.Square).then_inc(S["sq1"], 1)
                act.wait_ge(S["n2"], 1)
                link(nc.scalar.activation(col["lp"][:, :], col["n2"][:, :], ACT.Ln))
                link(nc.scalar.activation(col["rn"][:, :], col["lp"][:, :], ACT.Exp, scale=-0.5))
                nc.scalar.activation(col["n"][:, :], col["lp"][:, :], ACT.Exp, scale=0.5).then_inc(S["norm"], 1)
                act.wait_ge(S["m"], 1)
                link(nc.scalar.activation(col["lp"][:, :], col["m"][:, :], ACT.Ln, bias=1.0))
                nc.scalar.activation(col["lm"][:, :], col["m"][:, :], ACT.Ln, bias=1.0, scale=-1.0).then_inc(S["logs"], 1)
                act.wait_ge(S["sq2"], 1)
                nc.scalar.activation(big[:, :, :], v[:, :, :], ACT.Square).then_inc(S["sq3"], 1)
                act.wait_ge(S["s2v"], 1)
                link(nc.scalar.activation(col["lp"][:, :], col["s2v"][:, :], ACT.Ln))
                nc.scalar.activation(col["f"][:, :], col["lp"][:, :], ACT.Exp, scale=-0.5).then_inc(S["f"], 1)
                act.wait_ge(S["v"], 1)
                nc.scalar.activation(big[:, :, :], v[:, :, :], ACT.Square).then_inc(S["sq3"], 1)
                act.wait_ge(S["n2v"], 1)
                link(nc.scalar.activation(col["lp"][:, :], col["n2"][:, :], ACT.Ln))
                nc.scalar.activation(col["r"][:, :], col["lp"][:, :], ACT.Exp, scale=-0.5, bias=LN_A).then_inc(S["r"], 1)
                for i in range(0, NT, 2):
                    act.wait_ge(S["t"], i // 2 + 1)
                    nc.scalar.activation(
                        vT[:, :, i * P:(i + 2) * P].rearrange("p k (i t) -> p i k t", i=2),
                        ps[:, i // 2 % 8, :].rearrange("p (i k t) -> p i k t", i=2, k=KD), ACT.Copy).then_inc(S["used"], 1)

            @block.vector
            def _(dve):
                count = [0]

                def link(ins):
                    count[0] += 1
                    ins.then_inc(link_v, 1)
                    dve.wait_ge(link_v, count[0])

                c = {n: t[:, :] for n, t in col.items()}
                link(nc.vector.tensor_reduce(c["sum"], x[:, :, :], AX.X, ALU.add))
                link(nc.vector.tensor_scalar(c["mean"], c["sum"], 1.0 / D, None, ALU.mult))
                dve.wait_ge(S["sq1"], 1)
                link(nc.vector.tensor_reduce(c["n2"], big[:, :, :], AX.X, ALU.add))
                nc.vector.tensor_scalar(c["n2"], c["n2"], EPS * EPS, None, ALU.max).then_inc(S["n2"], 1)
                nc.vector.tensor_tensor(v[:, :, :], x[:, :, :], row(c["mean"], D), ALU.subtract).then_inc(S["sq2"], 1)
                dve.wait_ge(S["norm"], 1)
                nc.vector.tensor_scalar(c["m"], c["n"], MAXT, None, ALU.min).then_inc(S["m"], 1)
                dve.wait_ge(S["sq3"], 1)
                link(nc.vector.tensor_reduce(c["var"], big[:, :, :], AX.X, ALU.add))
                dve.wait_ge(S["logs"], 1)
                link(nc.vector.tensor_tensor(c["s"], c["lp"], c["lm"], ALU.subtract))
                link(nc.vector.scalar_tensor_tensor(c["s"], c["s"], 0.5, c["rn"], ALU.mult, ALU.mult))
                link(nc.vector.scalar_tensor_tensor(c["s2v"], c["s"], 1.0 / D, c["s"], ALU.mult, ALU.mult))
                link(nc.vector.tensor_tensor(c["s2v"], c["s2v"], c["var"], ALU.mult))
                nc.vector.tensor_scalar(c["s2v"], c["s2v"], 1e-6, None, ALU.add).then_inc(S["s2v"], 1)
                dve.wait_ge(S["f"], 1)
                link(nc.vector.tensor_tensor(c["f"], c["f"], c["s"], ALU.mult))
                link(nc.vector.tensor_tensor(v[:, :, :], v[:, :, :], row(c["f"], D), ALU.mult))
                for part, op in ((shift + 1, ALU.mult), (shift, ALU.add)):
                    for b in range(B):
                        tiles = v[:, b * TPB:(b + 1) * TPB, :]
                        rows = ada[:, b, part, :].unsqueeze(1).broadcast_to([P, TPB, D])
                        link(nc.vector.tensor_tensor(tiles, tiles, rows, op))
                dve.sem_inc(S["v"], 1)
                dve.wait_ge(S["sq3"], 2)
                link(nc.vector.tensor_reduce(c["n2"], big[:, :, :], AX.X, ALU.add))
                nc.vector.tensor_scalar(c["n2"], c["n2"], EPS * EPS, None, ALU.max).then_inc(S["n2v"], 1)
                dve.wait_ge(S["r"], 1)
                link(nc.vector.tensor_scalar(c["r"], c["r"], 1.0, None, ALU.min))
                nc.vector.tensor_tensor(v[:, :, :], v[:, :, :], row(c["r"], D), ALU.mult).then_inc(S["ready"], 1)

            @block.tensor
            def _(pe):
                pe.wait_ge(S["ready"], 1)
                for i in range(NT):
                    for k in range(KD):
                        at = (i % 2 * KD + k) * P
                        last = nc.tensor.transpose(ps[:, i // 2 % 8, at:at + P], v[:, i, k * P:(k + 1) * P], ident[:, :])
                    if i % 2:
                        last.then_inc(S["t"], 1)


def qkv(nc, sems, A, ident16, vT, qT, kT, va, sq, nh):
    W3 = 3 * D
    with ExitStack() as stack:
        s = Scope(nc, stack, sems)
        w = s.sb("w_qkv", [P, KD, W3])
        bias = s.sb("b_qkv", [1, W3])
        one = s.sb("one_q", [1, P])
        x = s.sb("x_qkv", [P, NT, W3])
        nf = s.sb("nf", [P, NT * 3])
        pair = s.sb("pair", [P, 2, 2, H, 4, HD], F16)
        ps = s.ps("ps_qkv", [P, 3, 2, BANK])
        ps_t = s.ps("ps_t", [P, 2, 2 * BANK], F16)
        loaded = s.sem("q_loaded")
        S = {n: s.sem("q_" + n) for n in "one full x sq nh nh_used lh lf alpha_f alpha scaled hi lo t used".split()}
        link_v = s.sem("q_link")
        with nc.Block() as block:

            @block.sync
            def _(sp):
                sems.clear_last(sp)
                sp.dma_start(w[:, :, :], A["w_qkv"].rearrange("(k p) n -> p k n", p=P)).then_inc(loaded, 16)
                sp.dma_start(bias[:, :], A["b_qkv"]).then_inc(loaded, 16)
                sp.dma_start(ident16[:, :], A["ident16"]).then_inc(loaded, 16)

            @block.tensor
            def _(pe):
                pe.wait_ge(loaded, 48)
                pe.wait_ge(S["one"], 1)
                for i in range(NT):
                    if i >= 3:
                        pe.wait_ge(S["x"], 2 * (i - 2))
                    for part, (lo, hi) in enumerate(((0, BANK), (BANK, W3))):
                        out = ps[:, i % 3, part, 0:hi - lo]
                        for k in range(KD):
                            nc.tensor.matmul(out, vT[:, k, i * P:(i + 1) * P], w[:, k, lo:hi], start=k == 0, stop=False)
                        nc.tensor.matmul(out, one[0:1, :], bias[0:1, lo:hi], start=False, stop=True).then_inc(S["full"], 1)
                with pe.Fori(0, NT - 1, 2) as i0:
                    for u in range(2):
                        i = i0 + u
                        pe.wait_ge(S["lo"], i * 4 + 4)
                        for qk in range(2):
                            pe.wait_ge(S["used"], i * 2 + (qk + 2))
                            for h in range(0, H, 2):
                                last = nc.tensor.transpose(ps_t[:, qk, h // 2 * P:(h // 2 + 1) * P],
                                                           pair[:, u, qk, h:h + 2, :, :].rearrange("p h r d -> p (h r d)"),
                                                           ident16[:, :])
                            last.then_inc(S["t"], 1)

            @block.scalar
            def _(act):
                act.preload_act_table(ACT.Exp)
                for i in range(NT):
                    for part, (lo, hi) in enumerate(((0, BANK), (BANK, W3))):
                        act.wait_ge(S["full"], 2 * i + part + 1)
                        nc.scalar.activation(x[:, i, lo:hi], ps[:, i % 3, part, 0:hi - lo], ACT.Copy).then_inc(S["x"], 1)
                for j in range(4):
                    if j:
                        act.wait_ge(S["nh"], j)
                    act.wait_ge(S["x"], 2 * NT)
                    nc.scalar.activation(sq, x[:, j * 4:(j + 1) * 4, :], ACT.Square).then_inc(S["sq"], 1)
                act.wait_ge(S["nh_used"], 1)
                nc.scalar.activation(nh[:, :, :], nh[:, :, :], ACT.Ln).then_inc(S["lh"], 1)
                nc.scalar.activation(nf[:, :], nf[:, :], ACT.Ln).then_inc(S["lf"], 1)
                act.wait_ge(S["lh"], 1)
                act.wait_ge(S["lf"], 1)
                nc.scalar.activation(nh[:, :, :], nh[:, :, :], ACT.Exp, scale=-0.5, bias=LN_A).then_inc(S["alpha"], 1)
                nc.scalar.activation(nf[:, :], nf[:, :], ACT.Exp, scale=-0.5,
                                     bias=math.log(ATANH * R_HEADS)).then_inc(S["alpha_f"], 1)
                with act.Fori(0, NT - 1, 2) as i0:
                    for u in range(2):
                        i = i0 + u
                        for qk, dst in enumerate((qT, kT)):
                            act.wait_ge(S["t"], i * 2 + (qk + 1))
                            nc.scalar.activation(dst[:, :, bass.ds(i * P, P)],
                                                 ps_t[:, qk, :].rearrange("p (h t) -> p h t", t=P),
                                                 ACT.Copy).then_inc(S["used"], 1)

            @block.vector
            def _(dve):
                count = [0]

                def link(ins):
                    count[0] += 1
                    ins.then_inc(link_v, 1)
                    dve.wait_ge(link_v, count[0])

                dve.sem_inc(S["used"], 3)
                nc.vector.memset(one[:, :], 1.0).then_inc(S["one"], 1)
                for j in range(4):
                    dve.wait_ge(S["sq"], j + 1)
                    nc.vector.tensor_reduce(nh[:, j * 12:(j + 1) * 12, :],
                                            sq.rearrange("p i (a h d) -> p (i a) h d", a=3, d=HD),
                                            AX.X, ALU.add).then_inc(S["nh"], 1)
                dve.wait_ge(S["nh"], 4)
                link(nc.vector.tensor_reduce(nf[:, :], nh[:, :, :], AX.X, ALU.add))
                link(nc.vector.tensor_scalar(nf[:, :], nf[:, :], EPS * EPS, None, ALU.max))
                nc.vector.tensor_scalar(nh[:, :, :], nh[:, :, :], TINY, None, ALU.max).then_inc(S["nh_used"], 1)
                dve.wait_ge(S["alpha_f"], 1)
                dve.wait_ge(S["alpha"], 1)
                link(nc.vector.tensor_scalar(nf[:, :], nf[:, :], R_HEADS, None, ALU.min))
                link(nc.vector.tensor_tensor(nh[:, :, :], nh[:, :, :], row(nf[:, :], H), ALU.min))
                alpha = nh[:, :, :].rearrange("p (i a) h -> p i a h", a=3)
                with dve.Fori(0, NT - 1, 2) as i0:
                    for u in range(2):
                        i = i0 + u
                        xi = x[:, bass.ds(i, 1), :].rearrange("p i (a h d) -> p (i a) h d", a=3, d=HD)
                        ai = alpha[:, bass.ds(i, 1), :, :].rearrange("p i a h -> p (i a) h")
                        dve.wait_ge(S["used"], i * 2 + 1)
                        for qk in range(2):
                            nc.vector.scalar_tensor_tensor(xi[:, qk, :, :], xi[:, qk, :, :], QSC, row(ai[:, qk, :], HD),
                                                           ALU.mult, ALU.mult).then_inc(S["scaled"], 1)
                        nc.vector.tensor_tensor(va[:, bass.ds(i, 1), :, :].rearrange("p i h d -> p (i h) d"),
                                                xi[:, 2, :, :], row(ai[:, 2, :], HD), ALU.mult).then_inc(S["scaled"], 1)
                        dve.wait_ge(S["scaled"], (i + 1) * 3)
                        for qk in range(2):
                            for rep in range(2):
                                part = (2 * rep, rep)[qk]
                                nc.vector.tensor_scalar(pair[:, u, qk, :, part, :],
                                                        xi[:, qk, :, :],
                                                        1.0, None, ALU.mult).then_inc(S["hi"], 1)
                        dve.wait_ge(S["hi"], (i + 1) * 4)
                        for qk in range(2):
                            for rep in range(2):
                                part = (2 * rep + 1, rep + 2)[qk]
                                nc.vector.tensor_tensor(pair[:, u, qk, :, part, :],
                                                        xi[:, qk, :, :],
                                                        pair[:, u, qk, :, 0, :], ALU.subtract).then_inc(S["lo"], 1)


def attention(nc, sems, qT, kT, va, oT):
    HG = 4
    NKC = T // P
    IT = B * H // HG
    with ExitStack() as stack:
        s = Scope(nc, stack, sems)
        qs = s.sb("qs", [P, 2, HG // 2, T], F16)
        ks = s.sb("ks", [P, 2, HG // 2, T], F16)
        vs = s.sb("vs", [P, 2, NKC, HG, 32])
        pt = s.sb("pt", [P, 2, T])
        ps_s = s.ps("ps_s", [P, 2, T])
        ps_o = s.ps("ps_o2", [P, 2, T])
        S = {n: s.sem("t_" + n) for n in "pad staged stage_free s e pv out used".split()}
        NS = HG * NKC
        with nc.Block() as block:

            @block.sync
            def _(sp):
                sems.clear_last(sp)

            @block.tensor
            def _(pe):
                with pe.Fori(0, IT - 1, 2) as i0:
                    for u in range(2):
                        i = i0 + u

                        def scores(n):
                            h, kc = n // NKC, n % NKC
                            rows = slice(h % 2 * 64, h % 2 * 64 + 64)
                            pe.wait_ge(S["e"], i * NS + (n + 1))
                            for half in range(2):
                                last = nc.tensor.matmul(ps_s[:, n % 2, half * BANK:(half + 1) * BANK],
                                                        ks[rows, u, h // 2, kc * P:(kc + 1) * P],
                                                        qs[rows, u, h // 2, half * BANK:(half + 1) * BANK],
                                                        start=True, stop=True)
                            last.then_inc(S["s"], 1)

                        pe.wait_ge(S["staged"], i * 3 + 3)
                        pe.wait_ge(S["used"], i + 1)
                        scores(0)
                        scores(1)
                        for n in range(NS):
                            h, kc = n // NKC, n % NKC
                            pe.wait_ge(S["e"], i * NS + (n + 3))
                            for half in range(2):
                                last = nc.tensor.matmul(ps_o[h * 32:(h + 1) * 32, u, half * BANK:(half + 1) * BANK],
                                                        vs[:, u, kc, h, :], pt[:, n % 2, half * BANK:(half + 1) * BANK],
                                                        start=kc == 0, stop=kc == NKC - 1)
                            last.then_inc(S["pv"], 1)
                            if n + 2 < NS:
                                scores(n + 2)

            @block.scalar
            def _(act):
                act.preload_act_table(ACT.Exp)
                act.sem_inc(S["e"], 2)
                with act.Fori(0, IT - 1, 2) as i0:
                    for u in range(2):
                        i = i0 + u
                        for n in range(NS):
                            act.wait_ge(S["s"], i * NS + (n + 1))
                            act.wait_ge(S["pv"], i * NS + (n + 1))
                            nc.scalar.activation(pt[:, n % 2, :], ps_s[:, n % 2, :], ACT.Exp,
                                                 scale=0.25 / (QSC * QSC)).then_inc(S["e"], 1)

            @block.vector
            def _(dve):
                dve.sem_inc(S["pv"], 2)
                dve.sem_inc(S["used"], 2)
                nc.vector.memset(vs[:, :, :, :, HD:HD + 1], 1.0).then_inc(S["pad"], 1)
                nc.vector.memset(vs[:, :, :, :, HD + 1:], 0.0).then_inc(S["pad"], 1)
                dve.wait_ge(S["pad"], 2)

                def take_out(i):
                    b, g = i // (H // HG), i % (H // HG)
                    dve.wait_ge(S["pv"], (i + 1) * NS + 2)
                    nc.vector.tensor_copy(oT[:, g, b * T:(b + 1) * T], ps_o[:, i % 2, :]).then_inc(S["used"], 1)

                for i in range(IT):
                    b, g, u = i // (H // HG), i % (H // HG), i % 2
                    if i >= 2:
                        dve.wait_ge(S["pv"], (i - 1) * NS + 2)
                    nc.vector.tensor_copy(qs[:, u, :, :], qT[:, 2 * g:2 * g + 2, b * T:(b + 1) * T]).then_inc(S["staged"], 1)
                    nc.vector.tensor_copy(ks[:, u, :, :], kT[:, 2 * g:2 * g + 2, b * T:(b + 1) * T]).then_inc(S["staged"], 1)
                    nc.vector.tensor_copy(vs[:, u, :, :, 0:HD], va[:, b * NKC:(b + 1) * NKC, HG * g:HG * (g + 1), :])\
                      .then_inc(S["staged"], 1)
                    if i:
                        take_out(i - 1)
                take_out(IT - 1)


def heads_out(nc, sems, ident, oT, aT, v):
    with ExitStack() as stack:
        s = Scope(nc, stack, sems)
        o = s.sb("o", [P, NT, H, 32])
        sq = s.sb("sq_o", [P, NT, H * HD])
        rden = s.sb("rden", [P, NT, H])
        nh = s.sb("nh_o", [P, NT, H])
        n2 = s.sb("ho_n2", [P, NT])
        ps = s.ps("ps_ot", [P, 8, BANK])
        S = {n: s.sem("h_" + n) for n in "t o sq n2h alpha sq2 v n2 r ready tt used".split()}
        link_v, link_a = s.sem("h_link_v"), s.sem("h_link_a")
        with nc.Block() as block:

            @block.sync
            def _(sp):
                sems.clear_last(sp)

            @block.tensor
            def _(pe):
                for i in range(NT):
                    if i >= 8:
                        pe.wait_ge(S["o"], i - 7)
                    for g in range(4):
                        last = nc.tensor.transpose(ps[:, i % 8, g * P:(g + 1) * P], oT[:, g, i * P:(i + 1) * P], ident[:, :])
                    last.then_inc(S["t"], 1)
                pe.wait_ge(S["o"], NT)
                pe.wait_ge(S["ready"], 1)
                for i in range(NT):
                    for k in range(KD):
                        at = (i % 2 * KD + k) * P
                        last = nc.tensor.transpose(ps[:, i // 2 % 8, at:at + P], v[:, i, k * P:(k + 1) * P], ident[:, :])
                    if i % 2:
                        last.then_inc(S["tt"], 1)

            @block.scalar
            def _(act):
                act.preload_act_table(ACT.Copy)
                for i in range(NT):
                    act.wait_ge(S["t"], i + 1)
                    nc.scalar.activation(o[:, i, :, :].rearrange("p h d -> p (h d)"), ps[:, i % 8, :],
                                         ACT.Copy).then_inc(S["o"], 1)
                act.wait_ge(S["o"], NT)
                nc.scalar.activation(sq[:, :, :].rearrange("p i (h d) -> p (i h) d", d=HD),
                                     o[:, :, :, 0:HD].rearrange("p i h d -> p (i h) d"), ACT.Square).then_inc(S["sq"], 1)
                act.wait_ge(S["n2h"], 1)
                nc.scalar.activation(nh[:, :, :], nh[:, :, :], ACT.Ln).then_inc(link_a, 1)
                act.wait_ge(link_a, 1)
                nc.scalar.activation(nh[:, :, :], nh[:, :, :], ACT.Exp, scale=-0.5, bias=LN_A).then_inc(S["alpha"], 1)
                act.wait_ge(S["v"], 1)
                nc.scalar.activation(sq[:, :, :], v[:, :, :], ACT.Square).then_inc(S["sq2"], 1)
                act.wait_ge(S["n2"], 1)
                nc.scalar.activation(n2[:, :], n2[:, :], ACT.Ln).then_inc(link_a, 1)
                act.wait_ge(link_a, 2)
                nc.scalar.activation(n2[:, :], n2[:, :], ACT.Exp, scale=-0.5, bias=LN_A).then_inc(S["r"], 1)
                for i in range(0, NT, 2):
                    act.wait_ge(S["tt"], i // 2 + 1)
                    nc.scalar.activation(
                        aT[:, :, i * P:(i + 2) * P].rearrange("p k (i t) -> p i k t", i=2),
                        ps[:, i // 2 % 8, :].rearrange("p (i k t) -> p i k t", i=2, k=KD), ACT.Copy).then_inc(S["used"], 1)

            @block.vector
            def _(dve):
                count = [0]

                def link(ins):
                    count[0] += 1
                    ins.then_inc(link_v, 1)
                    dve.wait_ge(link_v, count[0])

                dve.wait_ge(S["o"], NT)
                link(nc.vector.reciprocal(rden[:, :, :], o[:, :, :, HD:HD + 1].rearrange("p i h d -> p i (h d)")))
                dve.wait_ge(S["sq"], 1)
                link(nc.vector.tensor_reduce(nh[:, :, :], sq[:, :, :].rearrange("p i (h d) -> p i h d", d=HD), AX.X, ALU.add))
                nc.vector.tensor_scalar(nh[:, :, :], nh[:, :, :], TINY, None, ALU.max).then_inc(S["n2h"], 1)
                dve.wait_ge(S["alpha"], 1)
                link(nc.vector.tensor_tensor(nh[:, :, :], nh[:, :, :], rden[:, :, :], ALU.min))
                link(nc.vector.tensor_scalar(nh[:, :, :], nh[:, :, :], 1.0 / R_HEADS, None, ALU.mult))
                nc.vector.tensor_tensor(v[:, :, :].rearrange("p i (h d) -> p (i h) d", d=HD),
                                        o[:, :, :, 0:HD].rearrange("p i h d -> p (i h) d"),
                                        row(nh[:, :, :].rearrange("p i h -> p (i h)"), HD), ALU.mult).then_inc(S["v"], 1)
                dve.wait_ge(S["v"], 1)
                dve.wait_ge(S["sq2"], 1)
                link(nc.vector.tensor_reduce(n2[:, :], sq[:, :, :], AX.X, ALU.add))
                nc.vector.tensor_scalar(n2[:, :], n2[:, :], EPS * EPS, None, ALU.max).then_inc(S["n2"], 1)
                dve.wait_ge(S["r"], 1)
                link(nc.vector.tensor_scalar(n2[:, :], n2[:, :], 1.0, None, ALU.min))
                nc.vector.tensor_tensor(v[:, :, :], v[:, :, :], row(n2[:, :], D), ALU.mult).then_inc(S["ready"], 1)


def project_out(nc, sems, A, aT, lin):
    with ExitStack() as stack:
        s = Scope(nc, stack, sems)
        w = s.sb("w_o", [P, KD, D])
        bias = s.sb("b_o", [1, D])
        one = s.sb("one_o", [1, P])
        ps = s.ps("ps_po", [P, 8, BANK])
        loaded, made, full, out = s.sem("p_loaded"), s.sem("p_made"), s.sem("p_full"), s.sem("p_out")
        with nc.Block() as block:

            @block.sync
            def _(sp):
                sems.clear_last(sp)
                sp.dma_start(w[:, :, :], A["w_o"].rearrange("(k p) n -> p k n", p=P)).then_inc(loaded, 16)
                sp.dma_start(bias[:, :], A["b_o"]).then_inc(loaded, 16)

            @block.tensor
            def _(pe):
                pe.wait_ge(loaded, 32)
                pe.wait_ge(made, 1)
                for i in range(NT):
                    if i >= 8:
                        pe.wait_ge(out, i - 7)
                    for k in range(KD):
                        nc.tensor.matmul(ps[:, i % 8, 0:D], aT[:, k, i * P:(i + 1) * P], w[:, k, :], start=k == 0, stop=False)
                    nc.tensor.matmul(ps[:, i % 8, 0:D], one[0:1, :], bias[0:1, :], start=False, stop=True).then_inc(full, 1)

            @block.vector
            def _(dve):
                nc.vector.memset(one[:, :], 1.0).then_inc(made, 1)
                for i in range(NT):
                    dve.wait_ge(full, i + 1)
                    nc.vector.tensor_copy(lin[:, i, :], ps[:, i % 8, 0:D]).then_inc(out, 1)
                dve.wait_ge(out, NT)


def hyper_residual(nc, sems, tag, x, lin, ada, gate, out):
    with ExitStack() as stack:
        s = Scope(nc, stack, sems)
        sq = s.sb(tag + "sq", [P, NT, D])
        w = s.sb(tag + "w", [P, NT, D])
        col = {n: s.sb(tag + n, [P, NT])[:, :] for n in "nl x2 w2 xw rho n rn th tau y2 xy num den c1 c2".split()}
        link_v, link_a = s.sem(tag + "link_v"), s.sem(tag + "link_a")
        S = {n: s.sem(tag + n) for n in "sl nl rho sx x2 w sw n2 n th".split()}
        with nc.Block() as block:

            @block.sync
            def _(sp):
                sems.clear_last(sp)

            @block.scalar
            def _(act):
                count = [0]

                def link(ins):
                    count[0] += 1
                    ins.then_inc(link_a, 1)
                    act.wait_ge(link_a, count[0])

                nc.scalar.activation(sq[:, :, :], lin[:, :, :], ACT.Square).then_inc(S["sl"], 1)
                act.wait_ge(S["nl"], 1)
                link(nc.scalar.activation(col["rho"], col["nl"], ACT.Ln))
                nc.scalar.activation(col["rho"], col["rho"], ACT.Exp, scale=-0.5, bias=LN_A).then_inc(S["rho"], 1)
                nc.scalar.activation(sq[:, :, :], x[:, :, :], ACT.Square).then_inc(S["sx"], 1)
                act.wait_ge(S["w"], 1)
                act.wait_ge(S["x2"], 1)
                nc.scalar.activation(sq[:, :, :], w[:, :, :], ACT.Square).then_inc(S["sw"], 1)
                act.wait_ge(S["n2"], 1)
                link(nc.scalar.activation(col["th"], col["n"], ACT.Ln))
                link(nc.scalar.activation(col["rn"], col["th"], ACT.Exp, scale=-0.5))
                link(nc.scalar.activation(col["n"], col["th"], ACT.Exp, scale=0.5))
                nc.scalar.activation(col["th"], col["n"], ACT.Tanh).then_inc(S["th"], 1)

            @block.vector
            def _(dve):
                count = [0]

                def link(ins):
                    count[0] += 1
                    ins.then_inc(link_v, 1)
                    dve.wait_ge(link_v, count[0])

                c, V = col, nc.vector
                dve.wait_ge(S["sl"], 1)
                link(V.tensor_reduce(c["nl"], sq[:, :, :], AX.X, ALU.add))
                V.tensor_scalar(c["nl"], c["nl"], EPS * EPS, None, ALU.max).then_inc(S["nl"], 1)
                for b in range(B):
                    tiles = slice(b * TPB, (b + 1) * TPB)
                    link(V.tensor_tensor(w[:, tiles, :], lin[:, tiles, :],
                                         ada[:, b, gate, :].unsqueeze(1).broadcast_to([P, TPB, D]), ALU.mult))
                dve.sem_inc(S["w"], 1)
                dve.wait_ge(S["sx"], 1)
                V.tensor_reduce(c["x2"], sq[:, :, :], AX.X, ALU.add).then_inc(S["x2"], 1)
                dve.wait_ge(S["sw"], 1)
                link(V.tensor_reduce(c["w2"], sq[:, :, :], AX.X, ALU.add))
                link(V.tensor_tensor(sq[:, :, :], x[:, :, :], w[:, :, :], ALU.mult))
                link(V.tensor_reduce(c["xw"], sq[:, :, :], AX.X, ALU.add))
                dve.wait_ge(S["rho"], 1)
                link(V.tensor_scalar(c["rho"], c["rho"], 1.0, None, ALU.min))
                link(V.tensor_tensor(c["n"], c["rho"], c["rho"], ALU.mult))
                link(V.tensor_tensor(c["n"], c["n"], c["w2"], ALU.mult))
                V.tensor_scalar(c["n"], c["n"], EPS * EPS, None, ALU.max).then_inc(S["n2"], 1)
                dve.wait_ge(S["th"], 1)
                link(V.tensor_tensor(c["tau"], c["th"], c["rn"], ALU.mult))
                link(V.tensor_tensor(c["tau"], c["tau"], c["rho"], ALU.mult))
                link(V.tensor_tensor(c["xy"], c["tau"], c["xw"], ALU.mult))
                link(V.tensor_tensor(c["y2"], c["tau"], c["tau"], ALU.mult))
                link(V.tensor_tensor(c["y2"], c["y2"], c["w2"], ALU.mult))
                link(V.tensor_scalar(c["xy"], c["xy"], 2.0, 1.0, ALU.mult, ALU.add))
                link(V.tensor_tensor(c["num"], c["xy"], c["y2"], ALU.add))
                link(V.tensor_tensor(c["den"], c["x2"], c["y2"], ALU.mult))
                link(V.tensor_tensor(c["den"], c["den"], c["xy"], ALU.add))
                link(V.tensor_scalar(c["den"], c["den"], EPS, None, ALU.max))
                link(V.reciprocal(c["den"], c["den"]))
                link(V.tensor_tensor(c["c1"], c["num"], c["den"], ALU.mult))
                link(V.tensor_scalar(c["c2"], c["x2"], -1.0, 1.0, ALU.mult, ALU.add))
                link(V.tensor_tensor(c["c2"], c["c2"], c["tau"], ALU.mult))
                link(V.tensor_tensor(c["c2"], c["c2"], c["den"], ALU.mult))
                link(V.tensor_tensor(w[:, :, :], w[:, :, :], row(c["c2"], D), ALU.mult))
                link(V.tensor_tensor(sq[:, :, :], x[:, :, :], row(c["c1"], D), ALU.mult))
                link(V.tensor_tensor(out[:, :, :], sq[:, :, :], w[:, :, :], ALU.add))


def feed_forward(nc, sems, A, vT, lin):
    L, FC = BANK, FF // P
    TL = L // P
    with ExitStack() as stack:
        s = Scope(nc, stack, sems)
        w1 = s.sb("w_f1", [P, KD, FF])
        w2 = s.sb("w_f2", [P, FC, D])
        b1 = s.sb("b_f1", [P, FC])
        b2 = s.sb("b_f2", [1, D])
        b2_all = s.sb("b2_all", [P, D])
        ones = s.sb("ones_f", [P, P])
        h = s.sb("h_f", [P, FC, L])
        sq = s.sb("sq_f", [P, FC, L])
        nrow = s.sb("nrow", [1, N])
        n2 = s.sb("ff_n2", [P, NT])
        ps_h = s.ps("ps_h", [P, 2, BANK])
        ps_n = s.ps("ps_n", [P, 2, BANK])
        ps_o = s.ps("ps_fo", [P, TL, BANK])
        loaded = s.sem("f_loaded")
        S = {n: s.sem("f_" + n) for n in "ones h h_in sq n nrow out out_used ncol b2 b2_in lo n2 ln r".split()}
        NB = N // L
        with nc.Block() as block:

            @block.sync
            def _(sp):
                sems.clear_last(sp)
                sp.dma_start(w1[:, :, :], A["w_f1"].rearrange("(k p) n -> p k n", p=P)).then_inc(loaded, 16)
                sp.dma_start(b1[:, :], A["b_f1"]).then_inc(loaded, 16)
                sp.dma_start(b2[:, :], A["b_f2"]).then_inc(loaded, 16)
                sp.dma_start(w2[:, :, :], A["w_f2"].rearrange("(c p) n -> p c n", p=P)).then_inc(loaded, 16)

            @block.tensor
            def _(pe):
                pe.wait_ge(loaded, 64)
                pe.wait_ge(S["ones"], 1)
                nc.tensor.matmul(ps_n[:, 1, 0:D], ones[0:1, :], b2[0:1, :], start=True, stop=True).then_inc(S["b2"], 1)
                with pe.Fori(0, NB) as q:
                    for c in range(FC):
                        pe.wait_ge(S["h_in"], q * FC + (c + 1))
                        for k in range(KD):
                            last = nc.tensor.matmul(ps_h[:, c % 2, :], w1[:, k, c * P:(c + 1) * P],
                                                    vT[:, k, bass.ds(q * L, L)], start=k == 0, stop=k == KD - 1)
                        last.then_inc(S["h"], 1)
                    pe.wait_ge(S["h_in"], q * FC + (FC + 2))
                    pe.wait_ge(S["out_used"], q * TL + TL)
                    for m in range(TL):
                        for c in range(FC):
                            last = nc.tensor.matmul(ps_o[:, m, 0:D], h[:, c, m * P:(m + 1) * P], w2[:, c, :],
                                                    start=c == 0, stop=c == FC - 1)
                        last.then_inc(S["out"], 1)
                    pe.wait_ge(S["nrow"], q + 1)
                    for c in range(FC):
                        pe.wait_ge(S["sq"], q * FC + (c + 1))
                        last = nc.tensor.matmul(ps_n[0:1, 0, :], ones[:, 0:1], sq[:, c, :], start=c == 0, stop=c == FC - 1)
                    last.then_inc(S["n"], 1)
                pe.wait_ge(S["nrow"], NB + 1)
                pe.wait_ge(S["b2_in"], 1)
                for i in range(NT):
                    last = nc.tensor.matmul(ps_n[:, 1, i:i + 1], nrow[0:1, i * P:(i + 1) * P], ones[0:1, 0:1],
                                            start=True, stop=True)
                last.then_inc(S["ncol"], 1)

            @block.scalar
            def _(act):
                act.preload_act_table(ACT.Exp)
                act.sem_inc(S["h_in"], 2)
                act.sem_inc(S["nrow"], 1)
                act.wait_ge(loaded, 64)
                with act.Fori(0, NB) as q:
                    for c in range(FC):
                        act.wait_ge(S["h"], q * FC + (c + 1))
                        if c == 0:
                            act.wait_ge(S["lo"], q * TL + TL)
                        nc.scalar.activation(h[:, c, :], ps_h[:, c % 2, :], ACT.Identity,
                                             bias=b1[:, c:c + 1]).then_inc(S["h_in"], 1)
                    act.wait_ge(S["n"], q + 1)
                    nc.scalar.activation(nrow[0:1, bass.ds(q * L, L)], ps_n[0:1, 0, :], ACT.Copy).then_inc(S["nrow"], 1)
                act.wait_ge(S["n2"], 1)
                nc.scalar.activation(n2[:, :], n2[:, :], ACT.Ln).then_inc(S["ln"], 1)
                act.wait_ge(S["ln"], 1)
                nc.scalar.activation(n2[:, :], n2[:, :], ACT.Exp, scale=-0.5, bias=LN_A).then_inc(S["r"], 1)

            @block.vector
            def _(dve):
                nc.vector.memset(ones[:, :], 1.0).then_inc(S["ones"], 1)
                dve.sem_inc(S["out_used"], TL)
                dve.sem_inc(S["lo"], TL)
                dve.wait_ge(S["b2"], 1)
                nc.vector.tensor_copy(b2_all[:, :], ps_n[:, 1, 0:D]).then_inc(S["b2_in"], 1)
                with dve.Fori(0, NB) as q:
                    for c in range(FC):
                        dve.wait_ge(S["h_in"], q * FC + (c + 3))
                        nc.vector.tensor_tensor(sq[:, c, :], h[:, c, :], h[:, c, :], ALU.mult).then_inc(S["sq"], 1)
                    dve.wait_ge(S["n"], q + 1)
                    for m in range(TL):
                        dve.wait_ge(S["out"], q * TL + (m + 1))
                        nc.vector.tensor_scalar(lin[:, bass.ds(q * TL + m, 1), :], ps_o[:, m, 0:D], 1.0, None,
                                                ALU.mult).then_inc(S["out_used"], 1)
                        dve.sem_inc(S["lo"], 1)
                dve.wait_ge(S["ncol"], 1)
                nc.vector.tensor_scalar(n2[:, :], ps_n[:, 1, 0:NT], EPS * EPS, None, ALU.max).then_inc(S["n2"], 1)
                dve.wait_ge(S["r"], 1)
                nc.vector.tensor_scalar(n2[:, :], n2[:, :], 1.0, None, ALU.min).then_inc(S["b2_in"], 1)
                dve.wait_ge(S["b2_in"], 2)
                dve.wait_ge(S["out_used"], (NB + 1) * TL)
                nc.vector.tensor_tensor(lin[:, :, :], lin[:, :, :], row(n2[:, :], D), ALU.mult).then_inc(S["b2_in"], 1)
                dve.wait_ge(S["b2_in"], 3)
                nc.vector.tensor_tensor(lin[:, :, :], lin[:, :, :], b2_all[:, :].unsqueeze(1).broadcast_to([P, NT, D]),
                                        ALU.add).then_inc(S["b2_in"], 1)
                dve.wait_ge(S["b2_in"], 4)


def glu_ffn(nc, sems, A, ident, x1, x3, out):
    L, FC = BANK, FF // P
    TL = L // P
    with ExitStack() as stack:
        s = Scope(nc, stack, sems)
        xT = s.sb("x3T", [P, KD, N])
        w1 = s.sb("g_w1", [P, KD, FF])
        w2 = s.sb("g_w2", [P, KD, FF])
        h1 = s.sb("g_h1", [P, FC, FF])
        h2 = s.sb("g_h2", [P, FC, FF])
        w3 = s.sb("g_w3", [P, FC, D])
        sc = s.sb("g_sc", [P, 4, FC])
        s3 = s.sb("g_s3", [1, D])
        s3_all = s.sb("g_s3_all", [P, D])
        one = s.sb("g_one", [1, P])
        sil = s.sb("g_sil", [P, 2, L])
        ha = s.sb("g_ha", [P, FC, L])
        hb = s.sb("g_hb", [P, FC, L])
        y = s.sb("g_y", [P, 2, TL, D])
        ps = s.ps("ps_glu", [P, 8, BANK])
        loaded, h_loaded, t_done = s.sem("g_loaded"), s.sem("g_h_loaded"), s.sem("g_t")
        xT_in, s3_in, s3_ps, one_in = s.sem("g_xT"), s.sem("g_s3_in"), s.sem("g_s3_ps"), s.sem("g_one_in")
        S = {n: s.sem("g_" + n) for n in "a b sil glu l1 ga l2 gb o y1 y stored0 stored1".split()}
        NB = N // L
        with nc.Block() as block:

            @block.sync
            def _(sp):
                sems.clear_last(sp)
                for dst, name in ((w1, "w1T"), (w2, "w2T")):
                    sp.dma_start(dst[:, :, :], A[name].rearrange("(k p) n -> p k n", p=P)).then_inc(loaded, 16)
                sp.dma_start(sc[:, :, :], A["ffn_s"]).then_inc(loaded, 16)
                sp.dma_start(s3[:, :], A["w3_s"]).then_inc(loaded, 16)
                for dst, name in ((h1, "h1T"), (h2, "h2T"), (w3, "w3T")):
                    sp.dma_start(dst[:, :, :], A[name].rearrange("(k p) n -> p k n", p=P)).then_inc(h_loaded, 16)
                out_v = out.rearrange("(q m p) d -> p q m d", p=P, m=TL)
                with sp.Fori(0, NB - 1, 2) as q0:
                    for u in range(2):
                        q = q0 + u
                        sp.wait_ge(S["y"], (q + 1) * TL)
                        sp.dma_start(out_v[:, bass.ds(q, 1), :, :].rearrange("p q m d -> p (q m) d"),
                                     y[:, u, :, :]).then_inc(S[f"stored{u}"], 16)
                for u in range(2):
                    sp.wait_ge(S[f"stored{u}"], 16 + 16 * NB // 2)

            @block.tensor
            def _(pe):
                for i in range(NT):
                    for k in range(KD):
                        at = (i % 2 * KD + k) * P
                        last = nc.tensor.transpose(ps[:, i // 2 % 8, at:at + P], x3[:, i, k * P:(k + 1) * P], ident[:, :])
                    if i % 2:
                        last.then_inc(t_done, 1)
                pe.wait_ge(loaded, 64)
                pe.wait_ge(one_in, 1)
                pe.sem_inc(S["o"], 1)
                pe.wait_ge(xT_in, NT // 2)
                nc.tensor.matmul(ps[:, 0, 0:D], one[0:1, :], s3[0:1, :], start=True, stop=True).then_inc(s3_ps, 1)
                pe.wait_ge(s3_in, 1)
                pe.wait_ge(h_loaded, 48)
                with pe.Fori(0, NB) as q:
                    for c in range(FC):
                        pe.wait_ge(S["glu"], q * FC + (c + 1))
                        for w, at, done in ((w1, 0, "a"), (w2, 1, "b")):
                            for k in range(KD):
                                last = nc.tensor.matmul(ps[:, c % 2 * 2 + at, :], w[:, k, c * P:(c + 1) * P],
                                                        xT[:, k, bass.ds(q * L, L)], start=k == 0, stop=k == KD - 1)
                            last.then_inc(S[done], 1)
                    for w, src, before, done, after, bank in ((h1, ha, "glu", "l1", "ga", 4), (h2, hb, "ga", "l2", "gb", 6)):
                        pe.wait_ge(S[before], q * FC + (FC + 2))
                        for c in range(FC):
                            pe.wait_ge(S[after], q * FC + (c + 1))
                            for k in range(FC):
                                last = nc.tensor.matmul(ps[:, bank + c % 2, :], w[:, k, c * P:(c + 1) * P], src[:, k, :],
                                                        start=k == 0, stop=k == FC - 1)
                            last.then_inc(S[done], 1)
                    pe.wait_ge(S["gb"], q * FC + (FC + 2))
                    for m in range(TL):
                        for c in range(FC):
                            last = nc.tensor.matmul(ps[:, m, 0:D], ha[:, c, m * P:(m + 1) * P], w3[:, c, :],
                                                    start=c == 0, stop=c == FC - 1)
                        last.then_inc(S["o"], 1)
                    pe.wait_ge(S["y1"], (q + 1) * TL)

            @block.scalar
            def _(act):
                for i in range(0, NT, 2):
                    act.wait_ge(t_done, i // 2 + 1)
                    nc.scalar.activation(
                        xT[:, :, i * P:(i + 2) * P].rearrange("p k (i t) -> p i k t", i=2),
                        ps[:, i // 2 % 8, :].rearrange("p (i k t) -> p i k t", i=2, k=KD), ACT.Copy).then_inc(xT_in, 1)
                act.wait_ge(loaded, 64)
                act.sem_inc(S["ga"], 2)
                act.sem_inc(S["gb"], 2)
                with act.Fori(0, NB) as q:
                    for c in range(FC):
                        act.wait_ge(S["a"], q * FC + (c + 1))
                        act.wait_ge(S["glu"], q * FC + (c + 1))
                        nc.scalar.activation(sil[:, c % 2, :], ps[:, c % 2 * 2, :], ACT.Silu,
                                             scale=sc[:, 0, c:c + 1]).then_inc(S["sil"], 1)
                    for c in range(FC):
                        act.wait_ge(S["l1"], q * FC + (c + 1))
                        nc.scalar.activation(hb[:, c, :], ps[:, 4 + c % 2, :], ACT.Gelu,
                                             scale=sc[:, 2, c:c + 1]).then_inc(S["ga"], 1)
                    for c in range(FC):
                        act.wait_ge(S["l2"], q * FC + (c + 1))
                        nc.scalar.activation(ha[:, c, :], ps[:, 6 + c % 2, :], ACT.Gelu,
                                             scale=sc[:, 3, c:c + 1]).then_inc(S["gb"], 1)

            @block.vector
            def _(dve):
                nc.vector.memset(one[:, :], 1.0).then_inc(one_in, 1)
                dve.wait_ge(s3_ps, 1)
                nc.vector.tensor_copy(s3_all[:, :], ps[:, 0, 0:D]).then_inc(s3_in, 1)
                dve.wait_ge(s3_in, 1)
                dve.wait_ge(loaded, 64)
                dve.sem_inc(S["glu"], 2)
                dve.sem_inc(S["stored0"], 16)
                dve.sem_inc(S["stored1"], 16)
                with dve.Fori(0, NB - 1, 2) as q0:
                    for u in range(2):
                        q = q0 + u
                        for c in range(FC):
                            dve.wait_ge(S["sil"], q * FC + (c + 1))
                            dve.wait_ge(S["b"], q * FC + (c + 1))
                            if c == 0:
                                dve.wait_ge(S["o"], q * TL + 1)
                            nc.vector.scalar_tensor_tensor(ha[:, c, :], ps[:, c % 2 * 2 + 1, :], sc[:, 1, c:c + 1],
                                                           sil[:, c % 2, :], ALU.mult, ALU.mult).then_inc(S["glu"], 1)
                        dve.wait_ge(S[f"stored{u}"], q0 * 8 + 16)
                        for m in range(TL):
                            dve.wait_ge(S["o"], q * TL + (m + 2))
                            nc.vector.tensor_tensor(y[:, u, m, :], ps[:, m, 0:D], s3_all[:, :], ALU.mult).then_inc(S["y1"], 1)
                            dve.wait_ge(S["y1"], q * TL + (m + 1))
                            nc.vector.tensor_tensor(y[:, u, m, :], y[:, u, m, :],
                                                    x1[:, bass.ds(q * TL + m, 1), :].rearrange("p i d -> p (i d)"),
                                                    ALU.add).then_inc(S["y"], 1)


def hyperbolic_block(nc, sems, A, ident, x1, x3):
    with ExitStack() as stack:
        s = Scope(nc, stack)
        ada = s.sb("ada", [P, B, 6, D])
        ada_rows(nc, sems, A, ada)
        with ExitStack() as inner:
            heads = ExitStack()
            s2 = Scope(nc, heads)
            va = s2.sb("va", [P, NT, H, HD], side="right")
            qT = s2.sb("qT", [P, H // 2, N], F16, side="right")
            kT = s2.sb("kT", [P, H // 2, N], F16, side="right")
            with ExitStack() as first:
                s3 = Scope(nc, first)
                vT = s3.sb("vT", [P, KD, N])
                ident16 = s3.sb("ident16", [P, P], F16)
                scratch = x3[:, :, :].rearrange("p i d -> p (i d)")
                sums = 4 * 3 * D
                norm_modulate(nc, sems, "n1_", x1, ada, 0, ident, vT)
                qkv(nc, sems, A, ident16, vT, qT, kT, va, scratch[:, 0:sums].rearrange("p (i n) -> p i n", i=4),
                    scratch[:, sums:sums + NT * 3 * H].rearrange("p (i h) -> p i h", h=H))
            oT = Scope(nc, inner).sb("oT", [P, 4, N])
            attention(nc, sems, qT, kT, va, oT)
            heads.close()
            aT = Scope(nc, inner).sb("aT", [P, KD, N])
            heads_out(nc, sems, ident, oT, aT, x3)
            project_out(nc, sems, A, aT, x3)
        lin = s.sb("lin", [P, NT, D])
        hyper_residual(nc, sems, "r1_", x1, x3, ada, 2, x3)
        with ExitStack() as inner:
            s2 = Scope(nc, inner)
            vT = s2.sb("vT2", [P, KD, N])
            norm_modulate(nc, sems, "n2_", x3, ada, 3, ident, vT)
            feed_forward(nc, sems, A, vT, lin)
        hyper_residual(nc, sems, "r2_", x3, lin, ada, 5, x3)


def build(nc, A, out):
    sems = Semaphores(nc)
    with ExitStack() as stack:
        s = Scope(nc, stack)
        ident = s.sb("ident", [P, P])
        x1 = s.sb("x1", [P, NT, D])
        with ExitStack() as inner:
            hist = Scope(nc, inner).sb("hist", [P, T, KD, B])
            with ExitStack() as first:
                s2 = Scope(nc, first)
                xw = s2.sb("xw", [P, T, G8 * B])
                wq = s2.sb("wq", [P, 2, KD, 4 * D], F16)
                gate_scale = s2.sb("gate_scale", [P, 1])
                lstm_inputs(nc, sems, A, xw, wq, gate_scale, ident)
                lstm(nc, sems, xw, wq, gate_scale, ident, hist)
            mamba(nc, sems, A, ident, hist, x1)
        x3 = s.sb("x3", [P, NT, D])
        hyperbolic_block(nc, sems, A, ident, x1, x3)
        glu_ffn(nc, sems, A, ident, x1, x3, out)



def kernel(**inputs):
    import concourse.bacc as bacc
    from concourse.bass_utils import run_bass_kernel_spmd

    a = {k.replace("L0_", ""): np.asarray(v) for k, v in inputs.items()}

    def chunks(v):
        v = v.reshape((-1, P) + v.shape[1:])
        return np.moveaxis(v, 0, 1)

    def gates(w):
        return np.concatenate([w[..., 0:2 * D], w[..., 3 * D:4 * D], w[..., 2 * D:3 * D]], axis=-1)

    x = a["x"].reshape(N, D)
    arrays = {
        "x": x, "xT": x.T, "condT": a["cond_1024"].T,
        "Wx": gates(a["cond_Wx"]), "Wh": gates(a["cond_Wh"]), "b": chunks(gates(a["cond_b"])),
        "ident": np.eye(P, dtype=np.float32), "ident16": np.eye(P, dtype=np.float16),
        "norm_w": chunks(a["attn_norm_w"]), "w_in": a["attn_W_in"], "conv_w": chunks(a["attn_conv_w"][:, 0, :]),
        "conv_b": chunks(a["attn_conv_b"]), "w_x": a["attn_W_x"], "w_dt": chunks(a["attn_w_dt"]),
        "b_dt": chunks(a["attn_b_dt"]), "a_log": chunks(a["attn_A_log"]), "d_par": chunks(a["attn_D_param"]),
        "w_out": a["attn_W_out"],
        "w_qkv": np.concatenate([a["cond2_w_q"], a["cond2_w_k"], a["cond2_w_v"]], axis=1),
        "b_qkv": np.concatenate([a["cond2_b_q"], a["cond2_b_k"], a["cond2_b_v"]])[None, :],
        "w_o": a["cond2_w_o"], "b_o": a["cond2_b_o"][None, :], "w_f1": a["cond2_w_f1"], "b_f1": chunks(a["cond2_b_f1"]),
        "w_f2": a["cond2_w_f2"], "b_f2": a["cond2_b_f2"][None, :], "w_ada": a["cond2_w_ada"], "b_ada": a["cond2_b_ada"][None, :],
        "w1T": a["ffn_w1_w"].T, "w2T": a["ffn_w2_w"].T, "h1T": a["ffn_h1_w"].T, "h2T": a["ffn_h2_w"].T, "w3T": a["ffn_w3_w"].T,
        "w3_s": a["ffn_w3_s"][None, :],
        "ffn_s": np.stack([chunks(a["ffn_" + n]) for n in ("w1_s", "w2_s", "h1_s", "h2_s")], axis=1),
    }
    arrays = {f"in_{k}": np.ascontiguousarray(v) for k, v in arrays.items()}
    nc = bacc.Bacc("TRN2", target_bir_lowering=False, num_devices=1)
    A = {k[3:]: nc.dram_tensor(k, v.shape, mybir.dt.from_np(v.dtype), kind="ExternalInput").ap() for k, v in arrays.items()}
    out = nc.dram_tensor("out_0_dram", (N, D), F32, kind="ExternalOutput").ap()
    build(nc, A, out)
    r = run_bass_kernel_spmd(nc, [arrays], core_ids=[0])
    return r.results[0]["out_0_dram"].reshape(B, T, D)
```

```python
import math
from contextlib import ExitStack

import numpy as np

import concourse.bass as bass
from concourse import mybir

F32 = mybir.dt.float32
F16 = mybir.dt.float16
I32 = mybir.dt.int32
ALU = mybir.AluOpType
ACT = mybir.ActivationFunctionType
AX = mybir.AxisListType

P = 128
B, T, D = 2, 1024, 256
N = B * T
KD = D // P
NT = N // P
BANK = 512
G8 = 4 * D // P
HC = KD * B
HEXP = 14
DI, DS, DCONV = 512, 16, 4
CI = DI // P


class Semaphores:

    def __init__(self, nc):
        self.nc, self.cleared, self.last, self.now = nc, [], [], []

    def new(self, name):
        guard = self.nc.semaphore(name)
        sem = guard.__enter__()
        self.now.append((guard, sem))
        return sem

    def next_stage(self):
        for guard, _ in self.cleared:
            guard.__exit__(None, None, None)
        self.cleared, self.last, self.now = self.last, self.now, []

    def clear_last(self, sp):
        for _, sem in self.last:
            sp.sem_clear(sem)


class Scope:

    def __init__(self, nc, stack, sems=None):
        self.nc, self.stack, self.sems = nc, stack, sems
        if sems:
            sems.next_stage()

    def sb(self, name, shape, dtype=F32, side="left"):
        return self.stack.enter_context(self.nc.sbuf_tensor(name, shape, dtype, side=side))

    def ps(self, name, shape, dtype=F32):
        return self.stack.enter_context(self.nc.psum_tensor(name, shape, dtype))

    def sem(self, name):
        return self.sems.new(name)


def lstm_inputs(nc, sems, A, xw, wq, gate_scale, ident):
    with ExitStack() as stack:
        s = Scope(nc, stack, sems)
        xT = s.sb("xT", [P, KD, N])
        wx = s.sb("wx", [P, KD, 4 * D])
        wh = s.sb("wh", [P, KD, 4 * D])
        ws = s.sb("ws", [P, KD, 4 * D])
        bias = s.sb("bias", [P, G8])
        bias_k = s.sb("bias_k", [P, G8])
        h0 = s.sb("h0", [P, KD, B])
        pmax = s.sb("pmax", [P, 1])
        wmax = s.sb("wmax", [P, 1])
        wmax_c = s.sb("wmax_c", [P, 1])
        pow2 = s.sb("pow2", [P, 1], I32)
        sc = s.sb("sc", [P, 2])
        kk = s.sb("kk", [P, 2])
        ps = s.ps("ps_in", [P, 8, BANK])
        loaded, wh_loaded = s.sem("a_loaded"), s.sem("a_wh_loaded")
        pmax_ready, wmax_ready, chain = s.sem("a_pmax"), s.sem("a_wmax"), s.sem("a_chain")
        scales_ready = s.sem("a_scales")
        bank_full, bank_free = s.sem("a_full"), s.sem("a_free")
        h0_product, scaled, split, evac = s.sem("a_h0"), s.sem("a_scaled"), s.sem("a_split"), s.sem("a_evac")
        TB = T // BANK
        HALF = (0, 1, 2, 3, 6, 7)
        with nc.Block() as block:

            @block.sync
            def _(sp):
                sems.clear_last(sp)
                sp.dma_start(wh[:, :, :], A["Wh"].rearrange("(k p) n -> p k n", p=P)).then_inc(wh_loaded, 16)
                sp.dma_start(wx[:, :, :], A["Wx"].rearrange("(k p) n -> p k n", p=P)).then_inc(loaded, 16)
                sp.dma_start(xT[:, :, :], A["xT"].rearrange("(k p) n -> p k n", p=P)).then_inc(loaded, 16)
                sp.dma_start(bias[:, :], A["b"]).then_inc(loaded, 16)
                sp.dma_start(h0[:, :, :], A["condT"].rearrange("(k p) b -> p k b", p=P)).then_inc(loaded, 16)
                sp.dma_start(ident[:, :], A["ident"]).then_inc(loaded, 16)

            @block.gpsimd
            def _(pool):
                pool.wait_ge(pmax_ready, 1)
                nc.gpsimd.partition_all_reduce(wmax[:, :], pmax[:, :], P,
                                               bass.bass_isa.ReduceOp.max).then_inc(wmax_ready, 1)

            @block.tensor
            def _(pe):
                pe.wait_ge(loaded, 16 * 5)
                with pe.Fori(0, TB) as tb:
                    for b in range(B):
                        for g in range(G8):
                            i = b * G8 + g
                            pe.wait_ge(bank_free, tb * (B * G8) + (i + 1))
                            for k in range(KD):
                                last = nc.tensor.matmul(ps[:, i % 8, :], wx[:, k, g * P:(g + 1) * P],
                                                        xT[:, k, bass.ds(tb * BANK + b * T, BANK)],
                                                        start=k == 0, stop=k == KD - 1)
                            last.then_inc(bank_full, 1)
                pe.wait_ge(wh_loaded, 16)
                pe.wait_ge(bank_free, TB * B * G8 + 1)
                for g in range(G8):
                    for k in range(KD):
                        last = nc.tensor.matmul(ps[:, 0, g * B:(g + 1) * B], wh[:, k, g * P:(g + 1) * P],
                                                h0[:, k, :], start=k == 0, stop=k == KD - 1)
                last.then_inc(h0_product, 1)

            @block.scalar
            def _(act):
                act.preload_act_table(ACT.Identity)
                act.sem_inc(bank_free, 8)
                act.wait_ge(scales_ready, 1)
                with act.Fori(0, TB) as tb:
                    for b in range(B):
                        for g in range(G8):
                            i = b * G8 + g
                            act.wait_ge(bank_full, tb * (B * G8) + (i + 1))
                            half = int(g in HALF)
                            nc.scalar.activation(xw[:, bass.ds(tb * BANK, BANK), g * B + b], ps[:, i % 8, :],
                                                 ACT.Identity, bias=bias_k[:, g:g + 1],
                                                 scale=kk[:, half:half + 1]).then_inc(bank_free, 1)

            @block.vector
            def _(dve):
                dve.wait_ge(wh_loaded, 16)
                nc.vector.tensor_scalar(ws[:, :, :], wh[:, :, :], -1.0, None, ALU.mult).then_inc(chain, 1)
                dve.wait_ge(chain, 1)
                nc.vector.tensor_tensor(ws[:, :, :], ws[:, :, :], wh[:, :, :], ALU.max).then_inc(chain, 1)
                dve.wait_ge(chain, 2)
                nc.vector.tensor_reduce(pmax[:, :], ws[:, :, :].rearrange("p k n -> p (k n)"),
                                        AX.X, ALU.max).then_inc(pmax_ready, 1)
                dve.wait_ge(wmax_ready, 1)
                nc.vector.tensor_scalar(wmax_c[:, :], wmax[:, :], 2.0 ** -40, 2.0 ** 100,
                                        ALU.max, ALU.min).then_inc(chain, 1)
                dve.wait_ge(chain, 3)
                nc.vector.tensor_scalar(pow2[:, :], wmax_c[:, :].bitcast(I32), 0x7F800000, None,
                                        ALU.bitwise_and).then_inc(chain, 1)
                dve.wait_ge(chain, 4)
                for col, e in ((0, 267), (1, 266)):
                    nc.vector.tensor_scalar(sc[:, col:col + 1].bitcast(I32), pow2[:, :], -1.0, float(e << 23),
                                            ALU.mult, ALU.add).then_inc(chain, 1)
                for col, e in ((0, 267 + HEXP), (1, 266 + HEXP)):
                    nc.vector.tensor_scalar(kk[:, col:col + 1].bitcast(I32), pow2[:, :], -1.0, float(e << 23),
                                            ALU.mult, ALU.add).then_inc(chain, 1)
                nc.vector.tensor_scalar(gate_scale[:, :].bitcast(I32), pow2[:, :], 1.0, -float((13 + HEXP) << 23),
                                        ALU.mult, ALU.add).then_inc(chain, 1)
                dve.wait_ge(chain, 9)
                dve.wait_ge(loaded, 16 * 5)
                nc.vector.tensor_scalar(bias_k[:, 0:4], bias[:, 0:4], kk[:, 1:2], None, ALU.mult).then_inc(chain, 1)
                nc.vector.tensor_scalar(bias_k[:, 4:6], bias[:, 4:6], kk[:, 0:1], None, ALU.mult).then_inc(chain, 1)
                nc.vector.tensor_scalar(bias_k[:, 6:8], bias[:, 6:8], kk[:, 1:2], None, ALU.mult).then_inc(chain, 1)
                dve.wait_ge(chain, 12)
                dve.sem_inc(scales_ready, 1)
                for lo, hi, half in ((0, 4, 1), (4, 6, 0), (6, 8, 1)):
                    nc.vector.tensor_scalar(ws[:, :, lo * P:hi * P], wh[:, :, lo * P:hi * P],
                                            sc[:, half:half + 1], None, ALU.mult).then_inc(scaled, 1)
                dve.wait_ge(scaled, 3)
                nc.vector.tensor_copy(wq[:, 0, :, :], ws[:, :, :]).then_inc(split, 1)
                dve.wait_ge(split, 1)
                nc.vector.tensor_tensor(wq[:, 1, :, :], ws[:, :, :], wq[:, 0, :, :], ALU.subtract).then_inc(split, 1)
                dve.wait_ge(h0_product, 1)
                dve.wait_ge(bank_free, 8 + TB * B * G8)
                for lo, hi, half in ((0, 4, 1), (4, 6, 0), (6, 8, 1)):
                    c = slice(lo * B, hi * B)
                    nc.vector.scalar_tensor_tensor(xw[:, 0, c], ps[:, 0, c], kk[:, half:half + 1], xw[:, 0, c],
                                                   ALU.mult, ALU.add).then_inc(evac, 1)
                dve.wait_ge(evac, 3)


def row(ap, width):
    return ap.unsqueeze(len(ap.shape)).broadcast_to(list(ap.shape) + [width])


def lstm_mamba(nc, sems, A, xw, wq, gate_scale, ident, hist, x1, W):
    IFG, O = 6 * B, 2 * B
    LB = 128
    NB = T // LB
    L = B * LB
    U = DS * CI
    PE_U, ACT_U, DVE_U = 37, 35, 36
    HALF = 2.0 ** (HEXP - 1)
    with ExitStack() as stack:
        s_ = Scope(nc, stack, sems)
        gates = s_.sb("gates", [P, 2, IFG + HC])
        pre = s_.sb("pre", [P, IFG])
        pre_o = s_.sb("pre_o", [P, O])
        pre_x = s_.sb("pre_x", [P, O])
        xo = s_.sb("xo", [P, O])
        og = s_.sb("og", [P, O])
        og1 = s_.sb("og1", [P, O])
        prod = s_.sb("prod", [P, 2 * HC])
        tc = s_.sb("tc", [P, HC])
        h16 = s_.sb("h16", [P, 2, KD, 2, B], F16)
        hs = s_.sb("hs", [P, KD, B, LB])
        msv = s_.sb("msv", [P, B])
        minus_half = s_.sb("minus_half", [P, B])
        one2 = s_.sb("one2", [P, B])
        rstd = s_.sb("rstd", [P, B])
        rstd_b = s_.sb("rstd_b", [P, B, P])
        xn = s_.sb("xn", [P, KD, L])
        xp = s_.sb("xp", [P, CI, B, DCONV - 1 + LB])
        acc = s_.sb("acc", [P, CI, B, LB])
        th = s_.sb("th", [P, CI, L])
        xc = s_.sb("xc", [P, CI, L])
        par = s_.sb("par", [2 * DS + 1, L])
        rows = s_.sb("rows", [1, DS + 1, 2, L])
        dt = s_.sb("dt", [P, CI, L])
        uu = s_.sb("uu", [P, CI, L])
        ab = s_.sb("ab", [P, CI, L])
        bx = s_.sb("bx", [P, CI, L])
        hh = s_.sb("hh", [P, CI, L])
        cb = s_.sb("cb", [P, 2, L])
        sq = cb.rearrange("p k (b t) -> p k b t", b=B)
        hc = s_.sb("hc", [P, 2, L])
        state = s_.sb("state", [P, CI, B, DS])
        y = s_.sb("y", [P, CI, L])
        hf = s_.sb("hf", [P, HC])
        v = acc.rearrange("p c b t -> p c (b t)")
        w_in, conv_w, conv_b, w_dt, b_dt, w_x, norm_w, ones, a_neg, d_par, w_out = W
        ps_g, ps_o = s_.ps("ps_g", [P, BANK]), s_.ps("ps_o", [P, BANK])
        ps_z = s_.ps("ps_z", [P, 2, BANK])
        ps_b = s_.ps("ps_b", [P, 2, BANK])
        ps_c = s_.ps("ps_c", [P, 2, BANK])
        h_kept, xo_in = s_.sem("h_kept"), s_.sem("xo_in")
        ready = s_.sem("ready")
        ifg_sum, o_sum, ifg_pre, o_pre0, o_pre = (s_.sem(n) for n in ("ifg_sum", "o_sum", "ifg_pre", "o_pre0", "o_pre"))
        ifg_gate, o_gate, o_scaled = s_.sem("ifg_gate"), s_.sem("o_gate"), s_.sem("o_scaled")
        p_ready, cell, tanh_c = s_.sem("p_ready"), s_.sem("cell"), s_.sem("tanh_c")
        h_parts, h_ready = s_.sem("h_parts"), s_.sem("h_ready")
        S = {n: s_.sem("m_" + n) for n in (
            "init mh hs sq ms msv rstd rb xn xproj xp tap halo th xc prm par rows_in dtb v abs exp ln dt u xd y0 "
            "b_row c_row cb ab bx scan state kept hc y z thz z2 yz out x1").split()}

        with nc.Block() as block:

            @block.sync
            def _(sp):
                sems.clear_last(sp)
                with sp.Fori(0, NB) as j:
                    sp.wait_ge(S["par"], j + 1)
                    for bc in range(2):
                        sp.dma_start(rows[0:1, 0:DS, bc, :], par[1 + bc * DS:1 + (bc + 1) * DS, :]).then_inc(S["rows_in"], 16)

            @block.gpsimd
            def _(pool):
                nc.gpsimd.memset(minus_half[:, :], -0.5).then_inc(S["mh"], 1)
                nc.gpsimd.memset(one2[:, :], 1.0).then_inc(S["mh"], 1)
                pool.wait_ge(S["mh"], 2)
                with pool.Fori(0, NB) as j:
                    pool.wait_ge(S["hs"], j + 1)
                    nc.gpsimd.tensor_tensor(sq[:, :, :, :], hs[:, :, :, :], hs[:, :, :, :], ALU.mult).then_inc(S["sq"], 1)
                    pool.wait_ge(S["msv"], j + 1)
                    nc.gpsimd.tensor_tensor(rstd[:, :], msv[:, :], minus_half[:, :], ALU.pow).then_inc(S["rstd"], 1)
                    for c in range(CI):
                        pool.wait_ge(S["xc"], j * 2 + (c // 2 + 1))
                        nc.gpsimd.tensor_tensor(y[:, c, :], xc[:, c, :], d_par[:, c:c + 1].broadcast_to([P, L]),
                                                ALU.mult).then_inc(S["xd"], 1)
                    for c in range(CI):
                        pool.wait_ge(S["dt"], j * 2 + (c // 2 + 1))
                        nc.gpsimd.tensor_tensor(uu[:, c, :], dt[:, c, :], xc[:, c, :], ALU.mult).then_inc(S["u"], 1)
                    with pool.Fori(0, DS - 1, 2) as n0:
                        for i in range(2 * CI):
                            g, c = j * U + n0 * CI + i, i % CI
                            if c == 0:
                                pool.wait_ge(S["cb"], j * DS + n0 + (i // CI + 2))
                            pool.wait_ge(S["scan"], g * 2 + 10)
                            nc.gpsimd.tensor_tensor(state[:, c, :, bass.ds(n0 + i // CI, 1)].rearrange("p b n -> p (b n)"),
                                                    hh[:, c, :].rearrange("p (b t) -> p b t", b=B)[:, :, LB - 1:LB]
                                                    .rearrange("p b t -> p (b t)"), one2[:, :], ALU.mult).then_inc(S["state"], 1)
                            nc.gpsimd.tensor_tensor(hc[:, c % 2, :], hh[:, c, :], cb[:, i // CI, :],
                                                    ALU.mult).then_inc(S["hc"], 1)
                            pool.wait_ge(S["hc"], g + 9)
                            pool.wait_ge(S["xd"], j * CI + (c + 1))
                            pool.wait_ge(S["y"], g + 5)
                            nc.gpsimd.tensor_tensor(y[:, c, :], y[:, c, :], hc[:, c % 2, :], ALU.add).then_inc(S["y"], 1)
                            pool.wait_ge(S["state"], g + 1)
                            pool.sem_inc(S["kept"], 1)

            @block.tensor
            def _(pe):
                def lstm_products(t, u, extra):
                    pe.wait_ge(ifg_pre, t + 1)
                    nc.tensor.matmul(ps_g[:, 0:IFG], ident[:, :], xw[:, bass.ds(t, 1), 0:IFG],
                                     start=True, stop=False, skip_group_check=True)
                    extra()
                    pe.wait_ge(h_ready, t + 1)
                    for g in range(G8):
                        bank, at, width, done = (ps_g, g * B, IFG, ifg_sum) if g < 6 else (ps_o, (g - 6) * B, O, o_sum)
                        cols = bank[:, 0:2 * width].rearrange("p (h c) -> p h c", h=2)[:, :, at:at + B]
                        for k in range(KD):
                            for w in range(2):
                                last = nc.tensor.matmul(cols, wq[:, w, k, g * P:(g + 1) * P], h16[:, u, k, :, :],
                                                        start=g == 6 and k == 0 and w == 0,
                                                        stop=k == KD - 1 and w == 1, skip_group_check=True)
                        if g in (5, 7):
                            last.then_inc(done, 1)

                def b_row(m, n, bx_done):
                    pe.wait_ge(S["bx"], bx_done)
                    nc.tensor.matmul(ps_b[:, m, 0:L], ones[0:1, :], n(0), start=True, stop=True).then_inc(S["b_row"], 1)

                def c_row(m, n, cb_done):
                    pe.wait_ge(S["cb"], cb_done)
                    nc.tensor.matmul(ps_c[:, m, 0:L], ones[0:1, :], n(1), start=True, stop=True).then_inc(S["c_row"], 1)

                def part1(s, j):
                    if s in (3, 4):
                        b = s - 3
                        pe.wait_ge(S["sq"], j + 1)
                        for k in range(KD):
                            last = nc.tensor.matmul(ps_c[:, 0, b:b + 1], sq[:, k, b, :], ones[:, 0:1],
                                                    start=k == 0 and b == 0, stop=k == KD - 1, skip_group_check=True)
                        last.then_inc(S["ms"], 1)
                    elif s == 7:
                        pe.wait_ge(S["rb"], j + 1)
                        for b in range(B):
                            last = nc.tensor.matmul(ps_c[:, 0, b * LB:(b + 1) * LB], rstd_b[:, b, :], ident[:, :],
                                                    start=b == 0, stop=True, skip_group_check=True)
                        last.then_inc(S["ms"], 1)
                    elif 10 <= s < 18:
                        c, k = (s - 10) // 2, (s - 10) % 2
                        if k == 0:
                            pe.wait_ge(S["xn"], j * KD + KD)
                            pe.wait_ge(S["xp"], j * CI + (c + 1))
                        last = nc.tensor.matmul(ps_c[:, (c + 1) % 2, 0:L], w_in[:, k, c * P:(c + 1) * P], xn[:, k, :],
                                                start=k == 0, stop=k == KD - 1)
                        if k:
                            last.then_inc(S["xproj"], 1)
                    elif 24 <= s < 28:
                        c = s - 24
                        pe.wait_ge(S["xc"], j * 2 + (c // 2 + 1))
                        if c == 0:
                            pe.wait_ge(S["xp"], j * CI + (CI + 2))
                        last = nc.tensor.matmul(ps_c[0:2 * DS + 1, 0, 0:L], w_x[:, c, :], xc[:, c, :],
                                                start=c == 0, stop=c == CI - 1)
                        if c == CI - 1:
                            last.then_inc(S["prm"], 1)
                    elif s == 29:
                        pe.wait_ge(S["par"], j + 1)
                        nc.tensor.matmul(ps_c[:, 1, 0:L], ones[0:1, :], par[0:1, :], start=True, stop=True).then_inc(S["dtb"], 1)
                    elif s == 33:
                        pe.wait_ge(S["rows_in"], j * 32 + 32)
                        pe.wait_ge(S["v"], j * CI + CI)
                        c_row(0, lambda bc: rows[0:1, 0, bc, :], j * DS + 1)
                    elif s == 34:
                        b_row(0, lambda bc: rows[0:1, 0, bc, :], j * U + 4)

                def unit(j, n0, i):
                    c, nxt = i % CI, i // CI + 1
                    row_of = lambda bc: rows[0:1, bass.ds(n0 + nxt, 1), bc, :]
                    if c == 0:
                        c_row(nxt % 2, row_of, j * DS + n0 + nxt)
                    elif c == 1:
                        b_row(nxt % 2, row_of, j * U + n0 * CI + nxt * CI)

                def part3(s, j):
                    if 101 <= s < 109:
                        c, k = (s - 101) // 2, (s - 101) % 2
                        if k == 0:
                            pe.wait_ge(S["z2"], j * CI + (c + 1))
                        last = nc.tensor.matmul(ps_z[:, c % 2, 0:L], w_in[:, k, DI + c * P:DI + (c + 1) * P], xn[:, k, :],
                                                start=k == 0, stop=k == KD - 1)
                        if k:
                            last.then_inc(S["z"], 1)
                    elif 109 <= s < 119:
                        b, part = (s - 109) // 5, (s - 109) % 5
                        if part == 0:
                            pe.wait_ge(S["cb"], j * DS + (DS + 1))
                            for k in range(KD):
                                nc.tensor.matmul(ps_c[:, b, k * P:(k + 1) * P], hs[:, k, b, :], ident[:, :],
                                                 start=k == 0, stop=False, skip_group_check=True)
                        else:
                            c = part - 1
                            pe.wait_ge(S["yz"], j * CI + (c + 1))
                            last = nc.tensor.matmul(ps_c[:, b, 0:D], y[:, c, b * LB:(b + 1) * LB], w_out[:, c, :],
                                                    start=False, stop=c == CI - 1, skip_group_check=True)
                            if c == CI - 1:
                                last.then_inc(S["out"], 1)

                none = lambda: None
                pe.wait_ge(ready, 1)
                with pe.Fori(0, LB - 1, 2) as t0:
                    for u in range(2):
                        lstm_products(t0 + u, u, none)
                with pe.Fori(1, NB) as k:
                    for s in range(PE_U):
                        lstm_products(k * LB + s, s % 2, lambda: part1(s, k - 1))
                    with pe.Fori(0, DS - 1, 2) as n0:
                        for i in range(2 * CI):
                            lstm_products(k * LB + n0 * CI + (PE_U + i), (PE_U + i) % 2, lambda: unit(k - 1, n0, i))
                    for s in range(PE_U + U, LB):
                        lstm_products(k * LB + s, s % 2, lambda: part3(s, k - 1))
                for s in range(PE_U):
                    part1(s, NB - 1)
                with pe.Fori(0, DS - 1, 2) as n0:
                    for i in range(2 * CI):
                        unit(NB - 1, n0, i)
                for s in range(PE_U + U, LB):
                    part3(s, NB - 1)

            @block.scalar
            def _(act):
                unscale = act.alloc_register("unscale")
                act.reg_load(unscale, gate_scale[0:1, 0:1].bitcast(I32))
                act.preload_act_table_set("exp_and_others")
                act.sem_inc(S["xp"], 2)
                act.sem_inc(S["cb"], 1)

                def lstm_gates(t, u):
                    nc.scalar.activation(xo[:, :], xw[:, bass.ds(t, 1), IFG:IFG + O].rearrange("p t c -> p (t c)"),
                                         ACT.Copy).then_inc(xo_in, 1)
                    act.wait_ge(ifg_pre, t + 2)
                    nc.scalar.activation(gates[:, u, 0:IFG], pre[:, :], ACT.Tanh, scale=unscale).then_inc(ifg_gate, 1)
                    act.wait_ge(o_pre, t + 1)
                    nc.scalar.activation(og[:, :], pre_x[:, :], ACT.Tanh, scale=unscale).then_inc(o_gate, 1)
                    act.wait_ge(cell, t + 1)
                    nc.scalar.activation(tc[:, :], gates[:, 1 - u, IFG:IFG + HC], ACT.Tanh, scale=0.5).then_inc(tanh_c, 1)

                def part1(s, j):
                    if s in (11, 13, 15, 17):
                        c = (s - 11) // 2
                        act.wait_ge(S["xproj"], j * CI + (c + 1))
                        act.wait_ge(S["halo"], j + 1)
                        nc.scalar.activation(xp[:, c, :, DCONV - 1:],
                                             ps_c[:, (c + 1) % 2, 0:L].rearrange("p (b t) -> p b t", b=B),
                                             ACT.Copy).then_inc(S["xp"], 1)
                    elif s in (18, 22):
                        q = (s - 18) // 4
                        act.wait_ge(S["tap"], j * 16 + (q + 1) * 8)
                        nc.scalar.activation(th[:, 2 * q:2 * q + 2, :], acc[:, 2 * q:2 * q + 2, :, :]
                                             .rearrange("p c b t -> p c (b t)"), ACT.Tanh).then_inc(S["th"], 1)
                    elif s == 27:
                        act.wait_ge(S["prm"], j + 1)
                        nc.scalar.activation(par[:, :], ps_c[0:2 * DS + 1, 0, 0:L], ACT.Copy).then_inc(S["par"], 1)
                    elif s in (30, 31):
                        q = s - 30
                        act.wait_ge(S["v"], j * CI + (q + 1) * 2)
                        nc.scalar.activation(th[:, 2 * q:2 * q + 2, :], v[:, 2 * q:2 * q + 2, :], ACT.Abs).then_inc(S["abs"], 1)
                    elif s == 32:
                        act.wait_ge(S["abs"], j * 2 + 2)
                        nc.scalar.activation(th[:, :, :], th[:, :, :], ACT.Exp, scale=-1.0).then_inc(S["exp"], 1)
                    elif s == 33:
                        act.wait_ge(S["exp"], j + 1)
                        nc.scalar.activation(th[:, :, :], th[:, :, :], ACT.Ln, bias=1.0).then_inc(S["ln"], 1)
                        act.preload_act_table_set("exp_and_others")

                def unit(j, n0, i):
                    g, c = j * U + n0 * CI + i, i % CI
                    if c == 0:
                        act.wait_ge(S["c_row"], j * (DS + 1) + n0 + (i // CI + 1))
                        act.wait_ge(S["hc"], j * U + n0 * CI + (i + 4))
                        nc.scalar.activation(cb[:, i // CI, :], ps_c[:, i // CI, 0:L], ACT.Copy).then_inc(S["cb"], 1)
                    act.wait_ge(S["dt"], j * 2 + (c // 2 + 1))
                    act.wait_ge(S["scan"], g * 2 + 2)
                    nc.scalar.activation(ab[:, c, :], dt[:, c, :], ACT.Exp,
                                         scale=a_neg[:, c, bass.ds(n0 + i // CI, 1)]).then_inc(S["ab"], 1)

                def part3(s, j):
                    if s in (102, 104, 106, 108):
                        c = (s - 102) // 2
                        act.wait_ge(S["z"], j * CI + (c + 1))
                        nc.scalar.activation(th[:, c, :], ps_z[:, c % 2, 0:L], ACT.Tanh, scale=0.5).then_inc(S["thz"], 1)

                with act.Fori(0, LB - 1, 2) as t0:
                    for u in range(2):
                        lstm_gates(t0 + u, u)
                with act.Fori(1, NB) as k:
                    for s in range(ACT_U):
                        lstm_gates(k * LB + s, s % 2)
                        part1(s, k - 1)
                    with act.Fori(0, DS - 1, 2) as n0:
                        for i in range(2 * CI):
                            lstm_gates(k * LB + n0 * CI + (ACT_U + i), (ACT_U + i) % 2)
                            unit(k - 1, n0, i)
                    for s in range(ACT_U + U, LB):
                        lstm_gates(k * LB + s, s % 2)
                        part3(s, k - 1)
                for s in range(ACT_U):
                    part1(s, NB - 1)
                with act.Fori(0, DS - 1, 2) as n0:
                    for i in range(2 * CI):
                        unit(NB - 1, n0, i)
                for s in range(ACT_U + U, LB):
                    part3(s, NB - 1)

            @block.vector
            def _(dve):
                none = lambda: None

                def lstm_state(t, u, mid, end):
                    dve.wait_ge(ifg_sum, t + 1)
                    dve.wait_ge(xo_in, t + 1)
                    nc.vector.tensor_reduce(pre[:, :], ps_g[:, 0:2 * IFG].rearrange("p (h c) -> p c h", h=2),
                                            AX.X, ALU.add).then_inc(ifg_pre, 1)
                    dve.wait_ge(o_sum, t + 1)
                    nc.vector.tensor_reduce(pre_o[:, :], ps_o[:, 0:2 * O].rearrange("p (h c) -> p c h", h=2),
                                            AX.X, ALU.add).then_inc(o_pre0, 1)
                    dve.wait_ge(o_pre0, t + 1)
                    nc.vector.tensor_tensor(pre_x[:, :], pre_o[:, :], xo[:, :], ALU.add).then_inc(o_pre, 1)
                    dve.wait_ge(ifg_gate, t + 1)
                    nc.vector.scalar_tensor_tensor(prod[:, :], gates[:, u, 0:2 * HC], 1.0, gates[:, u, IFG - HC:IFG + HC],
                                                   ALU.add, ALU.mult).then_inc(p_ready, 1)
                    dve.wait_ge(p_ready, t + 1)
                    nc.vector.scalar_tensor_tensor(gates[:, 1 - u, IFG:IFG + HC], prod[:, HC:2 * HC], 0.5, prod[:, 0:HC],
                                                   ALU.mult, ALU.add).then_inc(cell, 1)
                    mid()
                    dve.wait_ge(o_gate, t + 1)
                    nc.vector.tensor_scalar(og1[:, :], og[:, :], HALF, HALF, ALU.mult, ALU.add).then_inc(o_scaled, 1)
                    for sem in (tanh_c, o_scaled) if mid is none else (o_scaled, tanh_c):
                        dve.wait_ge(sem, t + 1)
                    h = hf[:, :].rearrange("p (k b) -> p k b", k=KD)
                    o_kb = og1[:, :].rearrange("p (k b) -> p k b", k=KD)
                    tc_kb = tc[:, :].rearrange("p (k b) -> p k b", k=KD)
                    nc.vector.tensor_tensor(h, o_kb, tc_kb, ALU.mult).then_inc(h_parts, 1)
                    nc.vector.tensor_tensor(h16[:, 1 - u, :, 0, :], o_kb, tc_kb, ALU.mult).then_inc(h_parts, 1)
                    dve.wait_ge(h_parts, 2 * t + 2)
                    nc.vector.tensor_tensor(h16[:, 1 - u, :, 1, :], h, h16[:, 1 - u, :, 0, :],
                                            ALU.subtract).then_inc(h_ready, 1)
                    nc.vector.tensor_scalar(hist[:, bass.ds(t, 1), :, :].rearrange("p t k b -> p (t k b)"), hf[:, :],
                                            2.0 ** -HEXP, None, ALU.mult).then_inc(h_kept, 1)
                    end()

                def part1(s, j):
                    if s == 0:
                        dve.wait_ge(S["out"], j * B + 1)
                        dve.wait_ge(h_kept, j * LB + LB)
                        nc.vector.tensor_scalar(hs[:, :, :, :], hist[:, bass.ds(j * LB, LB), :, :].rearrange("p t k b -> p k b t"),
                                                1.0, None, ALU.mult).then_inc(S["hs"], 1)
                    elif s == 4:
                        dve.wait_ge(S["ms"], j * 3 + 2)
                        nc.vector.tensor_scalar(msv[:, :], ps_c[:, 0, 0:B], 1.0 / D, 1e-6, ALU.mult, ALU.add).then_inc(S["msv"], 1)
                    elif s == 5:
                        dve.wait_ge(S["rstd"], j + 1)
                        nc.vector.tensor_scalar(rstd_b[:, :, :], row(rstd[:, :], P), 1.0, None, ALU.mult).then_inc(S["rb"], 1)
                    elif s in (7, 8):
                        k = s - 7
                        dve.wait_ge(S["ms"], j * 3 + 3)
                        nc.vector.scalar_tensor_tensor(xn[:, k, :], hs[:, k, :, :].rearrange("p b t -> p (b t)"),
                                                       norm_w[:, k:k + 1], ps_c[:, 0, 0:L], ALU.mult, ALU.mult).then_inc(S["xn"], 1)
                    elif 14 <= s < 22:
                        q, tap = (s - 14) // 4, (s - 14) % 4
                        for c in (2 * q, 2 * q + 1):
                            src = xp[:, c, :, tap:tap + LB]
                            if tap == 0:
                                dve.wait_ge(S["xp"], j * CI + (c + 3))
                                nc.vector.tensor_scalar(acc[:, c, :, :], src, conv_w[:, c, 0:1], conv_b[:, c:c + 1],
                                                        ALU.mult, ALU.add).then_inc(S["tap"], 1)
                            else:
                                dve.wait_ge(S["tap"], j * 16 + (q * 8 + tap * 2 + c % 2 - 1))
                                nc.vector.scalar_tensor_tensor(acc[:, c, :, :], src, conv_w[:, c, tap:tap + 1], acc[:, c, :, :],
                                                               ALU.mult, ALU.add).then_inc(S["tap"], 1)
                    elif s in (22, 23):
                        q = s - 22
                        if q == 0:
                            nc.vector.tensor_scalar(xp[:, :, :, 0:DCONV - 1].rearrange("p c b t -> p (c b) t"),
                                                    xp[:, :, :, LB:].rearrange("p c b t -> p (c b) t"),
                                                    1.0, None, ALU.mult).then_inc(S["halo"], 1)
                        dve.wait_ge(S["th"], j * 2 + (q + 1))
                        nc.vector.scalar_tensor_tensor(xc[:, 2 * q:2 * q + 2, :], th[:, 2 * q:2 * q + 2, :], 1.0,
                                                       acc[:, 2 * q:2 * q + 2, :, :].rearrange("p c b t -> p c (b t)"),
                                                       ALU.add, ALU.mult).then_inc(S["xc"], 1)
                    elif s in (29, 30):
                        dve.wait_ge(S["dtb"], j + 1)
                        for c in range((s - 29) * 2, (s - 29) * 2 + 2):
                            nc.vector.tensor_scalar(v[:, c, :], ps_c[:, 1, 0:L], w_dt[:, c:c + 1], b_dt[:, c:c + 1],
                                                    ALU.mult, ALU.add).then_inc(S["v"], 1)
                    elif s in (34, 35):
                        q = s - 34
                        dve.wait_ge(S["ln"], j + 1)
                        nc.vector.scalar_tensor_tensor(dt[:, 2 * q:2 * q + 2, :], v[:, 2 * q:2 * q + 2, :], 0.0,
                                                       th[:, 2 * q:2 * q + 2, :], ALU.max, ALU.add).then_inc(S["dt"], 1)

                def unit_mid(j, n0, i):
                    g, c, m = j * U + n0 * CI + i, i % CI, i // CI
                    if c == 0:
                        dve.wait_ge(S["b_row"], j * (DS + 1) + n0 + (m + 1))
                    dve.wait_ge(S["u"], j * CI + (c + 1))
                    nc.vector.tensor_tensor(bx[:, c, :], uu[:, c, :], ps_b[:, m, 0:L], ALU.mult).then_inc(S["bx"], 1)

                def unit_end(j, n0, i):
                    g, c, m = j * U + n0 * CI + i, i % CI, i // CI
                    dve.wait_ge(S["bx"], g + 5)
                    dve.wait_ge(S["ab"], g + 5)
                    dve.wait_ge(S["kept"], g + 5)
                    for b in range(B):
                        cols = slice(b * LB, (b + 1) * LB)
                        nc.vector.tensor_tensor_scan(hh[:, c, cols], ab[:, c, cols], bx[:, c, cols],
                                                     state[:, c, b, bass.ds(n0 + m, 1)],
                                                     ALU.mult, ALU.add).then_inc(S["scan"], 1)

                def part3(s, j):
                    if s in (103, 105, 107, 109):
                        c = (s - 103) // 2
                        dve.wait_ge(S["thz"], j * CI + (c + 1))
                        nc.vector.scalar_tensor_tensor(th[:, c, :], th[:, c, :], 1.0, ps_z[:, c % 2, 0:L],
                                                       ALU.add, ALU.mult).then_inc(S["z2"], 1)
                    if s in (104, 106, 108, 110):
                        c = (s - 104) // 2
                        dve.wait_ge(S["y"], (j + 1) * U + 8)
                        dve.wait_ge(S["z2"], j * CI + (c + 3))
                        nc.vector.scalar_tensor_tensor(y[:, c, :], y[:, c, :], 0.5,
                                                       th[:, c, :], ALU.mult, ALU.mult).then_inc(S["yz"], 1)
                    if s in (113, 118):
                        b = (s - 113) // 5
                        dve.wait_ge(S["out"], j * B + (b + 2))
                        tile = x1[:, bass.ds(j + b * (T // P), 1), :].rearrange("p i d -> p (i d)")
                        nc.vector.tensor_tensor(tile, tile, ps_c[:, b, 0:D], ALU.add).then_inc(S["x1"], 1)

                nc.vector.memset(gates[:, 0, IFG:IFG + HC], 0.0).then_inc(S["init"], 1)
                nc.vector.memset(state[:, :, :, :], 0.0).then_inc(S["init"], 1)
                nc.vector.memset(xp[:, :, :, 0:DCONV - 1], 0.0).then_inc(S["init"], 1)
                nc.vector.memset(rows[0:1, DS, :, :], 0.0).then_inc(S["init"], 1)
                dve.wait_ge(S["init"], 4)
                for name, credit in (("halo", 1), ("out", 1), ("z2", 2), ("bx", 4), ("scan", 8),
                                     ("hc", 8), ("y", 8), ("ab", 4), ("kept", 8)):
                    dve.sem_inc(S[name], credit)
                dve.sem_inc(ifg_pre, 1)
                dve.sem_inc(ready, 1)
                nc.vector.memset(h16[:, 0, :, :, :], 0.0).then_inc(h_ready, 1)
                with dve.Fori(0, LB - 1, 2) as t0:
                    for u in range(2):
                        lstm_state(t0 + u, u, none, none)
                with dve.Fori(1, NB) as k:
                    for s in range(DVE_U):
                        lstm_state(k * LB + s, s % 2, none, lambda: part1(s, k - 1))
                    with dve.Fori(0, DS - 1, 2) as n0:
                        for i in range(2 * CI):
                            lstm_state(k * LB + n0 * CI + (DVE_U + i), (DVE_U + i) % 2,
                                       lambda: unit_mid(k - 1, n0, i), lambda: unit_end(k - 1, n0, i))
                    for s in range(DVE_U + U, LB):
                        lstm_state(k * LB + s, s % 2, none, lambda: part3(s, k - 1))
                for s in range(DVE_U):
                    part1(s, NB - 1)
                with dve.Fori(0, DS - 1, 2) as n0:
                    for i in range(2 * CI):
                        unit_mid(NB - 1, n0, i)
                        unit_end(NB - 1, n0, i)
                for s in range(DVE_U + U, LB):
                    part3(s, NB - 1)


def load_weights(nc, sems, A, x1, W):
    w_in, conv_w, conv_b, w_dt, b_dt, w_x, norm_w, ones, a_neg, d_par, w_out = W
    with ExitStack() as stack:
        s = Scope(nc, stack, sems)
        loaded, made, half = s.sem("w_loaded"), s.sem("w_made"), s.sem("w_half")
        with nc.Block() as block:

            @block.sync
            def _(sp):
                sems.clear_last(sp)
                for dst, src in ((w_in[:, :, :], A["w_in"].rearrange("(k p) n -> p k n", p=P)),
                                 (conv_w[:, :, :], A["conv_w"]), (conv_b[:, :], A["conv_b"]),
                                 (w_dt[:, :], A["w_dt"]), (b_dt[:, :], A["b_dt"]),
                                 (w_x[:, :, :], A["w_x"].rearrange("(c p) n -> p c n", p=P)),
                                 (norm_w[:, :], A["norm_w"]), (a_neg[:, :, :], A["a_log"]), (d_par[:, :], A["d_par"]),
                                 (w_out[:, :, :], A["w_out"].rearrange("(c p) n -> p c n", p=P)),
                                 (x1[:, :, :], A["x"].rearrange("(i p) d -> p i d", p=P))):
                    sp.dma_start(dst, src).then_inc(loaded, 16)
                sp.wait_ge(loaded, 16 * 11)

            @block.scalar
            def _(act):
                act.wait_ge(loaded, 16 * 11)
                nc.scalar.activation(a_neg[:, :, :], a_neg[:, :, :], ACT.Exp).then_inc(made, 1)
                act.wait_ge(made, 1)
                nc.scalar.activation(a_neg[:, :, :], a_neg[:, :, :], ACT.Copy, scale=-1.0).then_inc(made, 1)
                act.wait_ge(made, 2)

            @block.vector
            def _(dve):
                dve.wait_ge(loaded, 16 * 11)
                nc.vector.memset(ones[:, :], 1.0).then_inc(half, 1)
                nc.vector.tensor_scalar(conv_w[:, :, :], conv_w[:, :, :], 0.5, None, ALU.mult).then_inc(half, 1)
                nc.vector.tensor_scalar(conv_b[:, :], conv_b[:, :], 0.5, None, ALU.mult).then_inc(half, 1)
                dve.wait_ge(half, 3)


EPS = 1e-7
MAXT = float(np.float32(1.0 - 1e-5))
ATANH = math.atanh(MAXT)
LN_A = math.log(ATANH)
TINY = 1e-18
H, HD, FF = 16, 16, 1024


def _beta(a, b):
    return math.exp(math.lgamma(a) + math.lgamma(b) - math.lgamma(a + b))


R_HEADS = _beta(HD / 2, 0.5) / _beta(D / 2, 0.5)
QSC = 256.0
TPB = NT // B


def ada_rows(nc, sems, A, ada):
    W6 = 6 * D
    with ExitStack() as stack:
        s = Scope(nc, stack, sems)
        w = s.sb("w_ada", [P, KD, W6])
        cond = s.sb("cond", [P, KD, B])
        cond_b = s.sb("cond_b", [P, KD, B, P])
        bias = s.sb("bias_ada", [1, W6])
        one = s.sb("one_ada", [1, P])
        ps = s.ps("ps_ada", [P, B * W6 // BANK, BANK])
        loaded, made, full, out = s.sem("d_loaded"), s.sem("d_made"), s.sem("d_full"), s.sem("d_out")
        with nc.Block() as block:

            @block.sync
            def _(sp):
                sems.clear_last(sp)
                sp.dma_start(cond[:, :, :], A["condT"].rearrange("(k p) b -> p k b", p=P)).then_inc(loaded, 16)
                sp.dma_start(bias[:, :], A["b_ada"]).then_inc(loaded, 16)
                sp.dma_start(w[:, :, :], A["w_ada"].rearrange("(k p) n -> p k n", p=P)).then_inc(loaded, 16)

            @block.tensor
            def _(pe):
                pe.wait_ge(loaded, 48)
                pe.wait_ge(made, 2)
                for b in range(B):
                    for c in range(W6 // BANK):
                        cols = slice(c * BANK, (c + 1) * BANK)
                        out_ps = ps[:, b * (W6 // BANK) + c, :]
                        for k in range(KD):
                            nc.tensor.matmul(out_ps, cond_b[:, k, b, :], w[:, k, cols], start=k == 0, stop=False)
                        nc.tensor.matmul(out_ps, one[0:1, :], bias[0:1, cols], start=False, stop=True).then_inc(full, 1)

            @block.vector
            def _(dve):
                nc.vector.memset(one[:, :], 1.0).then_inc(made, 1)
                dve.wait_ge(loaded, 48)
                nc.vector.tensor_copy(cond_b[:, :, :, :], row(cond[:, :, :], P)).then_inc(made, 1)
                for b in range(B):
                    for c in range(W6 // BANK):
                        n = b * (W6 // BANK) + c
                        dve.wait_ge(full, n + 1)
                        for lo in range(c * BANK, (c + 1) * BANK, D):
                            plus = 1.0 if lo // D in (1, 4) else 0.0
                            at = lo - c * BANK
                            nc.vector.tensor_scalar(ada[:, b, lo // D, :], ps[:, n, at:at + D], plus, None,
                                                    ALU.add).then_inc(out, 1)
                dve.wait_ge(out, B * 6)


def norm_modulate(nc, sems, tag, x, ada, shift, ident, vT):
    with ExitStack() as stack:
        s = Scope(nc, stack, sems)
        big = s.sb(tag + "big", [P, NT, D])
        v = s.sb(tag + "v", [P, NT, D])
        col = {n: s.sb(tag + n, [P, NT]) for n in "sum mean n2 var n m lp lm rn s s2v f r".split()}
        ps = s.ps(tag + "ps", [P, 8, BANK])
        link_v, link_a = s.sem(tag + "link_v"), s.sem(tag + "link_a")
        S = {n: s.sem(tag + n) for n in "sq1 n2 sq2 norm m logs s2v f v sq3 n2v r ready t used".split()}
        with nc.Block() as block:

            @block.sync
            def _(sp):
                sems.clear_last(sp)

            @block.scalar
            def _(act):
                count = [0]

                def link(ins):
                    count[0] += 1
                    ins.then_inc(link_a, 1)
                    act.wait_ge(link_a, count[0])

                nc.scalar.activation(big[:, :, :], x[:, :, :], ACT.Square).then_inc(S["sq1"], 1)
                act.wait_ge(S["n2"], 1)
                link(nc.scalar.activation(col["lp"][:, :], col["n2"][:, :], ACT.Ln))
                link(nc.scalar.activation(col["rn"][:, :], col["lp"][:, :], ACT.Exp, scale=-0.5))
                nc.scalar.activation(col["n"][:, :], col["lp"][:, :], ACT.Exp, scale=0.5).then_inc(S["norm"], 1)
                act.wait_ge(S["m"], 1)
                link(nc.scalar.activation(col["lp"][:, :], col["m"][:, :], ACT.Ln, bias=1.0))
                nc.scalar.activation(col["lm"][:, :], col["m"][:, :], ACT.Ln, bias=1.0, scale=-1.0).then_inc(S["logs"], 1)
                act.wait_ge(S["sq2"], 1)
                nc.scalar.activation(big[:, :, :], v[:, :, :], ACT.Square).then_inc(S["sq3"], 1)
                act.wait_ge(S["s2v"], 1)
                link(nc.scalar.activation(col["lp"][:, :], col["s2v"][:, :], ACT.Ln))
                nc.scalar.activation(col["f"][:, :], col["lp"][:, :], ACT.Exp, scale=-0.5).then_inc(S["f"], 1)
                act.wait_ge(S["v"], 1)
                nc.scalar.activation(big[:, :, :], v[:, :, :], ACT.Square).then_inc(S["sq3"], 1)
                act.wait_ge(S["n2v"], 1)
                link(nc.scalar.activation(col["lp"][:, :], col["n2"][:, :], ACT.Ln))
                nc.scalar.activation(col["r"][:, :], col["lp"][:, :], ACT.Exp, scale=-0.5, bias=LN_A).then_inc(S["r"], 1)
                for i in range(0, NT, 2):
                    act.wait_ge(S["t"], i // 2 + 1)
                    nc.scalar.activation(
                        vT[:, :, i * P:(i + 2) * P].rearrange("p k (i t) -> p i k t", i=2),
                        ps[:, i // 2 % 8, :].rearrange("p (i k t) -> p i k t", i=2, k=KD), ACT.Copy).then_inc(S["used"], 1)

            @block.vector
            def _(dve):
                count = [0]

                def link(ins):
                    count[0] += 1
                    ins.then_inc(link_v, 1)
                    dve.wait_ge(link_v, count[0])

                c = {n: t[:, :] for n, t in col.items()}
                link(nc.vector.tensor_reduce(c["sum"], x[:, :, :], AX.X, ALU.add))
                link(nc.vector.tensor_scalar(c["mean"], c["sum"], 1.0 / D, None, ALU.mult))
                dve.wait_ge(S["sq1"], 1)
                link(nc.vector.tensor_reduce(c["n2"], big[:, :, :], AX.X, ALU.add))
                nc.vector.tensor_scalar(c["n2"], c["n2"], EPS * EPS, None, ALU.max).then_inc(S["n2"], 1)
                nc.vector.tensor_tensor(v[:, :, :], x[:, :, :], row(c["mean"], D), ALU.subtract).then_inc(S["sq2"], 1)
                dve.wait_ge(S["norm"], 1)
                nc.vector.tensor_scalar(c["m"], c["n"], MAXT, None, ALU.min).then_inc(S["m"], 1)
                dve.wait_ge(S["sq3"], 1)
                link(nc.vector.tensor_reduce(c["var"], big[:, :, :], AX.X, ALU.add))
                dve.wait_ge(S["logs"], 1)
                link(nc.vector.tensor_tensor(c["s"], c["lp"], c["lm"], ALU.subtract))
                link(nc.vector.scalar_tensor_tensor(c["s"], c["s"], 0.5, c["rn"], ALU.mult, ALU.mult))
                link(nc.vector.scalar_tensor_tensor(c["s2v"], c["s"], 1.0 / D, c["s"], ALU.mult, ALU.mult))
                link(nc.vector.tensor_tensor(c["s2v"], c["s2v"], c["var"], ALU.mult))
                nc.vector.tensor_scalar(c["s2v"], c["s2v"], 1e-6, None, ALU.add).then_inc(S["s2v"], 1)
                dve.wait_ge(S["f"], 1)
                link(nc.vector.tensor_tensor(c["f"], c["f"], c["s"], ALU.mult))
                link(nc.vector.tensor_tensor(v[:, :, :], v[:, :, :], row(c["f"], D), ALU.mult))
                for part, op in ((shift + 1, ALU.mult), (shift, ALU.add)):
                    for b in range(B):
                        tiles = v[:, b * TPB:(b + 1) * TPB, :]
                        rows = ada[:, b, part, :].unsqueeze(1).broadcast_to([P, TPB, D])
                        link(nc.vector.tensor_tensor(tiles, tiles, rows, op))
                dve.sem_inc(S["v"], 1)
                dve.wait_ge(S["sq3"], 2)
                link(nc.vector.tensor_reduce(c["n2"], big[:, :, :], AX.X, ALU.add))
                nc.vector.tensor_scalar(c["n2"], c["n2"], EPS * EPS, None, ALU.max).then_inc(S["n2v"], 1)
                dve.wait_ge(S["r"], 1)
                link(nc.vector.tensor_scalar(c["r"], c["r"], 1.0, None, ALU.min))
                nc.vector.tensor_tensor(v[:, :, :], v[:, :, :], row(c["r"], D), ALU.mult).then_inc(S["ready"], 1)

            @block.tensor
            def _(pe):
                pe.wait_ge(S["ready"], 1)
                for i in range(NT):
                    for k in range(KD):
                        at = (i % 2 * KD + k) * P
                        last = nc.tensor.transpose(ps[:, i // 2 % 8, at:at + P], v[:, i, k * P:(k + 1) * P], ident[:, :])
                    if i % 2:
                        last.then_inc(S["t"], 1)


def qkv(nc, sems, A, ident16, vT, qT, kT, va, sq, nh):
    W3 = 3 * D
    with ExitStack() as stack:
        s = Scope(nc, stack, sems)
        w = s.sb("w_qkv", [P, KD, W3])
        bias = s.sb("b_qkv", [1, W3])
        one = s.sb("one_q", [1, P])
        x = s.sb("x_qkv", [P, NT, W3])
        nf = s.sb("nf", [P, NT * 3])
        pair = s.sb("pair", [P, 2, 2, H, 4, HD], F16)
        ps = s.ps("ps_qkv", [P, 3, 2, BANK])
        ps_t = s.ps("ps_t", [P, 2, 2 * BANK], F16)
        loaded = s.sem("q_loaded")
        S = {n: s.sem("q_" + n) for n in "one full x sq nh nh_used lh lf alpha_f alpha scaled hi lo t used".split()}
        link_v = s.sem("q_link")
        with nc.Block() as block:

            @block.sync
            def _(sp):
                sems.clear_last(sp)
                sp.dma_start(w[:, :, :], A["w_qkv"].rearrange("(k p) n -> p k n", p=P)).then_inc(loaded, 16)
                sp.dma_start(bias[:, :], A["b_qkv"]).then_inc(loaded, 16)
                sp.dma_start(ident16[:, :], A["ident16"]).then_inc(loaded, 16)

            @block.tensor
            def _(pe):
                pe.wait_ge(loaded, 48)
                pe.wait_ge(S["one"], 1)
                for i in range(NT):
                    if i >= 3:
                        pe.wait_ge(S["x"], 2 * (i - 2))
                    for part, (lo, hi) in enumerate(((0, BANK), (BANK, W3))):
                        out = ps[:, i % 3, part, 0:hi - lo]
                        for k in range(KD):
                            nc.tensor.matmul(out, vT[:, k, i * P:(i + 1) * P], w[:, k, lo:hi], start=k == 0, stop=False)
                        nc.tensor.matmul(out, one[0:1, :], bias[0:1, lo:hi], start=False, stop=True).then_inc(S["full"], 1)
                with pe.Fori(0, NT - 1, 2) as i0:
                    for u in range(2):
                        i = i0 + u
                        pe.wait_ge(S["lo"], i * 4 + 4)
                        for qk in range(2):
                            pe.wait_ge(S["used"], i * 2 + (qk + 2))
                            for h in range(0, H, 2):
                                last = nc.tensor.transpose(ps_t[:, qk, h // 2 * P:(h // 2 + 1) * P],
                                                           pair[:, u, qk, h:h + 2, :, :].rearrange("p h r d -> p (h r d)"),
                                                           ident16[:, :])
                            last.then_inc(S["t"], 1)

            @block.scalar
            def _(act):
                act.preload_act_table(ACT.Exp)
                for i in range(NT):
                    for part, (lo, hi) in enumerate(((0, BANK), (BANK, W3))):
                        act.wait_ge(S["full"], 2 * i + part + 1)
                        nc.scalar.activation(x[:, i, lo:hi], ps[:, i % 3, part, 0:hi - lo], ACT.Copy).then_inc(S["x"], 1)
                for j in range(4):
                    if j:
                        act.wait_ge(S["nh"], j)
                    act.wait_ge(S["x"], 2 * NT)
                    nc.scalar.activation(sq, x[:, j * 4:(j + 1) * 4, :], ACT.Square).then_inc(S["sq"], 1)
                act.wait_ge(S["nh_used"], 1)
                nc.scalar.activation(nh[:, :, :], nh[:, :, :], ACT.Ln).then_inc(S["lh"], 1)
                nc.scalar.activation(nf[:, :], nf[:, :], ACT.Ln).then_inc(S["lf"], 1)
                act.wait_ge(S["lh"], 1)
                act.wait_ge(S["lf"], 1)
                nc.scalar.activation(nh[:, :, :], nh[:, :, :], ACT.Exp, scale=-0.5, bias=LN_A).then_inc(S["alpha"], 1)
                nc.scalar.activation(nf[:, :], nf[:, :], ACT.Exp, scale=-0.5,
                                     bias=math.log(ATANH * R_HEADS)).then_inc(S["alpha_f"], 1)
                with act.Fori(0, NT - 1, 2) as i0:
                    for u in range(2):
                        i = i0 + u
                        for qk, dst in enumerate((qT, kT)):
                            act.wait_ge(S["t"], i * 2 + (qk + 1))
                            nc.scalar.activation(dst[:, :, bass.ds(i * P, P)],
                                                 ps_t[:, qk, :].rearrange("p (h t) -> p h t", t=P),
                                                 ACT.Copy).then_inc(S["used"], 1)

            @block.vector
            def _(dve):
                count = [0]

                def link(ins):
                    count[0] += 1
                    ins.then_inc(link_v, 1)
                    dve.wait_ge(link_v, count[0])

                dve.sem_inc(S["used"], 3)
                nc.vector.memset(one[:, :], 1.0).then_inc(S["one"], 1)
                for j in range(4):
                    dve.wait_ge(S["sq"], j + 1)
                    nc.vector.tensor_reduce(nh[:, j * 12:(j + 1) * 12, :],
                                            sq.rearrange("p i (a h d) -> p (i a) h d", a=3, d=HD),
                                            AX.X, ALU.add).then_inc(S["nh"], 1)
                dve.wait_ge(S["nh"], 4)
                link(nc.vector.tensor_reduce(nf[:, :], nh[:, :, :], AX.X, ALU.add))
                link(nc.vector.tensor_scalar(nf[:, :], nf[:, :], EPS * EPS, None, ALU.max))
                nc.vector.tensor_scalar(nh[:, :, :], nh[:, :, :], TINY, None, ALU.max).then_inc(S["nh_used"], 1)
                dve.wait_ge(S["alpha_f"], 1)
                dve.wait_ge(S["alpha"], 1)
                link(nc.vector.tensor_scalar(nf[:, :], nf[:, :], R_HEADS, None, ALU.min))
                link(nc.vector.tensor_tensor(nh[:, :, :], nh[:, :, :], row(nf[:, :], H), ALU.min))
                alpha = nh[:, :, :].rearrange("p (i a) h -> p i a h", a=3)
                with dve.Fori(0, NT - 1, 2) as i0:
                    for u in range(2):
                        i = i0 + u
                        xi = x[:, bass.ds(i, 1), :].rearrange("p i (a h d) -> p (i a) h d", a=3, d=HD)
                        ai = alpha[:, bass.ds(i, 1), :, :].rearrange("p i a h -> p (i a) h")
                        dve.wait_ge(S["used"], i * 2 + 1)
                        for qk in range(2):
                            nc.vector.scalar_tensor_tensor(xi[:, qk, :, :], xi[:, qk, :, :], QSC, row(ai[:, qk, :], HD),
                                                           ALU.mult, ALU.mult).then_inc(S["scaled"], 1)
                        nc.vector.tensor_tensor(va[:, bass.ds(i, 1), :, :].rearrange("p i h d -> p (i h) d"),
                                                xi[:, 2, :, :], row(ai[:, 2, :], HD), ALU.mult).then_inc(S["scaled"], 1)
                        dve.wait_ge(S["scaled"], (i + 1) * 3)
                        for qk in range(2):
                            for rep in range(2):
                                part = (2 * rep, rep)[qk]
                                nc.vector.tensor_scalar(pair[:, u, qk, :, part, :],
                                                        xi[:, qk, :, :],
                                                        1.0, None, ALU.mult).then_inc(S["hi"], 1)
                        dve.wait_ge(S["hi"], (i + 1) * 4)
                        for qk in range(2):
                            for rep in range(2):
                                part = (2 * rep + 1, rep + 2)[qk]
                                nc.vector.tensor_tensor(pair[:, u, qk, :, part, :],
                                                        xi[:, qk, :, :],
                                                        pair[:, u, qk, :, 0, :], ALU.subtract).then_inc(S["lo"], 1)


def attention(nc, sems, qT, kT, va, oT):
    HG = 4
    NKC = T // P
    IT = B * H // HG
    with ExitStack() as stack:
        s = Scope(nc, stack, sems)
        qs = s.sb("qs", [P, 2, HG // 2, T], F16)
        ks = s.sb("ks", [P, 2, HG // 2, T], F16)
        vs = s.sb("vs", [P, 2, NKC, HG, 32])
        pt = s.sb("pt", [P, 2, T])
        ps_s = s.ps("ps_s", [P, 2, T])
        ps_o = s.ps("ps_o2", [P, 2, T])
        S = {n: s.sem("t_" + n) for n in "pad staged stage_free s e pv out used".split()}
        NS = HG * NKC
        with nc.Block() as block:

            @block.sync
            def _(sp):
                sems.clear_last(sp)

            @block.tensor
            def _(pe):
                with pe.Fori(0, IT - 1, 2) as i0:
                    for u in range(2):
                        i = i0 + u

                        def scores(n):
                            h, kc = n // NKC, n % NKC
                            rows = slice(h % 2 * 64, h % 2 * 64 + 64)
                            pe.wait_ge(S["e"], i * NS + (n + 1))
                            for half in range(2):
                                last = nc.tensor.matmul(ps_s[:, n % 2, half * BANK:(half + 1) * BANK],
                                                        ks[rows, u, h // 2, kc * P:(kc + 1) * P],
                                                        qs[rows, u, h // 2, half * BANK:(half + 1) * BANK],
                                                        start=True, stop=True)
                            last.then_inc(S["s"], 1)

                        pe.wait_ge(S["staged"], i * 3 + 3)
                        pe.wait_ge(S["used"], i + 1)
                        scores(0)
                        scores(1)
                        for n in range(NS):
                            h, kc = n // NKC, n % NKC
                            pe.wait_ge(S["e"], i * NS + (n + 3))
                            for half in range(2):
                                last = nc.tensor.matmul(ps_o[h * 32:(h + 1) * 32, u, half * BANK:(half + 1) * BANK],
                                                        vs[:, u, kc, h, :], pt[:, n % 2, half * BANK:(half + 1) * BANK],
                                                        start=kc == 0, stop=kc == NKC - 1)
                            last.then_inc(S["pv"], 1)
                            if n + 2 < NS:
                                scores(n + 2)

            @block.scalar
            def _(act):
                act.preload_act_table(ACT.Exp)
                act.sem_inc(S["e"], 2)
                with act.Fori(0, IT - 1, 2) as i0:
                    for u in range(2):
                        i = i0 + u
                        for n in range(NS):
                            act.wait_ge(S["s"], i * NS + (n + 1))
                            act.wait_ge(S["pv"], i * NS + (n + 1))
                            nc.scalar.activation(pt[:, n % 2, :], ps_s[:, n % 2, :], ACT.Exp,
                                                 scale=0.25 / (QSC * QSC)).then_inc(S["e"], 1)

            @block.vector
            def _(dve):
                dve.sem_inc(S["pv"], 2)
                dve.sem_inc(S["used"], 2)
                nc.vector.memset(vs[:, :, :, :, HD:HD + 1], 1.0).then_inc(S["pad"], 1)
                nc.vector.memset(vs[:, :, :, :, HD + 1:], 0.0).then_inc(S["pad"], 1)
                dve.wait_ge(S["pad"], 2)

                def take_out(i):
                    b, g = i // (H // HG), i % (H // HG)
                    dve.wait_ge(S["pv"], (i + 1) * NS + 2)
                    nc.vector.tensor_copy(oT[:, g, b * T:(b + 1) * T], ps_o[:, i % 2, :]).then_inc(S["used"], 1)

                for i in range(IT):
                    b, g, u = i // (H // HG), i % (H // HG), i % 2
                    if i >= 2:
                        dve.wait_ge(S["pv"], (i - 1) * NS + 2)
                    nc.vector.tensor_copy(qs[:, u, :, :], qT[:, 2 * g:2 * g + 2, b * T:(b + 1) * T]).then_inc(S["staged"], 1)
                    nc.vector.tensor_copy(ks[:, u, :, :], kT[:, 2 * g:2 * g + 2, b * T:(b + 1) * T]).then_inc(S["staged"], 1)
                    nc.vector.tensor_copy(vs[:, u, :, :, 0:HD], va[:, b * NKC:(b + 1) * NKC, HG * g:HG * (g + 1), :])\
                      .then_inc(S["staged"], 1)
                    if i:
                        take_out(i - 1)
                take_out(IT - 1)


def heads_out(nc, sems, ident, oT, aT, v):
    with ExitStack() as stack:
        s = Scope(nc, stack, sems)
        o = s.sb("o", [P, NT, H, 32])
        sq = s.sb("sq_o", [P, NT, H * HD])
        rden = s.sb("rden", [P, NT, H])
        nh = s.sb("nh_o", [P, NT, H])
        n2 = s.sb("ho_n2", [P, NT])
        ps = s.ps("ps_ot", [P, 8, BANK])
        S = {n: s.sem("h_" + n) for n in "t o sq n2h alpha sq2 v n2 r ready tt used".split()}
        link_v, link_a = s.sem("h_link_v"), s.sem("h_link_a")
        with nc.Block() as block:

            @block.sync
            def _(sp):
                sems.clear_last(sp)

            @block.tensor
            def _(pe):
                for i in range(NT):
                    if i >= 8:
                        pe.wait_ge(S["o"], i - 7)
                    for g in range(4):
                        last = nc.tensor.transpose(ps[:, i % 8, g * P:(g + 1) * P], oT[:, g, i * P:(i + 1) * P], ident[:, :])
                    last.then_inc(S["t"], 1)
                pe.wait_ge(S["o"], NT)
                pe.wait_ge(S["ready"], 1)
                for i in range(NT):
                    for k in range(KD):
                        at = (i % 2 * KD + k) * P
                        last = nc.tensor.transpose(ps[:, i // 2 % 8, at:at + P], v[:, i, k * P:(k + 1) * P], ident[:, :])
                    if i % 2:
                        last.then_inc(S["tt"], 1)

            @block.scalar
            def _(act):
                act.preload_act_table(ACT.Copy)
                for i in range(NT):
                    act.wait_ge(S["t"], i + 1)
                    nc.scalar.activation(o[:, i, :, :].rearrange("p h d -> p (h d)"), ps[:, i % 8, :],
                                         ACT.Copy).then_inc(S["o"], 1)
                act.wait_ge(S["o"], NT)
                nc.scalar.activation(sq[:, :, :].rearrange("p i (h d) -> p (i h) d", d=HD),
                                     o[:, :, :, 0:HD].rearrange("p i h d -> p (i h) d"), ACT.Square).then_inc(S["sq"], 1)
                act.wait_ge(S["n2h"], 1)
                nc.scalar.activation(nh[:, :, :], nh[:, :, :], ACT.Ln).then_inc(link_a, 1)
                act.wait_ge(link_a, 1)
                nc.scalar.activation(nh[:, :, :], nh[:, :, :], ACT.Exp, scale=-0.5, bias=LN_A).then_inc(S["alpha"], 1)
                act.wait_ge(S["v"], 1)
                nc.scalar.activation(sq[:, :, :], v[:, :, :], ACT.Square).then_inc(S["sq2"], 1)
                act.wait_ge(S["n2"], 1)
                nc.scalar.activation(n2[:, :], n2[:, :], ACT.Ln).then_inc(link_a, 1)
                act.wait_ge(link_a, 2)
                nc.scalar.activation(n2[:, :], n2[:, :], ACT.Exp, scale=-0.5, bias=LN_A).then_inc(S["r"], 1)
                for i in range(0, NT, 2):
                    act.wait_ge(S["tt"], i // 2 + 1)
                    nc.scalar.activation(
                        aT[:, :, i * P:(i + 2) * P].rearrange("p k (i t) -> p i k t", i=2),
                        ps[:, i // 2 % 8, :].rearrange("p (i k t) -> p i k t", i=2, k=KD), ACT.Copy).then_inc(S["used"], 1)

            @block.vector
            def _(dve):
                count = [0]

                def link(ins):
                    count[0] += 1
                    ins.then_inc(link_v, 1)
                    dve.wait_ge(link_v, count[0])

                dve.wait_ge(S["o"], NT)
                link(nc.vector.reciprocal(rden[:, :, :], o[:, :, :, HD:HD + 1].rearrange("p i h d -> p i (h d)")))
                dve.wait_ge(S["sq"], 1)
                link(nc.vector.tensor_reduce(nh[:, :, :], sq[:, :, :].rearrange("p i (h d) -> p i h d", d=HD), AX.X, ALU.add))
                nc.vector.tensor_scalar(nh[:, :, :], nh[:, :, :], TINY, None, ALU.max).then_inc(S["n2h"], 1)
                dve.wait_ge(S["alpha"], 1)
                link(nc.vector.tensor_tensor(nh[:, :, :], nh[:, :, :], rden[:, :, :], ALU.min))
                link(nc.vector.tensor_scalar(nh[:, :, :], nh[:, :, :], 1.0 / R_HEADS, None, ALU.mult))
                nc.vector.tensor_tensor(v[:, :, :].rearrange("p i (h d) -> p (i h) d", d=HD),
                                        o[:, :, :, 0:HD].rearrange("p i h d -> p (i h) d"),
                                        row(nh[:, :, :].rearrange("p i h -> p (i h)"), HD), ALU.mult).then_inc(S["v"], 1)
                dve.wait_ge(S["v"], 1)
                dve.wait_ge(S["sq2"], 1)
                link(nc.vector.tensor_reduce(n2[:, :], sq[:, :, :], AX.X, ALU.add))
                nc.vector.tensor_scalar(n2[:, :], n2[:, :], EPS * EPS, None, ALU.max).then_inc(S["n2"], 1)
                dve.wait_ge(S["r"], 1)
                link(nc.vector.tensor_scalar(n2[:, :], n2[:, :], 1.0, None, ALU.min))
                nc.vector.tensor_tensor(v[:, :, :], v[:, :, :], row(n2[:, :], D), ALU.mult).then_inc(S["ready"], 1)


def project_out(nc, sems, A, aT, lin):
    with ExitStack() as stack:
        s = Scope(nc, stack, sems)
        w = s.sb("w_o", [P, KD, D])
        bias = s.sb("b_o", [1, D])
        one = s.sb("one_o", [1, P])
        ps = s.ps("ps_po", [P, 8, BANK])
        loaded, made, full, out = s.sem("p_loaded"), s.sem("p_made"), s.sem("p_full"), s.sem("p_out")
        with nc.Block() as block:

            @block.sync
            def _(sp):
                sems.clear_last(sp)
                sp.dma_start(w[:, :, :], A["w_o"].rearrange("(k p) n -> p k n", p=P)).then_inc(loaded, 16)
                sp.dma_start(bias[:, :], A["b_o"]).then_inc(loaded, 16)

            @block.tensor
            def _(pe):
                pe.wait_ge(loaded, 32)
                pe.wait_ge(made, 1)
                for i in range(NT):
                    if i >= 8:
                        pe.wait_ge(out, i - 7)
                    for k in range(KD):
                        nc.tensor.matmul(ps[:, i % 8, 0:D], aT[:, k, i * P:(i + 1) * P], w[:, k, :], start=k == 0, stop=False)
                    nc.tensor.matmul(ps[:, i % 8, 0:D], one[0:1, :], bias[0:1, :], start=False, stop=True).then_inc(full, 1)

            @block.vector
            def _(dve):
                nc.vector.memset(one[:, :], 1.0).then_inc(made, 1)
                for i in range(NT):
                    dve.wait_ge(full, i + 1)
                    nc.vector.tensor_copy(lin[:, i, :], ps[:, i % 8, 0:D]).then_inc(out, 1)
                dve.wait_ge(out, NT)


def hyper_residual(nc, sems, tag, x, lin, ada, gate, out):
    with ExitStack() as stack:
        s = Scope(nc, stack, sems)
        sq = s.sb(tag + "sq", [P, NT, D])
        w = s.sb(tag + "w", [P, NT, D])
        col = {n: s.sb(tag + n, [P, NT])[:, :] for n in "nl x2 w2 xw rho n rn th tau y2 xy num den c1 c2".split()}
        link_v, link_a = s.sem(tag + "link_v"), s.sem(tag + "link_a")
        S = {n: s.sem(tag + n) for n in "sl nl rho sx x2 w sw n2 n th".split()}
        with nc.Block() as block:

            @block.sync
            def _(sp):
                sems.clear_last(sp)

            @block.scalar
            def _(act):
                count = [0]

                def link(ins):
                    count[0] += 1
                    ins.then_inc(link_a, 1)
                    act.wait_ge(link_a, count[0])

                nc.scalar.activation(sq[:, :, :], lin[:, :, :], ACT.Square).then_inc(S["sl"], 1)
                act.wait_ge(S["nl"], 1)
                link(nc.scalar.activation(col["rho"], col["nl"], ACT.Ln))
                nc.scalar.activation(col["rho"], col["rho"], ACT.Exp, scale=-0.5, bias=LN_A).then_inc(S["rho"], 1)
                nc.scalar.activation(sq[:, :, :], x[:, :, :], ACT.Square).then_inc(S["sx"], 1)
                act.wait_ge(S["w"], 1)
                act.wait_ge(S["x2"], 1)
                nc.scalar.activation(sq[:, :, :], w[:, :, :], ACT.Square).then_inc(S["sw"], 1)
                act.wait_ge(S["n2"], 1)
                link(nc.scalar.activation(col["th"], col["n"], ACT.Ln))
                link(nc.scalar.activation(col["rn"], col["th"], ACT.Exp, scale=-0.5))
                link(nc.scalar.activation(col["n"], col["th"], ACT.Exp, scale=0.5))
                nc.scalar.activation(col["th"], col["n"], ACT.Tanh).then_inc(S["th"], 1)

            @block.vector
            def _(dve):
                count = [0]

                def link(ins):
                    count[0] += 1
                    ins.then_inc(link_v, 1)
                    dve.wait_ge(link_v, count[0])

                c, V = col, nc.vector
                dve.wait_ge(S["sl"], 1)
                link(V.tensor_reduce(c["nl"], sq[:, :, :], AX.X, ALU.add))
                V.tensor_scalar(c["nl"], c["nl"], EPS * EPS, None, ALU.max).then_inc(S["nl"], 1)
                for b in range(B):
                    tiles = slice(b * TPB, (b + 1) * TPB)
                    link(V.tensor_tensor(w[:, tiles, :], lin[:, tiles, :],
                                         ada[:, b, gate, :].unsqueeze(1).broadcast_to([P, TPB, D]), ALU.mult))
                dve.sem_inc(S["w"], 1)
                dve.wait_ge(S["sx"], 1)
                V.tensor_reduce(c["x2"], sq[:, :, :], AX.X, ALU.add).then_inc(S["x2"], 1)
                dve.wait_ge(S["sw"], 1)
                link(V.tensor_reduce(c["w2"], sq[:, :, :], AX.X, ALU.add))
                link(V.tensor_tensor(sq[:, :, :], x[:, :, :], w[:, :, :], ALU.mult))
                link(V.tensor_reduce(c["xw"], sq[:, :, :], AX.X, ALU.add))
                dve.wait_ge(S["rho"], 1)
                link(V.tensor_scalar(c["rho"], c["rho"], 1.0, None, ALU.min))
                link(V.tensor_tensor(c["n"], c["rho"], c["rho"], ALU.mult))
                link(V.tensor_tensor(c["n"], c["n"], c["w2"], ALU.mult))
                V.tensor_scalar(c["n"], c["n"], EPS * EPS, None, ALU.max).then_inc(S["n2"], 1)
                dve.wait_ge(S["th"], 1)
                link(V.tensor_tensor(c["tau"], c["th"], c["rn"], ALU.mult))
                link(V.tensor_tensor(c["tau"], c["tau"], c["rho"], ALU.mult))
                link(V.tensor_tensor(c["xy"], c["tau"], c["xw"], ALU.mult))
                link(V.tensor_tensor(c["y2"], c["tau"], c["tau"], ALU.mult))
                link(V.tensor_tensor(c["y2"], c["y2"], c["w2"], ALU.mult))
                link(V.tensor_scalar(c["xy"], c["xy"], 2.0, 1.0, ALU.mult, ALU.add))
                link(V.tensor_tensor(c["num"], c["xy"], c["y2"], ALU.add))
                link(V.tensor_tensor(c["den"], c["x2"], c["y2"], ALU.mult))
                link(V.tensor_tensor(c["den"], c["den"], c["xy"], ALU.add))
                link(V.tensor_scalar(c["den"], c["den"], EPS, None, ALU.max))
                link(V.reciprocal(c["den"], c["den"]))
                link(V.tensor_tensor(c["c1"], c["num"], c["den"], ALU.mult))
                link(V.tensor_scalar(c["c2"], c["x2"], -1.0, 1.0, ALU.mult, ALU.add))
                link(V.tensor_tensor(c["c2"], c["c2"], c["tau"], ALU.mult))
                link(V.tensor_tensor(c["c2"], c["c2"], c["den"], ALU.mult))
                link(V.tensor_tensor(w[:, :, :], w[:, :, :], row(c["c2"], D), ALU.mult))
                link(V.tensor_tensor(sq[:, :, :], x[:, :, :], row(c["c1"], D), ALU.mult))
                link(V.tensor_tensor(out[:, :, :], sq[:, :, :], w[:, :, :], ALU.add))


def feed_forward(nc, sems, A, vT, lin):
    L, FC = BANK, FF // P
    TL = L // P
    with ExitStack() as stack:
        s = Scope(nc, stack, sems)
        w1 = s.sb("w_f1", [P, KD, FF])
        w2 = s.sb("w_f2", [P, FC, D])
        b1 = s.sb("b_f1", [P, FC])
        b2 = s.sb("b_f2", [1, D])
        b2_all = s.sb("b2_all", [P, D])
        ones = s.sb("ones_f", [P, P])
        h = s.sb("h_f", [P, FC, L])
        sq = s.sb("sq_f", [P, FC, L])
        nrow = s.sb("nrow", [1, N])
        n2 = s.sb("ff_n2", [P, NT])
        ps_h = s.ps("ps_h", [P, 2, BANK])
        ps_n = s.ps("ps_n", [P, 2, BANK])
        ps_o = s.ps("ps_fo", [P, TL, BANK])
        loaded = s.sem("f_loaded")
        S = {n: s.sem("f_" + n) for n in "ones h h_in sq n nrow out out_used ncol b2 b2_in lo n2 ln r".split()}
        NB = N // L
        with nc.Block() as block:

            @block.sync
            def _(sp):
                sems.clear_last(sp)
                sp.dma_start(w1[:, :, :], A["w_f1"].rearrange("(k p) n -> p k n", p=P)).then_inc(loaded, 16)
                sp.dma_start(b1[:, :], A["b_f1"]).then_inc(loaded, 16)
                sp.dma_start(b2[:, :], A["b_f2"]).then_inc(loaded, 16)
                sp.dma_start(w2[:, :, :], A["w_f2"].rearrange("(c p) n -> p c n", p=P)).then_inc(loaded, 16)

            @block.tensor
            def _(pe):
                pe.wait_ge(loaded, 64)
                pe.wait_ge(S["ones"], 1)
                nc.tensor.matmul(ps_n[:, 1, 0:D], ones[0:1, :], b2[0:1, :], start=True, stop=True).then_inc(S["b2"], 1)
                with pe.Fori(0, NB) as q:
                    for c in range(FC):
                        pe.wait_ge(S["h_in"], q * FC + (c + 1))
                        for k in range(KD):
                            last = nc.tensor.matmul(ps_h[:, c % 2, :], w1[:, k, c * P:(c + 1) * P],
                                                    vT[:, k, bass.ds(q * L, L)], start=k == 0, stop=k == KD - 1)
                        last.then_inc(S["h"], 1)
                    pe.wait_ge(S["h_in"], q * FC + (FC + 2))
                    pe.wait_ge(S["out_used"], q * TL + TL)
                    for m in range(TL):
                        for c in range(FC):
                            last = nc.tensor.matmul(ps_o[:, m, 0:D], h[:, c, m * P:(m + 1) * P], w2[:, c, :],
                                                    start=c == 0, stop=c == FC - 1)
                        last.then_inc(S["out"], 1)
                    pe.wait_ge(S["nrow"], q + 1)
                    for c in range(FC):
                        pe.wait_ge(S["sq"], q * FC + (c + 1))
                        last = nc.tensor.matmul(ps_n[0:1, 0, :], ones[:, 0:1], sq[:, c, :], start=c == 0, stop=c == FC - 1)
                    last.then_inc(S["n"], 1)
                pe.wait_ge(S["nrow"], NB + 1)
                pe.wait_ge(S["b2_in"], 1)
                for i in range(NT):
                    last = nc.tensor.matmul(ps_n[:, 1, i:i + 1], nrow[0:1, i * P:(i + 1) * P], ones[0:1, 0:1],
                                            start=True, stop=True)
                last.then_inc(S["ncol"], 1)

            @block.scalar
            def _(act):
                act.preload_act_table(ACT.Exp)
                act.sem_inc(S["h_in"], 2)
                act.sem_inc(S["nrow"], 1)
                act.wait_ge(loaded, 64)
                with act.Fori(0, NB) as q:
                    for c in range(FC):
                        act.wait_ge(S["h"], q * FC + (c + 1))
                        if c == 0:
                            act.wait_ge(S["lo"], q * TL + TL)
                        nc.scalar.activation(h[:, c, :], ps_h[:, c % 2, :], ACT.Identity,
                                             bias=b1[:, c:c + 1]).then_inc(S["h_in"], 1)
                    act.wait_ge(S["n"], q + 1)
                    nc.scalar.activation(nrow[0:1, bass.ds(q * L, L)], ps_n[0:1, 0, :], ACT.Copy).then_inc(S["nrow"], 1)
                act.wait_ge(S["n2"], 1)
                nc.scalar.activation(n2[:, :], n2[:, :], ACT.Ln).then_inc(S["ln"], 1)
                act.wait_ge(S["ln"], 1)
                nc.scalar.activation(n2[:, :], n2[:, :], ACT.Exp, scale=-0.5, bias=LN_A).then_inc(S["r"], 1)

            @block.vector
            def _(dve):
                nc.vector.memset(ones[:, :], 1.0).then_inc(S["ones"], 1)
                dve.sem_inc(S["out_used"], TL)
                dve.sem_inc(S["lo"], TL)
                dve.wait_ge(S["b2"], 1)
                nc.vector.tensor_copy(b2_all[:, :], ps_n[:, 1, 0:D]).then_inc(S["b2_in"], 1)
                with dve.Fori(0, NB) as q:
                    for c in range(FC):
                        dve.wait_ge(S["h_in"], q * FC + (c + 3))
                        nc.vector.tensor_tensor(sq[:, c, :], h[:, c, :], h[:, c, :], ALU.mult).then_inc(S["sq"], 1)
                    dve.wait_ge(S["n"], q + 1)
                    for m in range(TL):
                        dve.wait_ge(S["out"], q * TL + (m + 1))
                        nc.vector.tensor_scalar(lin[:, bass.ds(q * TL + m, 1), :], ps_o[:, m, 0:D], 1.0, None,
                                                ALU.mult).then_inc(S["out_used"], 1)
                        dve.sem_inc(S["lo"], 1)
                dve.wait_ge(S["ncol"], 1)
                nc.vector.tensor_scalar(n2[:, :], ps_n[:, 1, 0:NT], EPS * EPS, None, ALU.max).then_inc(S["n2"], 1)
                dve.wait_ge(S["r"], 1)
                nc.vector.tensor_scalar(n2[:, :], n2[:, :], 1.0, None, ALU.min).then_inc(S["b2_in"], 1)
                dve.wait_ge(S["b2_in"], 2)
                dve.wait_ge(S["out_used"], (NB + 1) * TL)
                nc.vector.tensor_tensor(lin[:, :, :], lin[:, :, :], row(n2[:, :], D), ALU.mult).then_inc(S["b2_in"], 1)
                dve.wait_ge(S["b2_in"], 3)
                nc.vector.tensor_tensor(lin[:, :, :], lin[:, :, :], b2_all[:, :].unsqueeze(1).broadcast_to([P, NT, D]),
                                        ALU.add).then_inc(S["b2_in"], 1)
                dve.wait_ge(S["b2_in"], 4)


def glu_ffn(nc, sems, A, ident, x1, x3, out):
    L, FC = BANK, FF // P
    TL = L // P
    with ExitStack() as stack:
        s = Scope(nc, stack, sems)
        xT = s.sb("x3T", [P, KD, N])
        w1 = s.sb("g_w1", [P, KD, FF])
        w2 = s.sb("g_w2", [P, KD, FF])
        h1 = s.sb("g_h1", [P, FC, FF])
        h2 = s.sb("g_h2", [P, FC, FF])
        w3 = s.sb("g_w3", [P, FC, D])
        sc = s.sb("g_sc", [P, 4, FC])
        s3 = s.sb("g_s3", [1, D])
        s3_all = s.sb("g_s3_all", [P, D])
        one = s.sb("g_one", [1, P])
        sil = s.sb("g_sil", [P, 2, L])
        ha = s.sb("g_ha", [P, FC, L])
        hb = s.sb("g_hb", [P, FC, L])
        y = s.sb("g_y", [P, 2, TL, D])
        ps = s.ps("ps_glu", [P, 8, BANK])
        loaded, h_loaded, t_done = s.sem("g_loaded"), s.sem("g_h_loaded"), s.sem("g_t")
        xT_in, s3_in, s3_ps, one_in = s.sem("g_xT"), s.sem("g_s3_in"), s.sem("g_s3_ps"), s.sem("g_one_in")
        S = {n: s.sem("g_" + n) for n in "a b sil glu l1 ga l2 gb o y1 y stored0 stored1".split()}
        NB = N // L
        with nc.Block() as block:

            @block.sync
            def _(sp):
                sems.clear_last(sp)
                for dst, name in ((w1, "w1T"), (w2, "w2T")):
                    sp.dma_start(dst[:, :, :], A[name].rearrange("(k p) n -> p k n", p=P)).then_inc(loaded, 16)
                sp.dma_start(sc[:, :, :], A["ffn_s"]).then_inc(loaded, 16)
                sp.dma_start(s3[:, :], A["w3_s"]).then_inc(loaded, 16)
                for dst, name in ((h1, "h1T"), (h2, "h2T"), (w3, "w3T")):
                    sp.dma_start(dst[:, :, :], A[name].rearrange("(k p) n -> p k n", p=P)).then_inc(h_loaded, 16)
                out_v = out.rearrange("(q m p) d -> p q m d", p=P, m=TL)
                with sp.Fori(0, NB - 1, 2) as q0:
                    for u in range(2):
                        q = q0 + u
                        sp.wait_ge(S["y"], (q + 1) * TL)
                        sp.dma_start(out_v[:, bass.ds(q, 1), :, :].rearrange("p q m d -> p (q m) d"),
                                     y[:, u, :, :]).then_inc(S[f"stored{u}"], 16)
                for u in range(2):
                    sp.wait_ge(S[f"stored{u}"], 16 + 16 * NB // 2)

            @block.tensor
            def _(pe):
                for i in range(NT):
                    for k in range(KD):
                        at = (i % 2 * KD + k) * P
                        last = nc.tensor.transpose(ps[:, i // 2 % 8, at:at + P], x3[:, i, k * P:(k + 1) * P], ident[:, :])
                    if i % 2:
                        last.then_inc(t_done, 1)
                pe.wait_ge(loaded, 64)
                pe.wait_ge(one_in, 1)
                pe.sem_inc(S["o"], 1)
                pe.wait_ge(xT_in, NT // 2)
                nc.tensor.matmul(ps[:, 0, 0:D], one[0:1, :], s3[0:1, :], start=True, stop=True).then_inc(s3_ps, 1)
                pe.wait_ge(s3_in, 1)
                pe.wait_ge(h_loaded, 48)
                with pe.Fori(0, NB) as q:
                    for c in range(FC):
                        pe.wait_ge(S["glu"], q * FC + (c + 1))
                        for w, at, done in ((w1, 0, "a"), (w2, 1, "b")):
                            for k in range(KD):
                                last = nc.tensor.matmul(ps[:, c % 2 * 2 + at, :], w[:, k, c * P:(c + 1) * P],
                                                        xT[:, k, bass.ds(q * L, L)], start=k == 0, stop=k == KD - 1)
                            last.then_inc(S[done], 1)
                    for w, src, before, done, after, bank in ((h1, ha, "glu", "l1", "ga", 4), (h2, hb, "ga", "l2", "gb", 6)):
                        pe.wait_ge(S[before], q * FC + (FC + 2))
                        for c in range(FC):
                            pe.wait_ge(S[after], q * FC + (c + 1))
                            for k in range(FC):
                                last = nc.tensor.matmul(ps[:, bank + c % 2, :], w[:, k, c * P:(c + 1) * P], src[:, k, :],
                                                        start=k == 0, stop=k == FC - 1)
                            last.then_inc(S[done], 1)
                    pe.wait_ge(S["gb"], q * FC + (FC + 2))
                    for m in range(TL):
                        for c in range(FC):
                            last = nc.tensor.matmul(ps[:, m, 0:D], ha[:, c, m * P:(m + 1) * P], w3[:, c, :],
                                                    start=c == 0, stop=c == FC - 1)
                        last.then_inc(S["o"], 1)
                    pe.wait_ge(S["y1"], (q + 1) * TL)

            @block.scalar
            def _(act):
                for i in range(0, NT, 2):
                    act.wait_ge(t_done, i // 2 + 1)
                    nc.scalar.activation(
                        xT[:, :, i * P:(i + 2) * P].rearrange("p k (i t) -> p i k t", i=2),
                        ps[:, i // 2 % 8, :].rearrange("p (i k t) -> p i k t", i=2, k=KD), ACT.Copy).then_inc(xT_in, 1)
                act.wait_ge(loaded, 64)
                act.sem_inc(S["ga"], 2)
                act.sem_inc(S["gb"], 2)
                with act.Fori(0, NB) as q:
                    for c in range(FC):
                        act.wait_ge(S["a"], q * FC + (c + 1))
                        act.wait_ge(S["glu"], q * FC + (c + 1))
                        nc.scalar.activation(sil[:, c % 2, :], ps[:, c % 2 * 2, :], ACT.Silu,
                                             scale=sc[:, 0, c:c + 1]).then_inc(S["sil"], 1)
                    for c in range(FC):
                        act.wait_ge(S["l1"], q * FC + (c + 1))
                        nc.scalar.activation(hb[:, c, :], ps[:, 4 + c % 2, :], ACT.Gelu,
                                             scale=sc[:, 2, c:c + 1]).then_inc(S["ga"], 1)
                    for c in range(FC):
                        act.wait_ge(S["l2"], q * FC + (c + 1))
                        nc.scalar.activation(ha[:, c, :], ps[:, 6 + c % 2, :], ACT.Gelu,
                                             scale=sc[:, 3, c:c + 1]).then_inc(S["gb"], 1)

            @block.vector
            def _(dve):
                nc.vector.memset(one[:, :], 1.0).then_inc(one_in, 1)
                dve.wait_ge(s3_ps, 1)
                nc.vector.tensor_copy(s3_all[:, :], ps[:, 0, 0:D]).then_inc(s3_in, 1)
                dve.wait_ge(s3_in, 1)
                dve.wait_ge(loaded, 64)
                dve.sem_inc(S["glu"], 2)
                dve.sem_inc(S["stored0"], 16)
                dve.sem_inc(S["stored1"], 16)
                with dve.Fori(0, NB - 1, 2) as q0:
                    for u in range(2):
                        q = q0 + u
                        for c in range(FC):
                            dve.wait_ge(S["sil"], q * FC + (c + 1))
                            dve.wait_ge(S["b"], q * FC + (c + 1))
                            if c == 0:
                                dve.wait_ge(S["o"], q * TL + 1)
                            nc.vector.scalar_tensor_tensor(ha[:, c, :], ps[:, c % 2 * 2 + 1, :], sc[:, 1, c:c + 1],
                                                           sil[:, c % 2, :], ALU.mult, ALU.mult).then_inc(S["glu"], 1)
                        dve.wait_ge(S[f"stored{u}"], q0 * 8 + 16)
                        for m in range(TL):
                            dve.wait_ge(S["o"], q * TL + (m + 2))
                            nc.vector.tensor_tensor(y[:, u, m, :], ps[:, m, 0:D], s3_all[:, :], ALU.mult).then_inc(S["y1"], 1)
                            dve.wait_ge(S["y1"], q * TL + (m + 1))
                            nc.vector.tensor_tensor(y[:, u, m, :], y[:, u, m, :],
                                                    x1[:, bass.ds(q * TL + m, 1), :].rearrange("p i d -> p (i d)"),
                                                    ALU.add).then_inc(S["y"], 1)


def hyperbolic_block(nc, sems, A, ident, x1, x3):
    with ExitStack() as stack:
        s = Scope(nc, stack)
        ada = s.sb("ada", [P, B, 6, D])
        ada_rows(nc, sems, A, ada)
        with ExitStack() as inner:
            heads = ExitStack()
            s2 = Scope(nc, heads)
            va = s2.sb("va", [P, NT, H, HD], side="right")
            qT = s2.sb("qT", [P, H // 2, N], F16, side="right")
            kT = s2.sb("kT", [P, H // 2, N], F16, side="right")
            with ExitStack() as first:
                s3 = Scope(nc, first)
                vT = s3.sb("vT", [P, KD, N])
                ident16 = s3.sb("ident16", [P, P], F16)
                scratch = x3[:, :, :].rearrange("p i d -> p (i d)")
                sums = 4 * 3 * D
                norm_modulate(nc, sems, "n1_", x1, ada, 0, ident, vT)
                qkv(nc, sems, A, ident16, vT, qT, kT, va, scratch[:, 0:sums].rearrange("p (i n) -> p i n", i=4),
                    scratch[:, sums:sums + NT * 3 * H].rearrange("p (i h) -> p i h", h=H))
            oT = Scope(nc, inner).sb("oT", [P, 4, N])
            attention(nc, sems, qT, kT, va, oT)
            heads.close()
            aT = Scope(nc, inner).sb("aT", [P, KD, N])
            heads_out(nc, sems, ident, oT, aT, x3)
            project_out(nc, sems, A, aT, x3)
        lin = s.sb("lin", [P, NT, D])
        hyper_residual(nc, sems, "r1_", x1, x3, ada, 2, x3)
        with ExitStack() as inner:
            s2 = Scope(nc, inner)
            vT = s2.sb("vT2", [P, KD, N])
            norm_modulate(nc, sems, "n2_", x3, ada, 3, ident, vT)
            feed_forward(nc, sems, A, vT, lin)
        hyper_residual(nc, sems, "r2_", x3, lin, ada, 5, x3)


def build(nc, A, out):
    sems = Semaphores(nc)
    with ExitStack() as stack:
        s = Scope(nc, stack)
        ident = s.sb("ident", [P, P])
        x1 = s.sb("x1", [P, NT, D])
        with ExitStack() as inner:
            s2 = Scope(nc, inner)
            hist = s2.sb("hist", [P, T, KD, B])
            xw = s2.sb("xw", [P, T, G8 * B])
            wq = s2.sb("wq", [P, 2, KD, 4 * D], F16)
            gate_scale = s2.sb("gate_scale", [P, 1])
            lstm_inputs(nc, sems, A, xw, wq, gate_scale, ident)
            weights = [s2.sb(name, [P] + shape) for name, shape in (
                ("w_in", [KD, 2 * DI]), ("conv_w", [CI, DCONV]), ("conv_b", [CI]), ("w_dt", [CI]), ("b_dt", [CI]),
                ("w_x", [CI, 2 * DS + 1]), ("norm_w", [KD]), ("ones", [P]),
                ("a_neg", [CI, DS]), ("d_par", [CI]), ("w_out", [CI, D]))]
            load_weights(nc, sems, A, x1, weights)
            lstm_mamba(nc, sems, A, xw, wq, gate_scale, ident, hist, x1, weights)
        x3 = s.sb("x3", [P, NT, D])
        hyperbolic_block(nc, sems, A, ident, x1, x3)
        glu_ffn(nc, sems, A, ident, x1, x3, out)



def kernel(**inputs):
    import concourse.bacc as bacc
    from concourse.bass_utils import run_bass_kernel_spmd

    a = {k.replace("L0_", ""): np.asarray(v) for k, v in inputs.items()}

    def chunks(v):
        v = v.reshape((-1, P) + v.shape[1:])
        return np.moveaxis(v, 0, 1)

    def gates(w):
        return np.concatenate([w[..., 0:2 * D], w[..., 3 * D:4 * D], w[..., 2 * D:3 * D]], axis=-1)

    x = a["x"].reshape(N, D)
    arrays = {
        "x": x, "xT": x.T, "condT": a["cond_1024"].T,
        "Wx": gates(a["cond_Wx"]), "Wh": gates(a["cond_Wh"]), "b": chunks(gates(a["cond_b"])),
        "ident": np.eye(P, dtype=np.float32), "ident16": np.eye(P, dtype=np.float16),
        "norm_w": chunks(a["attn_norm_w"]), "w_in": a["attn_W_in"], "conv_w": chunks(a["attn_conv_w"][:, 0, :]),
        "conv_b": chunks(a["attn_conv_b"]), "w_x": a["attn_W_x"], "w_dt": chunks(a["attn_w_dt"]),
        "b_dt": chunks(a["attn_b_dt"]), "a_log": chunks(a["attn_A_log"]), "d_par": chunks(a["attn_D_param"]),
        "w_out": a["attn_W_out"],
        "w_qkv": np.concatenate([a["cond2_w_q"], a["cond2_w_k"], a["cond2_w_v"]], axis=1),
        "b_qkv": np.concatenate([a["cond2_b_q"], a["cond2_b_k"], a["cond2_b_v"]])[None, :],
        "w_o": a["cond2_w_o"], "b_o": a["cond2_b_o"][None, :], "w_f1": a["cond2_w_f1"], "b_f1": chunks(a["cond2_b_f1"]),
        "w_f2": a["cond2_w_f2"], "b_f2": a["cond2_b_f2"][None, :], "w_ada": a["cond2_w_ada"], "b_ada": a["cond2_b_ada"][None, :],
        "w1T": a["ffn_w1_w"].T, "w2T": a["ffn_w2_w"].T, "h1T": a["ffn_h1_w"].T, "h2T": a["ffn_h2_w"].T, "w3T": a["ffn_w3_w"].T,
        "w3_s": a["ffn_w3_s"][None, :],
        "ffn_s": np.stack([chunks(a["ffn_" + n]) for n in ("w1_s", "w2_s", "h1_s", "h2_s")], axis=1),
    }
    arrays = {f"in_{k}": np.ascontiguousarray(v) for k, v in arrays.items()}
    nc = bacc.Bacc("TRN2", target_bir_lowering=False, num_devices=1)
    A = {k[3:]: nc.dram_tensor(k, v.shape, mybir.dt.from_np(v.dtype), kind="ExternalInput").ap() for k, v in arrays.items()}
    out = nc.dram_tensor("out_0_dram", (N, D), F32, kind="ExternalOutput").ap()
    build(nc, A, out)
    r = run_bass_kernel_spmd(nc, [arrays], core_ids=[0])
    return r.results[0]["out_0_dram"].reshape(B, T, D)
```

```python
import math
from contextlib import ExitStack

import numpy as np

import concourse.bass as bass
from concourse import mybir

F32 = mybir.dt.float32
F16 = mybir.dt.float16
I32 = mybir.dt.int32
ALU = mybir.AluOpType
ACT = mybir.ActivationFunctionType
AX = mybir.AxisListType

P = 128
B, T, D = 2, 1024, 256
N = B * T
KD = D // P
NT = N // P
BANK = 512
G8 = 4 * D // P
HC = KD * B
HEXP = 14
DI, DS, DCONV = 512, 16, 4
CI = DI // P


class Semaphores:

    def __init__(self, nc):
        self.nc, self.cleared, self.last, self.now = nc, [], [], []

    def new(self, name):
        guard = self.nc.semaphore(name)
        sem = guard.__enter__()
        self.now.append((guard, sem))
        return sem

    def next_stage(self):
        for guard, _ in self.cleared:
            guard.__exit__(None, None, None)
        self.cleared, self.last, self.now = self.last, self.now, []

    def clear_last(self, sp):
        for _, sem in self.last:
            sp.sem_clear(sem)


class Scope:

    def __init__(self, nc, stack, sems=None):
        self.nc, self.stack, self.sems = nc, stack, sems
        if sems:
            sems.next_stage()

    def sb(self, name, shape, dtype=F32, side="left"):
        return self.stack.enter_context(self.nc.sbuf_tensor(name, shape, dtype, side=side))

    def ps(self, name, shape, dtype=F32):
        return self.stack.enter_context(self.nc.psum_tensor(name, shape, dtype))

    def sem(self, name):
        return self.sems.new(name)


def fetch(sp, sems, tag, copies):
    if copies:
        done = sems.new(tag + "fetched")
        for dst, src in copies:
            sp.dma_start(dst, src).then_inc(done, 16)
        sp.wait_ge(done, 16 * len(copies))


def lstm_inputs(nc, sems, A, xw, wq, gate_scale, ident, copies):
    with ExitStack() as stack:
        s = Scope(nc, stack, sems)
        xT = s.sb("xT", [P, KD, N])
        wx = s.sb("wx", [P, KD, 4 * D])
        wh = s.sb("wh", [P, KD, 4 * D])
        ws = s.sb("ws", [P, KD, 4 * D])
        bias = s.sb("bias", [P, G8])
        bias_k = s.sb("bias_k", [P, G8])
        h0 = s.sb("h0", [P, KD, B])
        pmax = s.sb("pmax", [P, 1])
        wmax = s.sb("wmax", [P, 1])
        wmax_c = s.sb("wmax_c", [P, 1])
        pow2 = s.sb("pow2", [P, 1], I32)
        sc = s.sb("sc", [P, 2])
        kk = s.sb("kk", [P, 2])
        ps = s.ps("ps_in", [P, 8, BANK])
        loaded, wh_loaded = s.sem("a_loaded"), s.sem("a_wh_loaded")
        pmax_ready, wmax_ready, chain = s.sem("a_pmax"), s.sem("a_wmax"), s.sem("a_chain")
        scales_ready = s.sem("a_scales")
        bank_full, bank_free = s.sem("a_full"), s.sem("a_free")
        h0_product, scaled, split, evac = s.sem("a_h0"), s.sem("a_scaled"), s.sem("a_split"), s.sem("a_evac")
        TB = T // BANK
        HALF = (0, 1, 2, 3, 6, 7)
        with nc.Block() as block:

            @block.sync
            def _(sp):
                sems.clear_last(sp)
                sp.dma_start(wh[:, :, :], A["Wh"].rearrange("(k p) n -> p k n", p=P)).then_inc(wh_loaded, 16)
                sp.dma_start(wx[:, :, :], A["Wx"].rearrange("(k p) n -> p k n", p=P)).then_inc(loaded, 16)
                sp.dma_start(xT[:, :, :], A["xT"].rearrange("(k p) n -> p k n", p=P)).then_inc(loaded, 16)
                sp.dma_start(bias[:, :], A["b"]).then_inc(loaded, 16)
                sp.dma_start(h0[:, :, :], A["condT"].rearrange("(k p) b -> p k b", p=P)).then_inc(loaded, 16)
                sp.dma_start(ident[:, :], A["ident"]).then_inc(loaded, 16)
                fetch(sp, sems, "a_", copies)

            @block.gpsimd
            def _(pool):
                pool.wait_ge(pmax_ready, 1)
                nc.gpsimd.partition_all_reduce(wmax[:, :], pmax[:, :], P,
                                               bass.bass_isa.ReduceOp.max).then_inc(wmax_ready, 1)

            @block.tensor
            def _(pe):
                pe.wait_ge(loaded, 16 * 5)
                with pe.Fori(0, TB) as tb:
                    for b in range(B):
                        for g in range(G8):
                            i = b * G8 + g
                            pe.wait_ge(bank_free, tb * (B * G8) + (i + 1))
                            for k in range(KD):
                                last = nc.tensor.matmul(ps[:, i % 8, :], wx[:, k, g * P:(g + 1) * P],
                                                        xT[:, k, bass.ds(tb * BANK + b * T, BANK)],
                                                        start=k == 0, stop=k == KD - 1)
                            last.then_inc(bank_full, 1)
                pe.wait_ge(wh_loaded, 16)
                pe.wait_ge(bank_free, TB * B * G8 + 1)
                for g in range(G8):
                    for k in range(KD):
                        last = nc.tensor.matmul(ps[:, 0, g * B:(g + 1) * B], wh[:, k, g * P:(g + 1) * P],
                                                h0[:, k, :], start=k == 0, stop=k == KD - 1)
                last.then_inc(h0_product, 1)

            @block.scalar
            def _(act):
                act.preload_act_table(ACT.Identity)
                act.sem_inc(bank_free, 8)
                act.wait_ge(scales_ready, 1)
                with act.Fori(0, TB) as tb:
                    for b in range(B):
                        for g in range(G8):
                            i = b * G8 + g
                            act.wait_ge(bank_full, tb * (B * G8) + (i + 1))
                            half = int(g in HALF)
                            nc.scalar.activation(xw[:, bass.ds(tb * BANK, BANK), g * B + b], ps[:, i % 8, :],
                                                 ACT.Identity, bias=bias_k[:, g:g + 1],
                                                 scale=kk[:, half:half + 1]).then_inc(bank_free, 1)

            @block.vector
            def _(dve):
                dve.wait_ge(wh_loaded, 16)
                nc.vector.tensor_scalar(ws[:, :, :], wh[:, :, :], -1.0, None, ALU.mult).then_inc(chain, 1)
                dve.wait_ge(chain, 1)
                nc.vector.tensor_tensor(ws[:, :, :], ws[:, :, :], wh[:, :, :], ALU.max).then_inc(chain, 1)
                dve.wait_ge(chain, 2)
                nc.vector.tensor_reduce(pmax[:, :], ws[:, :, :].rearrange("p k n -> p (k n)"),
                                        AX.X, ALU.max).then_inc(pmax_ready, 1)
                dve.wait_ge(wmax_ready, 1)
                nc.vector.tensor_scalar(wmax_c[:, :], wmax[:, :], 2.0 ** -40, 2.0 ** 100,
                                        ALU.max, ALU.min).then_inc(chain, 1)
                dve.wait_ge(chain, 3)
                nc.vector.tensor_scalar(pow2[:, :], wmax_c[:, :].bitcast(I32), 0x7F800000, None,
                                        ALU.bitwise_and).then_inc(chain, 1)
                dve.wait_ge(chain, 4)
                for col, e in ((0, 267), (1, 266)):
                    nc.vector.tensor_scalar(sc[:, col:col + 1].bitcast(I32), pow2[:, :], -1.0, float(e << 23),
                                            ALU.mult, ALU.add).then_inc(chain, 1)
                for col, e in ((0, 267 + HEXP), (1, 266 + HEXP)):
                    nc.vector.tensor_scalar(kk[:, col:col + 1].bitcast(I32), pow2[:, :], -1.0, float(e << 23),
                                            ALU.mult, ALU.add).then_inc(chain, 1)
                nc.vector.tensor_scalar(gate_scale[:, :].bitcast(I32), pow2[:, :], 1.0, -float((13 + HEXP) << 23),
                                        ALU.mult, ALU.add).then_inc(chain, 1)
                dve.wait_ge(chain, 9)
                dve.wait_ge(loaded, 16 * 5)
                nc.vector.tensor_scalar(bias_k[:, 0:4], bias[:, 0:4], kk[:, 1:2], None, ALU.mult).then_inc(chain, 1)
                nc.vector.tensor_scalar(bias_k[:, 4:6], bias[:, 4:6], kk[:, 0:1], None, ALU.mult).then_inc(chain, 1)
                nc.vector.tensor_scalar(bias_k[:, 6:8], bias[:, 6:8], kk[:, 1:2], None, ALU.mult).then_inc(chain, 1)
                dve.wait_ge(chain, 12)
                dve.sem_inc(scales_ready, 1)
                for lo, hi, half in ((0, 4, 1), (4, 6, 0), (6, 8, 1)):
                    nc.vector.tensor_scalar(ws[:, :, lo * P:hi * P], wh[:, :, lo * P:hi * P],
                                            sc[:, half:half + 1], None, ALU.mult).then_inc(scaled, 1)
                dve.wait_ge(scaled, 3)
                nc.vector.tensor_copy(wq[:, 0, :, :], ws[:, :, :]).then_inc(split, 1)
                dve.wait_ge(split, 1)
                nc.vector.tensor_tensor(wq[:, 1, :, :], ws[:, :, :], wq[:, 0, :, :], ALU.subtract).then_inc(split, 1)
                dve.wait_ge(h0_product, 1)
                dve.wait_ge(bank_free, 8 + TB * B * G8)
                for lo, hi, half in ((0, 4, 1), (4, 6, 0), (6, 8, 1)):
                    c = slice(lo * B, hi * B)
                    nc.vector.scalar_tensor_tensor(xw[:, 0, c], ps[:, 0, c], kk[:, half:half + 1], xw[:, 0, c],
                                                   ALU.mult, ALU.add).then_inc(evac, 1)
                dve.wait_ge(evac, 3)


def row(ap, width):
    return ap.unsqueeze(len(ap.shape)).broadcast_to(list(ap.shape) + [width])


def lstm_mamba(nc, sems, A, xw, wq, gate_scale, ident, hist, x1, W):
    IFG, O = 6 * B, 2 * B
    LB = 128
    NB = T // LB
    L = B * LB
    U = DS * CI
    PE_U, ACT_U, DVE_U = 37, 35, 36
    HALF = 2.0 ** (HEXP - 1)
    with ExitStack() as stack:
        s_ = Scope(nc, stack, sems)
        gates = s_.sb("gates", [P, 2, IFG + HC])
        pre = s_.sb("pre", [P, IFG])
        pre_o = s_.sb("pre_o", [P, O])
        pre_x = s_.sb("pre_x", [P, O])
        xo = s_.sb("xo", [P, O])
        og = s_.sb("og", [P, O])
        og1 = s_.sb("og1", [P, O])
        prod = s_.sb("prod", [P, 2 * HC])
        tc = s_.sb("tc", [P, HC])
        h16 = s_.sb("h16", [P, 2, KD, 2, B], F16)
        hs = s_.sb("hs", [P, KD, B, LB])
        msv = s_.sb("msv", [P, B])
        minus_half = s_.sb("minus_half", [P, B])
        one2 = s_.sb("one2", [P, B])
        rstd = s_.sb("rstd", [P, B])
        rstd_b = s_.sb("rstd_b", [P, B, P])
        xn = s_.sb("xn", [P, KD, L])
        xp = s_.sb("xp", [P, CI, B, DCONV - 1 + LB])
        acc = s_.sb("acc", [P, CI, B, LB])
        th = s_.sb("th", [P, CI, L])
        xc = s_.sb("xc", [P, CI, L])
        par = s_.sb("par", [2 * DS + 1, L])
        rows = s_.sb("rows", [1, DS + 1, 2, L])
        dt = s_.sb("dt", [P, CI, L])
        uu = s_.sb("uu", [P, CI, L])
        ab = s_.sb("ab", [P, CI, L])
        bx = s_.sb("bx", [P, CI, L])
        hh = s_.sb("hh", [P, CI, L])
        cb = s_.sb("cb", [P, 2, L])
        sq = cb.rearrange("p k (b t) -> p k b t", b=B)
        hc = s_.sb("hc", [P, 2, L])
        state = s_.sb("state", [P, CI, B, DS])
        y = s_.sb("y", [P, CI, L])
        hf = s_.sb("hf", [P, HC])
        v = acc.rearrange("p c b t -> p c (b t)")
        w_in, conv_w, conv_b, w_dt, b_dt, w_x, norm_w, ones, a_neg, d_par, w_out = W
        ps_g, ps_o = s_.ps("ps_g", [P, BANK]), s_.ps("ps_o", [P, BANK])
        ps_z = s_.ps("ps_z", [P, 2, BANK])
        ps_b = s_.ps("ps_b", [P, 2, BANK])
        ps_c = s_.ps("ps_c", [P, 2, BANK])
        h_kept, xo_in = s_.sem("h_kept"), s_.sem("xo_in")
        ready = s_.sem("ready")
        ifg_sum, o_sum, ifg_pre, o_pre0, o_pre = (s_.sem(n) for n in ("ifg_sum", "o_sum", "ifg_pre", "o_pre0", "o_pre"))
        ifg_gate, o_gate, o_and_c = s_.sem("ifg_gate"), s_.sem("o_gate"), s_.sem("o_and_c")
        p_ready, cell = s_.sem("p_ready"), s_.sem("cell")
        h_parts, h_ready = s_.sem("h_parts"), s_.sem("h_ready")
        S = {n: s_.sem("m_" + n) for n in (
            "init mh hs sq ms msv rstd rb xn xproj xp tap halo th xc prm par rows_in dtb v abs exp ln dt u xd y0 "
            "b_row c_row cb ab bx scan state kept hc y z thz z2 yz out x1").split()}

        def o_on_act(s):
            return ACT_U <= s < DVE_U + U

        def z_bank(c, tail):
            return (ps_g, ps_o)[c % 2][:, 0:L] if tail else ps_z[:, c % 2, 0:L]

        with nc.Block() as block:

            @block.sync
            def _(sp):
                sems.clear_last(sp)
                with sp.Fori(0, NB) as j:
                    sp.wait_ge(S["par"], j + 1)
                    for bc in range(2):
                        sp.dma_start(rows[0:1, 0:DS, bc, :], par[1 + bc * DS:1 + (bc + 1) * DS, :]).then_inc(S["rows_in"], 16)

            @block.gpsimd
            def _(pool):
                nc.gpsimd.memset(minus_half[:, :], -0.5).then_inc(S["mh"], 1)
                nc.gpsimd.memset(one2[:, :], 1.0).then_inc(S["mh"], 1)
                pool.wait_ge(S["mh"], 2)
                def work(j, tail):
                    pool.wait_ge(S["hs"], j + 1)
                    nc.gpsimd.tensor_tensor(sq[:, :, :, :], hs[:, :, :, :], hs[:, :, :, :], ALU.mult).then_inc(S["sq"], 1)
                    pool.wait_ge(S["msv"], j + 1)
                    nc.gpsimd.tensor_tensor(rstd[:, :], msv[:, :], minus_half[:, :], ALU.pow).then_inc(S["rstd"], 1)
                    for c in range(CI):
                        pool.wait_ge(S["xc"], j * 2 + (c // 2 + 1))
                        nc.gpsimd.tensor_tensor(y[:, c, :], xc[:, c, :], d_par[:, c:c + 1].broadcast_to([P, L]),
                                                ALU.mult).then_inc(S["xd"], 1)
                    for c in range(CI):
                        pool.wait_ge(S["dt"], j * 2 + (c // 2 + 1))
                        nc.gpsimd.tensor_tensor(uu[:, c, :], dt[:, c, :], xc[:, c, :], ALU.mult).then_inc(S["u"], 1)
                    with pool.Fori(0, DS - 1, 2) as n0:
                        for i in range(2 * CI):
                            g, c = j * U + n0 * CI + i, i % CI
                            if c == 0:
                                pool.wait_ge(S["cb"], j * DS + n0 + (i // CI + 2))
                            if tail:
                                pool.wait_ge(S["y"], g + 7)
                            pool.wait_ge(S["scan"], g * 2 + 10)
                            if not tail:
                                nc.gpsimd.tensor_tensor(state[:, c, :, bass.ds(n0 + i // CI, 1)].rearrange("p b n -> p (b n)"),
                                                        hh[:, c, :].rearrange("p (b t) -> p b t", b=B)[:, :, LB - 1:LB]
                                                        .rearrange("p b t -> p (b t)"), one2[:, :], ALU.mult).then_inc(S["state"], 1)
                            nc.gpsimd.tensor_tensor(hc[:, c % 2, :], hh[:, c, :], cb[:, i // CI, :],
                                                    ALU.mult).then_inc(S["hc"], 1)
                            if not tail:
                                pool.wait_ge(S["hc"], g + 9)
                                pool.wait_ge(S["xd"], j * CI + (c + 1))
                                pool.wait_ge(S["y"], g + 5)
                                nc.gpsimd.tensor_tensor(y[:, c, :], y[:, c, :], hc[:, c % 2, :], ALU.add).then_inc(S["y"], 1)
                                pool.wait_ge(S["state"], g + 1)
                                pool.sem_inc(S["kept"], 1)

                with pool.Fori(0, NB - 1) as j:
                    work(j, False)
                work(NB - 1, True)

            @block.tensor
            def _(pe):
                def lstm_products(t, u, extra):
                    pe.wait_ge(ifg_pre, t + 1)
                    nc.tensor.matmul(ps_g[:, 0:IFG], ident[:, :], xw[:, bass.ds(t, 1), 0:IFG],
                                     start=True, stop=False, skip_group_check=True)
                    extra()
                    pe.wait_ge(h_ready, t + 1)
                    for g in range(G8):
                        bank, at, width, done = (ps_g, g * B, IFG, ifg_sum) if g < 6 else (ps_o, (g - 6) * B, O, o_sum)
                        cols = bank[:, 0:2 * width].rearrange("p (h c) -> p h c", h=2)[:, :, at:at + B]
                        for k in range(KD):
                            for w in range(2):
                                last = nc.tensor.matmul(cols, wq[:, w, k, g * P:(g + 1) * P], h16[:, u, k, :, :],
                                                        start=g == 6 and k == 0 and w == 0,
                                                        stop=k == KD - 1 and w == 1, skip_group_check=True)
                        if g in (5, 7):
                            last.then_inc(done, 1)

                def b_row(m, n, bx_done):
                    pe.wait_ge(S["bx"], bx_done)
                    nc.tensor.matmul(ps_b[:, m, 0:L], ones[0:1, :], n(0), start=True, stop=True).then_inc(S["b_row"], 1)

                def c_row(m, n, cb_done):
                    pe.wait_ge(S["cb"], cb_done)
                    nc.tensor.matmul(ps_c[:, m, 0:L], ones[0:1, :], n(1), start=True, stop=True).then_inc(S["c_row"], 1)

                def part1(s, j, tail=False):
                    if s in (3, 4):
                        b = s - 3
                        pe.wait_ge(S["sq"], j + 1)
                        for k in range(KD):
                            last = nc.tensor.matmul(ps_c[:, 0, b:b + 1], sq[:, k, b, :], ones[:, 0:1],
                                                    start=k == 0 and b == 0, stop=k == KD - 1, skip_group_check=True)
                        last.then_inc(S["ms"], 1)
                    elif s == 7:
                        pe.wait_ge(S["rb"], j + 1)
                        for b in range(B):
                            last = nc.tensor.matmul(ps_c[:, 0, b * LB:(b + 1) * LB], rstd_b[:, b, :], ident[:, :],
                                                    start=b == 0, stop=True, skip_group_check=True)
                        last.then_inc(S["ms"], 1)
                    elif 10 <= s < 18:
                        c, k = (s - 10) // 2, (s - 10) % 2
                        if k == 0:
                            pe.wait_ge(S["xn"], j * KD + KD)
                            pe.wait_ge(S["xp"], j * CI + (c + 1))
                        last = nc.tensor.matmul(ps_c[:, (c + 1) % 2, 0:L], w_in[:, k, c * P:(c + 1) * P], xn[:, k, :],
                                                start=k == 0, stop=k == KD - 1)
                        if k:
                            last.then_inc(S["xproj"], 1)
                    elif 24 <= s < 28:
                        c = s - 24
                        pe.wait_ge(S["xc"], j * 2 + (c // 2 + 1))
                        if c == 0:
                            pe.wait_ge(S["xp"], j * CI + (CI + 2))
                        last = nc.tensor.matmul(ps_c[0:2 * DS + 1, 0, 0:L], w_x[:, c, :], xc[:, c, :],
                                                start=c == 0, stop=c == CI - 1)
                        if c == CI - 1:
                            last.then_inc(S["prm"], 1)
                    elif s == 29:
                        pe.wait_ge(S["par"], j + 1)
                        nc.tensor.matmul(ps_c[:, 1, 0:L], ones[0:1, :], par[0:1, :], start=True, stop=True).then_inc(S["dtb"], 1)
                    elif s == 28 and tail:
                        pe.wait_ge(S["xd"], j * CI + CI)
                        for q in range(2):
                            nc.tensor.matmul(ps_z[:, q, :], ident[:, :], y[:, 2 * q:2 * q + 2, :],
                                             start=True, stop=False, skip_group_check=True)
                    elif s == 33:
                        pe.wait_ge(S["rows_in"], j * 32 + 32)
                        pe.wait_ge(S["v"], j * CI + CI)
                        c_row(0, lambda bc: rows[0:1, 0, bc, :], j * DS + 1)
                    elif s == 34:
                        b_row(0, lambda bc: rows[0:1, 0, bc, :], j * U + 4)

                def unit(j, n0, i, tail=False):
                    c, nxt = i % CI, i // CI + 1
                    row_of = lambda bc: rows[0:1, bass.ds(n0 + nxt, 1), bc, :]
                    if c == 0:
                        c_row(nxt % 2, row_of, j * DS + n0 + nxt)
                    elif c == 1:
                        b_row(nxt % 2, row_of, j * U + n0 * CI + nxt * CI)
                    if tail:
                        pe.wait_ge(S["hc"], j * U + n0 * CI + (i + 9))
                        nc.tensor.matmul(ps_z[:, c // 2, c % 2 * L:(c % 2 + 1) * L], ident[:, :], hc[:, c % 2, :],
                                         start=False, stop=True, skip_group_check=True).then_inc(S["y"], 1)

                def part3(s, j, tail=False):
                    if 101 <= s < 109:
                        c, k = (s - 101) // 2, (s - 101) % 2
                        if k == 0:
                            pe.wait_ge(S["z2"], j * CI + (c + 1))
                        last = nc.tensor.matmul(z_bank(c, tail), w_in[:, k, DI + c * P:DI + (c + 1) * P], xn[:, k, :],
                                                start=k == 0, stop=k == KD - 1)
                        if k:
                            last.then_inc(S["z"], 1)
                    elif 109 <= s < 119:
                        b, part = (s - 109) // 5, (s - 109) % 5
                        if part == 0:
                            pe.wait_ge(S["cb"], j * DS + (DS + 1))
                            for k in range(KD):
                                nc.tensor.matmul(ps_c[:, b, k * P:(k + 1) * P], hs[:, k, b, :], ident[:, :],
                                                 start=k == 0, stop=False, skip_group_check=True)
                        else:
                            c = part - 1
                            pe.wait_ge(S["yz"], j * CI + (c + 1))
                            last = nc.tensor.matmul(ps_c[:, b, 0:D], y[:, c, b * LB:(b + 1) * LB], w_out[:, c, :],
                                                    start=False, stop=c == CI - 1, skip_group_check=True)
                            if c == CI - 1:
                                last.then_inc(S["out"], 1)

                none = lambda: None
                pe.wait_ge(ready, 1)
                with pe.Fori(0, LB - 1, 2) as t0:
                    for u in range(2):
                        lstm_products(t0 + u, u, none)
                with pe.Fori(1, NB) as k:
                    for s in range(PE_U):
                        lstm_products(k * LB + s, s % 2, lambda: part1(s, k - 1))
                    with pe.Fori(0, DS - 1, 2) as n0:
                        for i in range(2 * CI):
                            lstm_products(k * LB + n0 * CI + (PE_U + i), (PE_U + i) % 2, lambda: unit(k - 1, n0, i))
                    for s in range(PE_U + U, LB):
                        lstm_products(k * LB + s, s % 2, lambda: part3(s, k - 1))
                for s in range(PE_U):
                    part1(s, NB - 1, True)
                with pe.Fori(0, DS - 1, 2) as n0:
                    for i in range(2 * CI):
                        unit(NB - 1, n0, i, True)
                for s in range(PE_U + U, LB):
                    part3(s, NB - 1, True)

            @block.scalar
            def _(act):
                unscale = act.alloc_register("unscale")
                act.reg_load(unscale, gate_scale[0:1, 0:1].bitcast(I32))
                act.preload_act_table_set("exp_and_others")
                act.sem_inc(S["xp"], 2)
                act.sem_inc(S["cb"], 1)

                def lstm_gates(t, u, scale_o=False):
                    nc.scalar.activation(xo[:, :], xw[:, bass.ds(t, 1), IFG:IFG + O].rearrange("p t c -> p (t c)"),
                                         ACT.Copy).then_inc(xo_in, 1)
                    act.wait_ge(ifg_pre, t + 2)
                    nc.scalar.activation(gates[:, u, 0:IFG], pre[:, :], ACT.Tanh, scale=unscale).then_inc(ifg_gate, 1)
                    act.wait_ge(o_pre, t + 1)
                    nc.scalar.activation(og[:, :], pre_x[:, :], ACT.Tanh, scale=unscale).then_inc(o_gate, 1)
                    if scale_o:
                        act.wait_ge(o_gate, t + 1)
                        nc.scalar.activation(og1[:, :], og[:, :], ACT.Copy, scale=HALF, bias=HALF).then_inc(o_and_c, 1)
                    act.wait_ge(cell, t + 1)
                    nc.scalar.activation(tc[:, :], gates[:, 1 - u, IFG:IFG + HC], ACT.Tanh, scale=0.5).then_inc(o_and_c, 1)

                def part1(s, j):
                    if s in (11, 13, 15, 17):
                        c = (s - 11) // 2
                        act.wait_ge(S["xproj"], j * CI + (c + 1))
                        act.wait_ge(S["halo"], j + 1)
                        nc.scalar.activation(xp[:, c, :, DCONV - 1:],
                                             ps_c[:, (c + 1) % 2, 0:L].rearrange("p (b t) -> p b t", b=B),
                                             ACT.Copy).then_inc(S["xp"], 1)
                    elif s in (18, 22):
                        q = (s - 18) // 4
                        act.wait_ge(S["tap"], j * 16 + (q + 1) * 8)
                        nc.scalar.activation(th[:, 2 * q:2 * q + 2, :], acc[:, 2 * q:2 * q + 2, :, :]
                                             .rearrange("p c b t -> p c (b t)"), ACT.Tanh).then_inc(S["th"], 1)
                    elif s == 27:
                        act.wait_ge(S["prm"], j + 1)
                        nc.scalar.activation(par[:, :], ps_c[0:2 * DS + 1, 0, 0:L], ACT.Copy).then_inc(S["par"], 1)
                    elif s in (30, 31):
                        q = s - 30
                        act.wait_ge(S["v"], j * CI + (q + 1) * 2)
                        nc.scalar.activation(th[:, 2 * q:2 * q + 2, :], v[:, 2 * q:2 * q + 2, :], ACT.Abs).then_inc(S["abs"], 1)
                    elif s == 32:
                        act.wait_ge(S["abs"], j * 2 + 2)
                        nc.scalar.activation(th[:, :, :], th[:, :, :], ACT.Exp, scale=-1.0).then_inc(S["exp"], 1)
                    elif s == 33:
                        act.wait_ge(S["exp"], j + 1)
                        nc.scalar.activation(th[:, :, :], th[:, :, :], ACT.Ln, bias=1.0).then_inc(S["ln"], 1)
                        act.preload_act_table_set("exp_and_others")

                def unit(j, n0, i):
                    g, c = j * U + n0 * CI + i, i % CI
                    if c == 0:
                        act.wait_ge(S["c_row"], j * (DS + 1) + n0 + (i // CI + 1))
                        act.wait_ge(S["hc"], j * U + n0 * CI + (i + 4))
                        nc.scalar.activation(cb[:, i // CI, :], ps_c[:, i // CI, 0:L], ACT.Copy).then_inc(S["cb"], 1)
                    act.wait_ge(S["dt"], j * 2 + (c // 2 + 1))
                    act.wait_ge(S["scan"], g * 2 + 2)
                    nc.scalar.activation(ab[:, c, :], dt[:, c, :], ACT.Exp,
                                         scale=a_neg[:, c, bass.ds(n0 + i // CI, 1)]).then_inc(S["ab"], 1)

                def part3(s, j, tail=False):
                    if s in (102, 104, 106, 108):
                        c = (s - 102) // 2
                        act.wait_ge(S["z"], j * CI + (c + 1))
                        nc.scalar.activation(th[:, c, :], z_bank(c, tail), ACT.Tanh, scale=0.5).then_inc(S["thz"], 1)

                with act.Fori(0, LB - 1, 2) as t0:
                    for u in range(2):
                        lstm_gates(t0 + u, u)
                with act.Fori(1, NB) as k:
                    for s in range(ACT_U):
                        lstm_gates(k * LB + s, s % 2, o_on_act(s))
                        part1(s, k - 1)
                    with act.Fori(0, DS - 1, 2) as n0:
                        for i in range(2 * CI):
                            lstm_gates(k * LB + n0 * CI + (ACT_U + i), (ACT_U + i) % 2, o_on_act(ACT_U + i))
                            unit(k - 1, n0, i)
                    for s in range(ACT_U + U, LB):
                        lstm_gates(k * LB + s, s % 2, o_on_act(s))
                        part3(s, k - 1)
                for s in range(ACT_U):
                    part1(s, NB - 1)
                with act.Fori(0, DS - 1, 2) as n0:
                    for i in range(2 * CI):
                        unit(NB - 1, n0, i)
                for s in range(ACT_U + U, LB):
                    part3(s, NB - 1, True)

            @block.vector
            def _(dve):
                none = lambda: None

                def lstm_state(t, u, mid, end, scale_o=True):
                    both = 2 * t + 2
                    dve.wait_ge(ifg_sum, t + 1)
                    dve.wait_ge(xo_in, t + 1)
                    nc.vector.tensor_reduce(pre[:, :], ps_g[:, 0:2 * IFG].rearrange("p (h c) -> p c h", h=2),
                                            AX.X, ALU.add).then_inc(ifg_pre, 1)
                    dve.wait_ge(o_sum, t + 1)
                    nc.vector.tensor_reduce(pre_o[:, :], ps_o[:, 0:2 * O].rearrange("p (h c) -> p c h", h=2),
                                            AX.X, ALU.add).then_inc(o_pre0, 1)
                    dve.wait_ge(o_pre0, t + 1)
                    nc.vector.tensor_tensor(pre_x[:, :], pre_o[:, :], xo[:, :], ALU.add).then_inc(o_pre, 1)
                    dve.wait_ge(ifg_gate, t + 1)
                    nc.vector.scalar_tensor_tensor(prod[:, :], gates[:, u, 0:2 * HC], 1.0, gates[:, u, IFG - HC:IFG + HC],
                                                   ALU.add, ALU.mult).then_inc(p_ready, 1)
                    dve.wait_ge(p_ready, t + 1)
                    nc.vector.scalar_tensor_tensor(gates[:, 1 - u, IFG:IFG + HC], prod[:, HC:2 * HC], 0.5, prod[:, 0:HC],
                                                   ALU.mult, ALU.add).then_inc(cell, 1)
                    mid()
                    if scale_o:
                        dve.wait_ge(o_gate, t + 1)
                        nc.vector.tensor_scalar(og1[:, :], og[:, :], HALF, HALF, ALU.mult, ALU.add).then_inc(o_and_c, 1)
                    dve.wait_ge(o_and_c, both)
                    h = hf[:, :].rearrange("p (k b) -> p k b", k=KD)
                    o_kb = og1[:, :].rearrange("p (k b) -> p k b", k=KD)
                    tc_kb = tc[:, :].rearrange("p (k b) -> p k b", k=KD)
                    nc.vector.tensor_tensor(h, o_kb, tc_kb, ALU.mult).then_inc(h_parts, 1)
                    nc.vector.tensor_tensor(h16[:, 1 - u, :, 0, :], o_kb, tc_kb, ALU.mult).then_inc(h_parts, 1)
                    dve.wait_ge(h_parts, both)
                    nc.vector.tensor_tensor(h16[:, 1 - u, :, 1, :], h, h16[:, 1 - u, :, 0, :],
                                            ALU.subtract).then_inc(h_ready, 1)
                    nc.vector.tensor_scalar(hist[:, bass.ds(t, 1), :, :].rearrange("p t k b -> p (t k b)"), hf[:, :],
                                            2.0 ** -HEXP, None, ALU.mult).then_inc(h_kept, 1)
                    end()

                def part1(s, j):
                    if s == 0:
                        dve.wait_ge(S["out"], j * B + 1)
                        dve.wait_ge(h_kept, j * LB + LB)
                        nc.vector.tensor_scalar(hs[:, :, :, :], hist[:, bass.ds(j * LB, LB), :, :].rearrange("p t k b -> p k b t"),
                                                1.0, None, ALU.mult).then_inc(S["hs"], 1)
                    elif s == 4:
                        dve.wait_ge(S["ms"], j * 3 + 2)
                        nc.vector.tensor_scalar(msv[:, :], ps_c[:, 0, 0:B], 1.0 / D, 1e-6, ALU.mult, ALU.add).then_inc(S["msv"], 1)
                    elif s == 5:
                        dve.wait_ge(S["rstd"], j + 1)
                        nc.vector.tensor_scalar(rstd_b[:, :, :], row(rstd[:, :], P), 1.0, None, ALU.mult).then_inc(S["rb"], 1)
                    elif s in (7, 8):
                        k = s - 7
                        dve.wait_ge(S["ms"], j * 3 + 3)
                        nc.vector.scalar_tensor_tensor(xn[:, k, :], hs[:, k, :, :].rearrange("p b t -> p (b t)"),
                                                       norm_w[:, k:k + 1], ps_c[:, 0, 0:L], ALU.mult, ALU.mult).then_inc(S["xn"], 1)
                    elif 14 <= s < 22:
                        q, tap = (s - 14) // 4, (s - 14) % 4
                        for c in (2 * q, 2 * q + 1):
                            src = xp[:, c, :, tap:tap + LB]
                            if tap == 0:
                                dve.wait_ge(S["xp"], j * CI + (c + 3))
                                nc.vector.tensor_scalar(acc[:, c, :, :], src, conv_w[:, c, 0:1], conv_b[:, c:c + 1],
                                                        ALU.mult, ALU.add).then_inc(S["tap"], 1)
                            else:
                                dve.wait_ge(S["tap"], j * 16 + (q * 8 + tap * 2 + c % 2 - 1))
                                nc.vector.scalar_tensor_tensor(acc[:, c, :, :], src, conv_w[:, c, tap:tap + 1], acc[:, c, :, :],
                                                               ALU.mult, ALU.add).then_inc(S["tap"], 1)
                    elif s in (22, 23):
                        q = s - 22
                        if q == 0:
                            nc.vector.tensor_scalar(xp[:, :, :, 0:DCONV - 1].rearrange("p c b t -> p (c b) t"),
                                                    xp[:, :, :, LB:].rearrange("p c b t -> p (c b) t"),
                                                    1.0, None, ALU.mult).then_inc(S["halo"], 1)
                        dve.wait_ge(S["th"], j * 2 + (q + 1))
                        nc.vector.scalar_tensor_tensor(xc[:, 2 * q:2 * q + 2, :], th[:, 2 * q:2 * q + 2, :], 1.0,
                                                       acc[:, 2 * q:2 * q + 2, :, :].rearrange("p c b t -> p c (b t)"),
                                                       ALU.add, ALU.mult).then_inc(S["xc"], 1)
                    elif s in (29, 30):
                        dve.wait_ge(S["dtb"], j + 1)
                        for c in range((s - 29) * 2, (s - 29) * 2 + 2):
                            nc.vector.tensor_scalar(v[:, c, :], ps_c[:, 1, 0:L], w_dt[:, c:c + 1], b_dt[:, c:c + 1],
                                                    ALU.mult, ALU.add).then_inc(S["v"], 1)
                    elif s in (34, 35):
                        q = s - 34
                        dve.wait_ge(S["ln"], j + 1)
                        nc.vector.scalar_tensor_tensor(dt[:, 2 * q:2 * q + 2, :], v[:, 2 * q:2 * q + 2, :], 0.0,
                                                       th[:, 2 * q:2 * q + 2, :], ALU.max, ALU.add).then_inc(S["dt"], 1)

                def unit_mid(j, n0, i):
                    g, c, m = j * U + n0 * CI + i, i % CI, i // CI
                    if c == 0:
                        dve.wait_ge(S["b_row"], j * (DS + 1) + n0 + (m + 1))
                    dve.wait_ge(S["u"], j * CI + (c + 1))
                    nc.vector.tensor_tensor(bx[:, c, :], uu[:, c, :], ps_b[:, m, 0:L], ALU.mult).then_inc(S["bx"], 1)

                def unit_end(j, n0, i, tail=False):
                    g, c, m = j * U + n0 * CI + i, i % CI, i // CI
                    dve.wait_ge(S["bx"], g + 5)
                    dve.wait_ge(S["ab"], g + 5)
                    dve.wait_ge(S["hc" if tail else "kept"], g + 5)
                    for b in range(B):
                        cols = slice(b * LB, (b + 1) * LB)
                        nc.vector.tensor_tensor_scan(hh[:, c, cols], ab[:, c, cols], bx[:, c, cols],
                                                     state[:, c, b, bass.ds(n0 + m, 1)],
                                                     ALU.mult, ALU.add).then_inc(S["scan"], 1)

                def part3(s, j, tail=False):
                    if s in (103, 105, 107, 109):
                        c = (s - 103) // 2
                        dve.wait_ge(S["thz"], j * CI + (c + 1))
                        nc.vector.scalar_tensor_tensor(th[:, c, :], th[:, c, :], 1.0, z_bank(c, tail),
                                                       ALU.add, ALU.mult).then_inc(S["z2"], 1)
                    if s in (104, 106, 108, 110):
                        c = (s - 104) // 2
                        dve.wait_ge(S["y"], (j + 1) * U + 8)
                        dve.wait_ge(S["z2"], j * CI + (c + 3))
                        nc.vector.scalar_tensor_tensor(y[:, c, :], ps_z[:, c // 2, c % 2 * L:(c % 2 + 1) * L] if tail else y[:, c, :], 0.5,
                                                       th[:, c, :], ALU.mult, ALU.mult).then_inc(S["yz"], 1)
                    if s in (113, 118):
                        b = (s - 113) // 5
                        dve.wait_ge(S["out"], j * B + (b + 2))
                        tile = x1[:, bass.ds(j + b * (T // P), 1), :].rearrange("p i d -> p (i d)")
                        nc.vector.tensor_tensor(tile, tile, ps_c[:, b, 0:D], ALU.add).then_inc(S["x1"], 1)

                nc.vector.memset(gates[:, 0, IFG:IFG + HC], 0.0).then_inc(S["init"], 1)
                nc.vector.memset(state[:, :, :, :], 0.0).then_inc(S["init"], 1)
                nc.vector.memset(xp[:, :, :, 0:DCONV - 1], 0.0).then_inc(S["init"], 1)
                nc.vector.memset(rows[0:1, DS, :, :], 0.0).then_inc(S["init"], 1)
                dve.wait_ge(S["init"], 4)
                for name, credit in (("halo", 1), ("out", 1), ("z2", 2), ("bx", 4), ("scan", 8),
                                     ("hc", 8), ("y", 8), ("ab", 4), ("kept", 8)):
                    dve.sem_inc(S[name], credit)
                dve.sem_inc(ifg_pre, 1)
                dve.sem_inc(ready, 1)
                nc.vector.memset(h16[:, 0, :, :, :], 0.0).then_inc(h_ready, 1)
                with dve.Fori(0, LB - 1, 2) as t0:
                    for u in range(2):
                        lstm_state(t0 + u, u, none, none)
                with dve.Fori(1, NB) as k:
                    for s in range(DVE_U):
                        lstm_state(k * LB + s, s % 2, none, lambda: part1(s, k - 1), not o_on_act(s))
                    with dve.Fori(0, DS - 1, 2) as n0:
                        for i in range(2 * CI):
                            lstm_state(k * LB + n0 * CI + (DVE_U + i), (DVE_U + i) % 2,
                                       lambda: unit_mid(k - 1, n0, i), lambda: unit_end(k - 1, n0, i), False)
                    for s in range(DVE_U + U, LB):
                        lstm_state(k * LB + s, s % 2, none, lambda: part3(s, k - 1))
                for s in range(DVE_U):
                    part1(s, NB - 1)
                with dve.Fori(0, DS - 1, 2) as n0:
                    for i in range(2 * CI):
                        unit_mid(NB - 1, n0, i)
                        unit_end(NB - 1, n0, i, True)
                for s in range(DVE_U + U, LB):
                    part3(s, NB - 1, True)


def make_weights(nc, sems, W):
    w_in, conv_w, conv_b, w_dt, b_dt, w_x, norm_w, ones, a_neg, d_par, w_out = W
    with ExitStack() as stack:
        s = Scope(nc, stack, sems)
        made, half = s.sem("w_made"), s.sem("w_half")
        with nc.Block() as block:

            @block.sync
            def _(sp):
                sems.clear_last(sp)

            @block.scalar
            def _(act):
                nc.scalar.activation(a_neg[:, :, :], a_neg[:, :, :], ACT.Exp).then_inc(made, 1)
                act.wait_ge(made, 1)
                nc.scalar.activation(a_neg[:, :, :], a_neg[:, :, :], ACT.Copy, scale=-1.0).then_inc(made, 1)
                act.wait_ge(made, 2)

            @block.vector
            def _(dve):
                nc.vector.memset(ones[:, :], 1.0).then_inc(half, 1)
                nc.vector.tensor_scalar(conv_w[:, :, :], conv_w[:, :, :], 0.5, None, ALU.mult).then_inc(half, 1)
                nc.vector.tensor_scalar(conv_b[:, :], conv_b[:, :], 0.5, None, ALU.mult).then_inc(half, 1)
                dve.wait_ge(half, 3)


EPS = 1e-7
MAXT = float(np.float32(1.0 - 1e-5))
ATANH = math.atanh(MAXT)
LN_A = math.log(ATANH)
TINY = 1e-18
H, HD, FF = 16, 16, 1024


def _beta(a, b):
    return math.exp(math.lgamma(a) + math.lgamma(b) - math.lgamma(a + b))


R_HEADS = _beta(HD / 2, 0.5) / _beta(D / 2, 0.5)
QSC = 256.0
TPB = NT // B


def norm_modulate(nc, sems, tag, x, ada, shift, ident, vT, copies, A=None):
    with ExitStack() as stack:
        s = Scope(nc, stack, sems)
        big = s.sb(tag + "big", [P, NT, D])
        v = s.sb(tag + "v", [P, NT, D])
        col = {n: s.sb(tag + n, [P, NT]) for n in "sum mean n2 var n m lp lm rn s s2v f r".split()}
        ps = s.ps(tag + "ps", [P, 8, BANK])
        link_v, link_a = s.sem(tag + "link_v"), s.sem(tag + "link_a")
        S = {n: s.sem(tag + n) for n in "sq1 n2 sq2 mean norm m logs s2v f v sq3 n2v r ready t used".split()}
        if A:
            W6 = 6 * D
            NC = W6 // BANK
            w_ada = s.sb("w_ada", [P, KD, W6])
            cond = s.sb("cond", [P, KD, B])
            cond_b = s.sb("cond_b", [P, KD, B, P])
            bias = s.sb("bias_ada", [1, W6])
            one = s.sb("one_ada", [1, P])
            loaded, made, full, made_ada = s.sem("d_loaded"), s.sem("d_made"), s.sem("d_full"), s.sem("d_out")
        with nc.Block() as block:

            @block.sync
            def _(sp):
                sems.clear_last(sp)
                if A:
                    sp.dma_start(cond[:, :, :], A["condT"].rearrange("(k p) b -> p k b", p=P)).then_inc(loaded, 16)
                    sp.dma_start(bias[:, :], A["b_ada"]).then_inc(loaded, 16)
                    sp.dma_start(w_ada[:, :, :], A["w_ada"].rearrange("(k p) n -> p k n", p=P)).then_inc(loaded, 16)
                fetch(sp, sems, tag, copies)

            @block.scalar
            def _(act):
                count = [0]

                def link(ins):
                    count[0] += 1
                    ins.then_inc(link_a, 1)
                    act.wait_ge(link_a, count[0])

                act.preload_act_table_set("natural_log_exp_and_others")
                half = [slice(b * TPB, (b + 1) * TPB) for b in range(B)]
                c = [{n: t[:, h] for n, t in col.items()} for h in half]
                for b in range(B):
                    nc.scalar.activation(big[:, half[b], :], x[:, half[b], :], ACT.Square).then_inc(S["sq1"], 1)
                for b in range(B):
                    act.wait_ge(S["n2"], b + 1)
                    link(nc.scalar.activation(c[b]["lp"], c[b]["n2"], ACT.Ln))
                    link(nc.scalar.activation(c[b]["rn"], c[b]["lp"], ACT.Exp, scale=-0.5))
                    nc.scalar.activation(c[b]["n"], c[b]["lp"], ACT.Exp, scale=0.5).then_inc(S["norm"], 1)
                for b in range(B):
                    act.wait_ge(S["m"], b + 1)
                    link(nc.scalar.activation(c[b]["lp"], c[b]["m"], ACT.Ln, bias=1.0))
                    nc.scalar.activation(c[b]["lm"], c[b]["m"], ACT.Ln, bias=1.0, scale=-1.0).then_inc(S["logs"], 1)
                    act.wait_ge(S["sq2"], b + 1)
                    nc.scalar.activation(big[:, half[b], :], v[:, half[b], :], ACT.Square).then_inc(S["sq3"], 1)
                if A:
                    for b in range(B):
                        for lo in range(0, W6, D):
                            act.wait_ge(full, b * NC + lo // BANK + 1)
                            plus = 1.0 if lo // D in (1, 4) else 0.0
                            nc.scalar.activation(ada[:, b, lo // D, :], ps[:, b * NC + lo // BANK, lo % BANK:lo % BANK + D],
                                                 ACT.Copy, bias=plus).then_inc(made_ada, 1)
                for b in range(B):
                    act.wait_ge(S["s2v"], b + 1)
                    link(nc.scalar.activation(c[b]["lp"], c[b]["s2v"], ACT.Ln))
                    nc.scalar.activation(c[b]["f"], c[b]["lp"], ACT.Exp, scale=-0.5).then_inc(S["f"], 1)
                for b in range(B):
                    act.wait_ge(S["v"], b + 1)
                    nc.scalar.activation(big[:, half[b], :], v[:, half[b], :], ACT.Square).then_inc(S["sq3"], 1)
                for b in range(B):
                    act.wait_ge(S["n2v"], b + 1)
                    link(nc.scalar.activation(c[b]["lp"], c[b]["n2"], ACT.Ln))
                    nc.scalar.activation(c[b]["r"], c[b]["lp"], ACT.Exp, scale=-0.5, bias=LN_A).then_inc(S["r"], 1)
                for i in range(0, NT, 2):
                    act.wait_ge(S["t"], i // 2 + 1)
                    nc.scalar.activation(
                        vT[:, :, i * P:(i + 2) * P].rearrange("p k (i t) -> p i k t", i=2),
                        ps[:, i // 2 % 8, :].rearrange("p (i k t) -> p i k t", i=2, k=KD), ACT.Copy).then_inc(S["used"], 1)

            @block.vector
            def _(dve):
                count = [0]

                def link(ins):
                    count[0] += 1
                    ins.then_inc(link_v, 1)
                    dve.wait_ge(link_v, count[0])

                V = nc.vector
                half = [slice(b * TPB, (b + 1) * TPB) for b in range(B)]
                cols = [{n: t[:, h] for n, t in col.items()} for h in half]
                if A:
                    V.memset(one[:, :], 1.0).then_inc(made, 1)
                for b, c in enumerate(cols):
                    link(V.tensor_reduce(c["sum"], x[:, half[b], :], AX.X, ALU.add))
                    V.tensor_scalar(c["mean"], c["sum"], 1.0 / D, None, ALU.mult).then_inc(S["mean"], 1)
                if A:
                    dve.wait_ge(loaded, 48)
                    V.tensor_copy(cond_b[:, :, :, :], row(cond[:, :, :], P)).then_inc(made, 1)
                for b, c in enumerate(cols):
                    dve.wait_ge(S["sq1"], b + 1)
                    link(V.tensor_reduce(c["n2"], big[:, half[b], :], AX.X, ALU.add))
                    V.tensor_scalar(c["n2"], c["n2"], EPS * EPS, None, ALU.max).then_inc(S["n2"], 1)
                    dve.wait_ge(S["mean"], b + 1)
                    V.tensor_tensor(v[:, half[b], :], x[:, half[b], :], row(c["mean"], D), ALU.subtract).then_inc(S["sq2"], 1)
                for b, c in enumerate(cols):
                    dve.wait_ge(S["norm"], b + 1)
                    V.tensor_scalar(c["m"], c["n"], MAXT, None, ALU.min).then_inc(S["m"], 1)
                for b, c in enumerate(cols):
                    dve.wait_ge(S["sq3"], b + 1)
                    link(V.tensor_reduce(c["var"], big[:, half[b], :], AX.X, ALU.add))
                    dve.wait_ge(S["logs"], b + 1)
                    link(V.tensor_tensor(c["s"], c["lp"], c["lm"], ALU.subtract))
                    link(V.scalar_tensor_tensor(c["s"], c["s"], 0.5, c["rn"], ALU.mult, ALU.mult))
                    link(V.scalar_tensor_tensor(c["s2v"], c["s"], 1.0 / D, c["s"], ALU.mult, ALU.mult))
                    link(V.tensor_tensor(c["s2v"], c["s2v"], c["var"], ALU.mult))
                    V.tensor_scalar(c["s2v"], c["s2v"], 1e-6, None, ALU.add).then_inc(S["s2v"], 1)
                if A:
                    dve.wait_ge(made_ada, B * 6)
                for b, c in enumerate(cols):
                    dve.wait_ge(S["f"], b + 1)
                    link(V.tensor_tensor(c["f"], c["f"], c["s"], ALU.mult))
                    tiles = v[:, half[b], :]
                    link(V.tensor_tensor(tiles, tiles, row(c["f"], D), ALU.mult))
                    for part, op, done in ((shift + 1, ALU.mult, link_v), (shift, ALU.add, S["v"])):
                        ins = V.tensor_tensor(tiles, tiles, ada[:, b, part, :].unsqueeze(1).broadcast_to([P, TPB, D]), op)
                        if done is link_v:
                            link(ins)
                        else:
                            ins.then_inc(done, 1)
                for b, c in enumerate(cols):
                    dve.wait_ge(S["sq3"], B + b + 1)
                    link(V.tensor_reduce(c["n2"], big[:, half[b], :], AX.X, ALU.add))
                    V.tensor_scalar(c["n2"], c["n2"], EPS * EPS, None, ALU.max).then_inc(S["n2v"], 1)
                for b, c in enumerate(cols):
                    dve.wait_ge(S["r"], b + 1)
                    link(V.tensor_scalar(c["r"], c["r"], 1.0, None, ALU.min))
                    dve.wait_ge(S["v"], b + 1)
                    V.tensor_tensor(v[:, half[b], :], v[:, half[b], :], row(c["r"], D), ALU.mult).then_inc(S["ready"], 1)

            @block.tensor
            def _(pe):
                if A:
                    pe.wait_ge(loaded, 48)
                    pe.wait_ge(made, 2)
                    for b in range(B):
                        for c in range(NC):
                            cols = slice(c * BANK, (c + 1) * BANK)
                            for k in range(KD):
                                nc.tensor.matmul(ps[:, b * NC + c, :], cond_b[:, k, b, :], w_ada[:, k, cols],
                                                 start=k == 0, stop=False)
                            nc.tensor.matmul(ps[:, b * NC + c, :], one[0:1, :], bias[0:1, cols],
                                             start=False, stop=True).then_inc(full, 1)
                for i in range(NT):
                    if i % TPB == 0:
                        pe.wait_ge(S["ready"], i // TPB + 1)
                    for k in range(KD):
                        at = (i % 2 * KD + k) * P
                        last = nc.tensor.transpose(ps[:, i // 2 % 8, at:at + P], v[:, i, k * P:(k + 1) * P], ident[:, :])
                    if i % 2:
                        last.then_inc(S["t"], 1)


def qkv(nc, sems, w, bias, ident16, vT, qT, kT, va, sq, nh):
    W3 = 3 * D
    with ExitStack() as stack:
        s = Scope(nc, stack, sems)
        one = s.sb("one_q", [1, P])
        x = s.sb("x_qkv", [P, NT, W3])
        nf = s.sb("nf", [P, NT * 3])
        pair = s.sb("pair", [P, 2, 2, H, 4, HD], F16)
        ps = s.ps("ps_qkv", [P, 3, 2, BANK])
        ps_t = s.ps("ps_t", [P, 2, 2 * BANK], F16)
        S = {n: s.sem("q_" + n) for n in "one full x sq nh nh_used lh lf alpha_f alpha scaled hi lo t used".split()}
        link_v = s.sem("q_link")
        with nc.Block() as block:

            @block.sync
            def _(sp):
                sems.clear_last(sp)

            @block.tensor
            def _(pe):
                pe.wait_ge(S["one"], 1)
                for i in range(NT):
                    if i >= 3:
                        pe.wait_ge(S["x"], 2 * (i - 2))
                    for part, (lo, hi) in enumerate(((0, BANK), (BANK, W3))):
                        out = ps[:, i % 3, part, 0:hi - lo]
                        for k in range(KD):
                            nc.tensor.matmul(out, vT[:, k, i * P:(i + 1) * P], w[:, k, lo:hi], start=k == 0, stop=False)
                        nc.tensor.matmul(out, one[0:1, :], bias[0:1, lo:hi], start=False, stop=True).then_inc(S["full"], 1)
                with pe.Fori(0, NT - 1, 2) as i0:
                    for u in range(2):
                        i = i0 + u
                        pe.wait_ge(S["lo"], i * 4 + 4)
                        for qk in range(2):
                            pe.wait_ge(S["used"], i * 2 + (qk + 2))
                            for h in range(0, H, 2):
                                last = nc.tensor.transpose(ps_t[:, qk, h // 2 * P:(h // 2 + 1) * P],
                                                           pair[:, u, qk, h:h + 2, :, :].rearrange("p h r d -> p (h r d)"),
                                                           ident16[:, :])
                            last.then_inc(S["t"], 1)

            @block.scalar
            def _(act):
                act.preload_act_table_set("natural_log_exp_and_others")
                for i in range(NT):
                    for part, (lo, hi) in enumerate(((0, BANK), (BANK, W3))):
                        act.wait_ge(S["full"], 2 * i + part + 1)
                        nc.scalar.activation(x[:, i, lo:hi], ps[:, i % 3, part, 0:hi - lo], ACT.Copy).then_inc(S["x"], 1)
                for j in range(4):
                    if j:
                        act.wait_ge(S["nh"], j)
                    act.wait_ge(S["x"], 2 * NT)
                    nc.scalar.activation(sq, x[:, j * 4:(j + 1) * 4, :], ACT.Square).then_inc(S["sq"], 1)
                act.wait_ge(S["nh_used"], 1)
                nc.scalar.activation(nh[:, :, :], nh[:, :, :], ACT.Ln).then_inc(S["lh"], 1)
                nc.scalar.activation(nf[:, :], nf[:, :], ACT.Ln).then_inc(S["lf"], 1)
                act.wait_ge(S["lh"], 1)
                act.wait_ge(S["lf"], 1)
                nc.scalar.activation(nh[:, :, :], nh[:, :, :], ACT.Exp, scale=-0.5, bias=LN_A).then_inc(S["alpha"], 1)
                nc.scalar.activation(nf[:, :], nf[:, :], ACT.Exp, scale=-0.5,
                                     bias=math.log(ATANH * R_HEADS)).then_inc(S["alpha_f"], 1)
                with act.Fori(0, NT - 1, 2) as i0:
                    for u in range(2):
                        i = i0 + u
                        for qk, dst in enumerate((qT, kT)):
                            act.wait_ge(S["t"], i * 2 + (qk + 1))
                            nc.scalar.activation(dst[:, :, bass.ds(i * P, P)],
                                                 ps_t[:, qk, :].rearrange("p (h t) -> p h t", t=P),
                                                 ACT.Copy).then_inc(S["used"], 1)

            @block.vector
            def _(dve):
                count = [0]

                def link(ins):
                    count[0] += 1
                    ins.then_inc(link_v, 1)
                    dve.wait_ge(link_v, count[0])

                dve.sem_inc(S["used"], 3)
                nc.vector.memset(one[:, :], 1.0).then_inc(S["one"], 1)
                for j in range(4):
                    dve.wait_ge(S["sq"], j + 1)
                    nc.vector.tensor_reduce(nh[:, j * 12:(j + 1) * 12, :],
                                            sq.rearrange("p i (a h d) -> p (i a) h d", a=3, d=HD),
                                            AX.X, ALU.add).then_inc(S["nh"], 1)
                dve.wait_ge(S["nh"], 4)
                link(nc.vector.tensor_reduce(nf[:, :], nh[:, :, :], AX.X, ALU.add))
                link(nc.vector.tensor_scalar(nf[:, :], nf[:, :], EPS * EPS, None, ALU.max))
                nc.vector.tensor_scalar(nh[:, :, :], nh[:, :, :], TINY, None, ALU.max).then_inc(S["nh_used"], 1)
                dve.wait_ge(S["alpha_f"], 1)
                dve.wait_ge(S["alpha"], 1)
                link(nc.vector.tensor_scalar(nf[:, :], nf[:, :], R_HEADS, None, ALU.min))
                link(nc.vector.tensor_tensor(nh[:, :, :], nh[:, :, :], row(nf[:, :], H), ALU.min))
                alpha = nh[:, :, :].rearrange("p (i a) h -> p i a h", a=3)
                with dve.Fori(0, NT - 1, 2) as i0:
                    for u in range(2):
                        i = i0 + u
                        xi = x[:, bass.ds(i, 1), :].rearrange("p i (a h d) -> p (i a) h d", a=3, d=HD)
                        ai = alpha[:, bass.ds(i, 1), :, :].rearrange("p i a h -> p (i a) h")
                        dve.wait_ge(S["used"], i * 2 + 1)
                        for qk in range(2):
                            nc.vector.scalar_tensor_tensor(xi[:, qk, :, :], xi[:, qk, :, :], QSC, row(ai[:, qk, :], HD),
                                                           ALU.mult, ALU.mult).then_inc(S["scaled"], 1)
                        nc.vector.tensor_tensor(va[:, bass.ds(i, 1), :, :].rearrange("p i h d -> p (i h) d"),
                                                xi[:, 2, :, :], row(ai[:, 2, :], HD), ALU.mult).then_inc(S["scaled"], 1)
                        dve.wait_ge(S["scaled"], (i + 1) * 3)
                        for qk in range(2):
                            for rep in range(2):
                                part = (2 * rep, rep)[qk]
                                nc.vector.tensor_scalar(pair[:, u, qk, :, part, :],
                                                        xi[:, qk, :, :],
                                                        1.0, None, ALU.mult).then_inc(S["hi"], 1)
                        dve.wait_ge(S["hi"], (i + 1) * 4)
                        for qk in range(2):
                            for rep in range(2):
                                part = (2 * rep + 1, rep + 2)[qk]
                                nc.vector.tensor_tensor(pair[:, u, qk, :, part, :],
                                                        xi[:, qk, :, :],
                                                        pair[:, u, qk, :, 0, :], ALU.subtract).then_inc(S["lo"], 1)


def attention(nc, sems, qT, kT, va, oT):
    HG = 4
    NKC = T // P
    IT = B * H // HG
    with ExitStack() as stack:
        s = Scope(nc, stack, sems)
        qs = s.sb("qs", [P, 2, HG // 2, T], F16)
        ks = s.sb("ks", [P, 2, HG // 2, T], F16)
        vs = s.sb("vs", [P, 2, NKC, HG, 32])
        pt = s.sb("pt", [P, 4, T])
        ps_s = s.ps("ps_s", [P, 2, T])
        ps_o = s.ps("ps_o2", [P, 2, T])
        S = {n: s.sem("t_" + n) for n in "pad staged stage_free s e pv out used".split()}
        NS = HG * NKC
        with nc.Block() as block:

            @block.sync
            def _(sp):
                sems.clear_last(sp)

            @block.tensor
            def _(pe):
                with pe.Fori(0, IT - 1, 2) as i0:
                    for u in range(2):
                        i = i0 + u

                        def scores(n):
                            h, kc = n // NKC, n % NKC
                            rows = slice(h % 2 * 64, h % 2 * 64 + 64)
                            pe.wait_ge(S["e"], i * NS + (n + 1))
                            for half in range(2):
                                last = nc.tensor.matmul(ps_s[:, n % 2, half * BANK:(half + 1) * BANK],
                                                        ks[rows, u, h // 2, kc * P:(kc + 1) * P],
                                                        qs[rows, u, h // 2, half * BANK:(half + 1) * BANK],
                                                        start=True, stop=True)
                            last.then_inc(S["s"], 1)

                        pe.wait_ge(S["staged"], i * 3 + 3)
                        pe.wait_ge(S["used"], i + 1)
                        scores(0)
                        scores(1)
                        for n in range(NS):
                            h, kc = n // NKC, n % NKC
                            if n + 2 < NS:
                                scores(n + 2)
                            pe.wait_ge(S["e"], i * NS + (n + 3))
                            for half in range(2):
                                last = nc.tensor.matmul(ps_o[h * 32:(h + 1) * 32, u, half * BANK:(half + 1) * BANK],
                                                        vs[:, u, kc, h, :], pt[:, n % 4, half * BANK:(half + 1) * BANK],
                                                        start=kc == 0, stop=kc == NKC - 1)
                            last.then_inc(S["pv"], 1)

            @block.scalar
            def _(act):
                act.preload_act_table(ACT.Exp)
                act.sem_inc(S["e"], 2)
                with act.Fori(0, IT - 1, 2) as i0:
                    for u in range(2):
                        i = i0 + u
                        for n in range(NS):
                            act.wait_ge(S["s"], i * NS + (n + 1))
                            act.wait_ge(S["pv"], i * NS + (n + 1))
                            nc.scalar.activation(pt[:, n % 4, :], ps_s[:, n % 2, :], ACT.Exp,
                                                 scale=0.25 / (QSC * QSC)).then_inc(S["e"], 1)

            @block.vector
            def _(dve):
                dve.sem_inc(S["pv"], 4)
                dve.sem_inc(S["used"], 2)
                nc.vector.memset(vs[:, :, :, :, HD:HD + 1], 1.0).then_inc(S["pad"], 1)
                nc.vector.memset(vs[:, :, :, :, HD + 1:], 0.0).then_inc(S["pad"], 1)
                dve.wait_ge(S["pad"], 2)

                def take_out(i):
                    b, g = i // (H // HG), i % (H // HG)
                    dve.wait_ge(S["pv"], (i + 1) * NS + 4)
                    nc.vector.tensor_copy(oT[:, g, b * T:(b + 1) * T], ps_o[:, i % 2, :]).then_inc(S["used"], 1)

                for i in range(IT):
                    b, g, u = i // (H // HG), i % (H // HG), i % 2
                    if i >= 2:
                        dve.wait_ge(S["pv"], (i - 1) * NS + 4)
                    nc.vector.tensor_copy(qs[:, u, :, :], qT[:, 2 * g:2 * g + 2, b * T:(b + 1) * T]).then_inc(S["staged"], 1)
                    nc.vector.tensor_copy(ks[:, u, :, :], kT[:, 2 * g:2 * g + 2, b * T:(b + 1) * T]).then_inc(S["staged"], 1)
                    nc.vector.tensor_copy(vs[:, u, :, :, 0:HD], va[:, b * NKC:(b + 1) * NKC, HG * g:HG * (g + 1), :])\
                      .then_inc(S["staged"], 1)
                    if i:
                        take_out(i - 1)
                take_out(IT - 1)


def heads_out(nc, sems, ident, oT, aT, v, copies):
    with ExitStack() as stack:
        s = Scope(nc, stack, sems)
        o = s.sb("o", [P, NT, H, 32])
        sq = s.sb("sq_o", [P, NT, H * HD])
        rden = s.sb("rden", [P, NT, H])
        nh = s.sb("nh_o", [P, NT, H])
        n2 = s.sb("ho_n2", [P, NT])
        ps = s.ps("ps_ot", [P, 8, BANK])
        S = {n: s.sem("h_" + n) for n in "t o sq n2h alpha sq2 v n2 r ready tt used".split()}
        link_v, link_a = s.sem("h_link_v"), s.sem("h_link_a")
        with nc.Block() as block:

            @block.sync
            def _(sp):
                sems.clear_last(sp)
                fetch(sp, sems, "h_", copies)

            @block.tensor
            def _(pe):
                for i in range(NT):
                    if i >= 8:
                        pe.wait_ge(S["o"], i - 7)
                    for g in range(4):
                        last = nc.tensor.transpose(ps[:, i % 8, g * P:(g + 1) * P], oT[:, g, i * P:(i + 1) * P], ident[:, :])
                    last.then_inc(S["t"], 1)
                pe.wait_ge(S["o"], NT)
                pe.wait_ge(S["ready"], 1)
                for i in range(NT):
                    for k in range(KD):
                        at = (i % 2 * KD + k) * P
                        last = nc.tensor.transpose(ps[:, i // 2 % 8, at:at + P], v[:, i, k * P:(k + 1) * P], ident[:, :])
                    if i % 2:
                        last.then_inc(S["tt"], 1)

            @block.scalar
            def _(act):
                act.preload_act_table_set("natural_log_exp_and_others")
                for i in range(NT):
                    act.wait_ge(S["t"], i + 1)
                    nc.scalar.activation(o[:, i, :, :].rearrange("p h d -> p (h d)"), ps[:, i % 8, :],
                                         ACT.Copy).then_inc(S["o"], 1)
                act.wait_ge(S["o"], NT)
                nc.scalar.activation(sq[:, :, :].rearrange("p i (h d) -> p (i h) d", d=HD),
                                     o[:, :, :, 0:HD].rearrange("p i h d -> p (i h) d"), ACT.Square).then_inc(S["sq"], 1)
                act.wait_ge(S["n2h"], 1)
                nc.scalar.activation(nh[:, :, :], nh[:, :, :], ACT.Ln).then_inc(link_a, 1)
                act.wait_ge(link_a, 1)
                nc.scalar.activation(nh[:, :, :], nh[:, :, :], ACT.Exp, scale=-0.5, bias=LN_A).then_inc(S["alpha"], 1)
                act.wait_ge(S["v"], 1)
                nc.scalar.activation(sq[:, :, :], v[:, :, :], ACT.Square).then_inc(S["sq2"], 1)
                act.wait_ge(S["n2"], 1)
                nc.scalar.activation(n2[:, :], n2[:, :], ACT.Ln).then_inc(link_a, 1)
                act.wait_ge(link_a, 2)
                nc.scalar.activation(n2[:, :], n2[:, :], ACT.Exp, scale=-0.5, bias=LN_A).then_inc(S["r"], 1)
                for i in range(0, NT, 2):
                    act.wait_ge(S["tt"], i // 2 + 1)
                    nc.scalar.activation(
                        aT[:, :, i * P:(i + 2) * P].rearrange("p k (i t) -> p i k t", i=2),
                        ps[:, i // 2 % 8, :].rearrange("p (i k t) -> p i k t", i=2, k=KD), ACT.Copy).then_inc(S["used"], 1)

            @block.vector
            def _(dve):
                count = [0]

                def link(ins):
                    count[0] += 1
                    ins.then_inc(link_v, 1)
                    dve.wait_ge(link_v, count[0])

                dve.wait_ge(S["o"], NT)
                link(nc.vector.reciprocal(rden[:, :, :], o[:, :, :, HD:HD + 1].rearrange("p i h d -> p i (h d)")))
                dve.wait_ge(S["sq"], 1)
                link(nc.vector.tensor_reduce(nh[:, :, :], sq[:, :, :].rearrange("p i (h d) -> p i h d", d=HD), AX.X, ALU.add))
                nc.vector.tensor_scalar(nh[:, :, :], nh[:, :, :], TINY, None, ALU.max).then_inc(S["n2h"], 1)
                dve.wait_ge(S["alpha"], 1)
                link(nc.vector.tensor_tensor(nh[:, :, :], nh[:, :, :], rden[:, :, :], ALU.min))
                link(nc.vector.tensor_scalar(nh[:, :, :], nh[:, :, :], 1.0 / R_HEADS, None, ALU.mult))
                nc.vector.tensor_tensor(v[:, :, :].rearrange("p i (h d) -> p (i h) d", d=HD),
                                        o[:, :, :, 0:HD].rearrange("p i h d -> p (i h) d"),
                                        row(nh[:, :, :].rearrange("p i h -> p (i h)"), HD), ALU.mult).then_inc(S["v"], 1)
                dve.wait_ge(S["v"], 1)
                dve.wait_ge(S["sq2"], 1)
                link(nc.vector.tensor_reduce(n2[:, :], sq[:, :, :], AX.X, ALU.add))
                nc.vector.tensor_scalar(n2[:, :], n2[:, :], EPS * EPS, None, ALU.max).then_inc(S["n2"], 1)
                dve.wait_ge(S["r"], 1)
                link(nc.vector.tensor_scalar(n2[:, :], n2[:, :], 1.0, None, ALU.min))
                nc.vector.tensor_tensor(v[:, :, :], v[:, :, :], row(n2[:, :], D), ALU.mult).then_inc(S["ready"], 1)


def project_out(nc, sems, w, bias, aT, lin):
    with ExitStack() as stack:
        s = Scope(nc, stack, sems)
        one = s.sb("one_o", [1, P])
        ps = s.ps("ps_po", [P, 8, BANK])
        made, full, out = s.sem("p_made"), s.sem("p_full"), s.sem("p_out")
        with nc.Block() as block:

            @block.sync
            def _(sp):
                sems.clear_last(sp)

            @block.tensor
            def _(pe):
                pe.wait_ge(made, 1)
                for i in range(NT):
                    if i >= 8:
                        pe.wait_ge(out, i - 7)
                    for k in range(KD):
                        nc.tensor.matmul(ps[:, i % 8, 0:D], aT[:, k, i * P:(i + 1) * P], w[:, k, :], start=k == 0, stop=False)
                    nc.tensor.matmul(ps[:, i % 8, 0:D], one[0:1, :], bias[0:1, :], start=False, stop=True).then_inc(full, 1)

            @block.vector
            def _(dve):
                nc.vector.memset(one[:, :], 1.0).then_inc(made, 1)
                for i in range(NT):
                    dve.wait_ge(full, i + 1)
                    nc.vector.tensor_copy(lin[:, i, :], ps[:, i % 8, 0:D]).then_inc(out, 1)
                dve.wait_ge(out, NT)


def hyper_residual(nc, sems, tag, x, lin, ada, gate, out, copies):
    with ExitStack() as stack:
        s = Scope(nc, stack, sems)
        sq = s.sb(tag + "sq", [P, NT, D])
        sx = s.sb(tag + "sx", [P, NT, D])
        w = s.sb(tag + "w", [P, NT, D])
        col = {n: s.sb(tag + n, [P, NT])[:, :] for n in "nl x2 w2 xw rho n rn th tau y2 xy num den c1 c2".split()}
        link_v, link_a = s.sem(tag + "link_v"), s.sem(tag + "link_a")
        S = {n: s.sem(tag + n) for n in "sl nl rho sx x2 w sw n2 n xw xws th c1 yw".split()}
        with nc.Block() as block:

            @block.sync
            def _(sp):
                sems.clear_last(sp)
                fetch(sp, sems, tag, copies)

            @block.scalar
            def _(act):
                count = [0]

                def link(ins):
                    count[0] += 1
                    ins.then_inc(link_a, 1)
                    act.wait_ge(link_a, count[0])

                act.preload_act_table_set("natural_log_exp_and_others")
                half = [slice(b * TPB, (b + 1) * TPB) for b in range(B)]
                cols = [{n: t[:, h] for n, t in col.items()} for h in half]
                for b in range(B):
                    nc.scalar.activation(sq[:, half[b], :], lin[:, half[b], :], ACT.Square).then_inc(S["sl"], 1)
                    nc.scalar.activation(sx[:, half[b], :], x[:, half[b], :], ACT.Square).then_inc(S["sx"], 1)
                for b, c in enumerate(cols):
                    act.wait_ge(S["nl"], b + 1)
                    link(nc.scalar.activation(c["rho"], c["nl"], ACT.Ln))
                    nc.scalar.activation(c["rho"], c["rho"], ACT.Exp, scale=-0.5, bias=LN_A).then_inc(S["rho"], 1)
                    act.wait_ge(S["w"], b + 1)
                    nc.scalar.activation(sq[:, half[b], :], w[:, half[b], :], ACT.Square).then_inc(S["sw"], 1)
                for b, c in enumerate(cols):
                    act.wait_ge(S["n2"], b + 1)
                    link(nc.scalar.activation(c["th"], c["n"], ACT.Ln))
                    link(nc.scalar.activation(c["rn"], c["th"], ACT.Exp, scale=-0.5))
                    link(nc.scalar.activation(c["n"], c["th"], ACT.Exp, scale=0.5))
                for b, c in enumerate(cols):
                    nc.scalar.activation(c["th"], c["n"], ACT.Tanh).then_inc(S["th"], 1)

            @block.gpsimd
            def _(pool):
                for b in range(B):
                    tiles = slice(b * TPB, (b + 1) * TPB)
                    pool.wait_ge(S["x2"], b + 1)
                    pool.wait_ge(S["w"], b + 1)
                    nc.gpsimd.tensor_tensor(sx[:, tiles, :], x[:, tiles, :], w[:, tiles, :], ALU.mult).then_inc(S["xw"], 1)

            @block.vector
            def _(dve):
                count = [0]

                def link(ins):
                    count[0] += 1
                    ins.then_inc(link_v, 1)
                    dve.wait_ge(link_v, count[0])

                V = nc.vector
                half = [slice(b * TPB, (b + 1) * TPB) for b in range(B)]
                cols = [{n: t[:, h] for n, t in col.items()} for h in half]
                for b, c in enumerate(cols):
                    dve.wait_ge(S["sl"], b + 1)
                    link(V.tensor_reduce(c["nl"], sq[:, half[b], :], AX.X, ALU.add))
                    V.tensor_scalar(c["nl"], c["nl"], EPS * EPS, None, ALU.max).then_inc(S["nl"], 1)
                    V.tensor_tensor(w[:, half[b], :], lin[:, half[b], :],
                                    ada[:, b, gate, :].unsqueeze(1).broadcast_to([P, TPB, D]), ALU.mult).then_inc(S["w"], 1)
                    dve.wait_ge(S["sx"], b + 1)
                    V.tensor_reduce(c["x2"], sx[:, half[b], :], AX.X, ALU.add).then_inc(S["x2"], 1)
                for b, c in enumerate(cols):
                    dve.wait_ge(S["sw"], b + 1)
                    link(V.tensor_reduce(c["w2"], sq[:, half[b], :], AX.X, ALU.add))
                    dve.wait_ge(S["rho"], b + 1)
                    link(V.tensor_scalar(c["rho"], c["rho"], 1.0, None, ALU.min))
                    link(V.tensor_tensor(c["n"], c["rho"], c["rho"], ALU.mult))
                    link(V.tensor_tensor(c["n"], c["n"], c["w2"], ALU.mult))
                    V.tensor_scalar(c["n"], c["n"], EPS * EPS, None, ALU.max).then_inc(S["n2"], 1)
                for b, c in enumerate(cols):
                    dve.wait_ge(S["xw"], b + 1)
                    V.tensor_reduce(c["xw"], sx[:, half[b], :], AX.X, ALU.add).then_inc(S["xws"], 1)
                for b, c in enumerate(cols):
                    dve.wait_ge(S["th"], b + 1)
                    link(V.tensor_tensor(c["tau"], c["th"], c["rn"], ALU.mult))
                    link(V.tensor_tensor(c["tau"], c["tau"], c["rho"], ALU.mult))
                    dve.wait_ge(S["xws"], b + 1)
                    link(V.tensor_tensor(c["xy"], c["tau"], c["xw"], ALU.mult))
                    link(V.tensor_tensor(c["y2"], c["tau"], c["tau"], ALU.mult))
                    link(V.tensor_tensor(c["y2"], c["y2"], c["w2"], ALU.mult))
                    link(V.tensor_scalar(c["xy"], c["xy"], 2.0, 1.0, ALU.mult, ALU.add))
                    link(V.tensor_tensor(c["num"], c["xy"], c["y2"], ALU.add))
                    link(V.tensor_tensor(c["den"], c["x2"], c["y2"], ALU.mult))
                    link(V.tensor_tensor(c["den"], c["den"], c["xy"], ALU.add))
                    link(V.tensor_scalar(c["den"], c["den"], EPS, None, ALU.max))
                    link(V.reciprocal(c["den"], c["den"]))
                    V.tensor_tensor(c["c1"], c["num"], c["den"], ALU.mult).then_inc(S["c1"], 1)
                    link(V.tensor_scalar(c["c2"], c["x2"], -1.0, 1.0, ALU.mult, ALU.add))
                    link(V.tensor_tensor(c["c2"], c["c2"], c["tau"], ALU.mult))
                    link(V.tensor_tensor(c["c2"], c["c2"], c["den"], ALU.mult))
                    V.tensor_tensor(w[:, half[b], :], w[:, half[b], :], row(c["c2"], D), ALU.mult).then_inc(S["yw"], 1)
                    dve.wait_ge(S["c1"], b + 1)
                    link(V.tensor_tensor(sq[:, half[b], :], x[:, half[b], :], row(c["c1"], D), ALU.mult))
                    dve.wait_ge(S["yw"], b + 1)
                    link(V.tensor_tensor(out[:, half[b], :], sq[:, half[b], :], w[:, half[b], :], ALU.add))


def feed_forward(nc, sems, weights, vT, lin):
    L, FC = BANK, FF // P
    TL = L // P
    with ExitStack() as stack:
        s = Scope(nc, stack, sems)
        w1, w2, b1, b2 = weights
        b2_all = s.sb("b2_all", [P, D])
        ones = s.sb("ones_f", [P, P])
        h = s.sb("h_f", [P, FC, L])
        sq = s.sb("sq_f", [P, FC, L])
        nrow = s.sb("nrow", [1, N])
        n2 = s.sb("ff_n2", [P, NT])
        ps_h = s.ps("ps_h", [P, 2, BANK])
        ps_n = s.ps("ps_n", [P, 2, BANK])
        ps_o = s.ps("ps_fo", [P, TL, BANK])
        S = {n: s.sem("f_" + n) for n in "ones h h_in sq n nrow out out_used ncol b2 b2_in lo n2 ln r".split()}
        NB = N // L
        with nc.Block() as block:

            @block.sync
            def _(sp):
                sems.clear_last(sp)

            @block.tensor
            def _(pe):
                pe.wait_ge(S["ones"], 1)
                nc.tensor.matmul(ps_n[:, 1, 0:D], ones[0:1, :], b2[0:1, :], start=True, stop=True).then_inc(S["b2"], 1)
                with pe.Fori(0, NB) as q:
                    for c in range(FC):
                        pe.wait_ge(S["h_in"], q * FC + (c + 1))
                        for k in range(KD):
                            last = nc.tensor.matmul(ps_h[:, c % 2, :], w1[:, k, c * P:(c + 1) * P],
                                                    vT[:, k, bass.ds(q * L, L)], start=k == 0, stop=k == KD - 1)
                        last.then_inc(S["h"], 1)
                    pe.wait_ge(S["h_in"], q * FC + (FC + 2))
                    pe.wait_ge(S["out_used"], q * TL + TL)
                    for m in range(TL):
                        for c in range(FC):
                            last = nc.tensor.matmul(ps_o[:, m, 0:D], h[:, c, m * P:(m + 1) * P], w2[:, c, :],
                                                    start=c == 0, stop=c == FC - 1)
                        last.then_inc(S["out"], 1)
                    pe.wait_ge(S["nrow"], q + 1)
                    for c in range(FC):
                        pe.wait_ge(S["sq"], q * FC + (c + 1))
                        last = nc.tensor.matmul(ps_n[0:1, 0, :], ones[:, 0:1], sq[:, c, :], start=c == 0, stop=c == FC - 1)
                    last.then_inc(S["n"], 1)
                pe.wait_ge(S["nrow"], NB + 1)
                pe.wait_ge(S["b2_in"], 1)
                for i in range(NT):
                    last = nc.tensor.matmul(ps_n[:, 1, i:i + 1], nrow[0:1, i * P:(i + 1) * P], ones[0:1, 0:1],
                                            start=True, stop=True)
                last.then_inc(S["ncol"], 1)

            @block.scalar
            def _(act):
                act.preload_act_table_set("natural_log_exp_and_others")
                act.sem_inc(S["h_in"], 2)
                act.sem_inc(S["nrow"], 1)
                with act.Fori(0, NB) as q:
                    for c in range(FC):
                        act.wait_ge(S["h"], q * FC + (c + 1))
                        if c == 0:
                            act.wait_ge(S["lo"], q * TL + TL)
                        nc.scalar.activation(h[:, c, :], ps_h[:, c % 2, :], ACT.Identity,
                                             bias=b1[:, c:c + 1]).then_inc(S["h_in"], 1)
                    act.wait_ge(S["n"], q + 1)
                    nc.scalar.activation(nrow[0:1, bass.ds(q * L, L)], ps_n[0:1, 0, :], ACT.Copy).then_inc(S["nrow"], 1)
                act.wait_ge(S["n2"], 1)
                nc.scalar.activation(n2[:, :], n2[:, :], ACT.Ln).then_inc(S["ln"], 1)
                act.wait_ge(S["ln"], 1)
                nc.scalar.activation(n2[:, :], n2[:, :], ACT.Exp, scale=-0.5, bias=LN_A).then_inc(S["r"], 1)

            @block.vector
            def _(dve):
                nc.vector.memset(ones[:, :], 1.0).then_inc(S["ones"], 1)
                dve.sem_inc(S["out_used"], TL)
                dve.sem_inc(S["lo"], TL)
                dve.wait_ge(S["b2"], 1)
                nc.vector.tensor_copy(b2_all[:, :], ps_n[:, 1, 0:D]).then_inc(S["b2_in"], 1)
                with dve.Fori(0, NB) as q:
                    for c in range(FC):
                        dve.wait_ge(S["h_in"], q * FC + (c + 3))
                        nc.vector.tensor_tensor(sq[:, c, :], h[:, c, :], h[:, c, :], ALU.mult).then_inc(S["sq"], 1)
                    dve.wait_ge(S["n"], q + 1)
                    for m in range(TL):
                        dve.wait_ge(S["out"], q * TL + (m + 1))
                        nc.vector.tensor_scalar(lin[:, bass.ds(q * TL + m, 1), :], ps_o[:, m, 0:D], 1.0, None,
                                                ALU.mult).then_inc(S["out_used"], 1)
                        dve.sem_inc(S["lo"], 1)
                dve.wait_ge(S["ncol"], 1)
                nc.vector.tensor_scalar(n2[:, :], ps_n[:, 1, 0:NT], EPS * EPS, None, ALU.max).then_inc(S["n2"], 1)
                dve.wait_ge(S["r"], 1)
                nc.vector.tensor_scalar(n2[:, :], n2[:, :], 1.0, None, ALU.min).then_inc(S["b2_in"], 1)
                dve.wait_ge(S["b2_in"], 2)
                dve.wait_ge(S["out_used"], (NB + 1) * TL)
                nc.vector.tensor_tensor(lin[:, :, :], lin[:, :, :], row(n2[:, :], D), ALU.mult).then_inc(S["b2_in"], 1)
                dve.wait_ge(S["b2_in"], 3)
                nc.vector.tensor_tensor(lin[:, :, :], lin[:, :, :], b2_all[:, :].unsqueeze(1).broadcast_to([P, NT, D]),
                                        ALU.add).then_inc(S["b2_in"], 1)
                dve.wait_ge(S["b2_in"], 4)


def glu_ffn(nc, sems, weights, ident, x1, x3, out):
    L, FC = BANK, FF // P
    TL = L // P
    with ExitStack() as stack:
        s = Scope(nc, stack, sems)
        xT = s.sb("x3T", [P, KD, N])
        w1, w2, h1, h2, w3, sc, s3 = weights
        s3_all = s.sb("g_s3_all", [P, D])
        one = s.sb("g_one", [1, P])
        sil = s.sb("g_sil", [P, 2, L])
        ha = s.sb("g_ha", [P, FC, L])
        hb = s.sb("g_hb", [P, FC, L])
        y = s.sb("g_y", [P, 2, TL, D])
        ps = s.ps("ps_glu", [P, 8, BANK])
        t_done = s.sem("g_t")
        xT_in, s3_in, s3_ps, one_in = s.sem("g_xT"), s.sem("g_s3_in"), s.sem("g_s3_ps"), s.sem("g_one_in")
        S = {n: s.sem("g_" + n) for n in "a b sil glu l1 ga l2 gb o y1 y stored0 stored1".split()}
        NB = N // L
        with nc.Block() as block:

            @block.sync
            def _(sp):
                sems.clear_last(sp)
                out_v = out.rearrange("(q m p) d -> p q m d", p=P, m=TL)
                with sp.Fori(0, NB - 1, 2) as q0:
                    for u in range(2):
                        q = q0 + u
                        sp.wait_ge(S["y"], (q + 1) * TL)
                        sp.dma_start(out_v[:, bass.ds(q, 1), :, :].rearrange("p q m d -> p (q m) d"),
                                     y[:, u, :, :]).then_inc(S[f"stored{u}"], 16)
                for u in range(2):
                    sp.wait_ge(S[f"stored{u}"], 16 + 16 * NB // 2)

            @block.tensor
            def _(pe):
                for i in range(NT):
                    for k in range(KD):
                        at = (i % 2 * KD + k) * P
                        last = nc.tensor.transpose(ps[:, i // 2 % 8, at:at + P], x3[:, i, k * P:(k + 1) * P], ident[:, :])
                    if i % 2:
                        last.then_inc(t_done, 1)
                pe.wait_ge(one_in, 1)
                pe.sem_inc(S["o"], 1)
                pe.wait_ge(xT_in, NT // 2)
                nc.tensor.matmul(ps[:, 0, 0:D], one[0:1, :], s3[0:1, :], start=True, stop=True).then_inc(s3_ps, 1)
                pe.wait_ge(s3_in, 1)
                with pe.Fori(0, NB) as q:
                    for c in range(FC):
                        pe.wait_ge(S["glu"], q * FC + (c + 1))
                        for w, at, done in ((w1, 0, "a"), (w2, 1, "b")):
                            for k in range(KD):
                                last = nc.tensor.matmul(ps[:, c % 2 * 2 + at, :], w[:, k, c * P:(c + 1) * P],
                                                        xT[:, k, bass.ds(q * L, L)], start=k == 0, stop=k == KD - 1)
                            last.then_inc(S[done], 1)
                    for w, src, before, done, after, bank in ((h1, ha, "glu", "l1", "ga", 4), (h2, hb, "ga", "l2", "gb", 6)):
                        pe.wait_ge(S[before], q * FC + (FC + 2))
                        for c in range(FC):
                            pe.wait_ge(S[after], q * FC + (c + 1))
                            for k in range(FC):
                                last = nc.tensor.matmul(ps[:, bank + c % 2, :], w[:, k, c * P:(c + 1) * P], src[:, k, :],
                                                        start=k == 0, stop=k == FC - 1)
                            last.then_inc(S[done], 1)
                    pe.wait_ge(S["gb"], q * FC + (FC + 2))
                    for m in range(TL):
                        for c in range(FC):
                            last = nc.tensor.matmul(ps[:, m, 0:D], ha[:, c, m * P:(m + 1) * P], w3[:, c, :],
                                                    start=c == 0, stop=c == FC - 1)
                        last.then_inc(S["o"], 1)
                    pe.wait_ge(S["y1"], (q + 1) * TL)

            @block.scalar
            def _(act):
                for i in range(0, NT, 2):
                    act.wait_ge(t_done, i // 2 + 1)
                    nc.scalar.activation(
                        xT[:, :, i * P:(i + 2) * P].rearrange("p k (i t) -> p i k t", i=2),
                        ps[:, i // 2 % 8, :].rearrange("p (i k t) -> p i k t", i=2, k=KD), ACT.Copy).then_inc(xT_in, 1)
                act.sem_inc(S["ga"], 2)
                act.sem_inc(S["gb"], 2)
                with act.Fori(0, NB) as q:
                    for c in range(FC):
                        act.wait_ge(S["a"], q * FC + (c + 1))
                        act.wait_ge(S["glu"], q * FC + (c + 1))
                        nc.scalar.activation(sil[:, c % 2, :], ps[:, c % 2 * 2, :], ACT.Silu,
                                             scale=sc[:, 0, c:c + 1]).then_inc(S["sil"], 1)
                    for c in range(FC):
                        act.wait_ge(S["l1"], q * FC + (c + 1))
                        nc.scalar.activation(hb[:, c, :], ps[:, 4 + c % 2, :], ACT.Gelu,
                                             scale=sc[:, 2, c:c + 1]).then_inc(S["ga"], 1)
                    for c in range(FC):
                        act.wait_ge(S["l2"], q * FC + (c + 1))
                        nc.scalar.activation(ha[:, c, :], ps[:, 6 + c % 2, :], ACT.Gelu,
                                             scale=sc[:, 3, c:c + 1]).then_inc(S["gb"], 1)

            @block.vector
            def _(dve):
                nc.vector.memset(one[:, :], 1.0).then_inc(one_in, 1)
                dve.wait_ge(s3_ps, 1)
                nc.vector.tensor_copy(s3_all[:, :], ps[:, 0, 0:D]).then_inc(s3_in, 1)
                dve.wait_ge(s3_in, 1)
                dve.sem_inc(S["glu"], 2)
                dve.sem_inc(S["stored0"], 16)
                dve.sem_inc(S["stored1"], 16)
                with dve.Fori(0, NB - 1, 2) as q0:
                    for u in range(2):
                        q = q0 + u
                        for c in range(FC):
                            dve.wait_ge(S["sil"], q * FC + (c + 1))
                            dve.wait_ge(S["b"], q * FC + (c + 1))
                            if c == 0:
                                dve.wait_ge(S["o"], q * TL + 1)
                            nc.vector.scalar_tensor_tensor(ha[:, c, :], ps[:, c % 2 * 2 + 1, :], sc[:, 1, c:c + 1],
                                                           sil[:, c % 2, :], ALU.mult, ALU.mult).then_inc(S["glu"], 1)
                        dve.wait_ge(S[f"stored{u}"], q0 * 8 + 16)
                        for m in range(TL):
                            dve.wait_ge(S["o"], q * TL + (m + 2))
                            nc.vector.tensor_tensor(y[:, u, m, :], ps[:, m, 0:D], s3_all[:, :], ALU.mult).then_inc(S["y1"], 1)
                            dve.wait_ge(S["y1"], q * TL + (m + 1))
                            nc.vector.tensor_tensor(y[:, u, m, :], y[:, u, m, :],
                                                    x1[:, bass.ds(q * TL + m, 1), :].rearrange("p i d -> p (i d)"),
                                                    ALU.add).then_inc(S["y"], 1)


def hyperbolic_block(nc, sems, A, ident, x1, x3, last_copies):
    rows_of = lambda name: A[name].rearrange("(k p) n -> p k n", p=P)
    with ExitStack() as stack:
        s = Scope(nc, stack)
        ada = s.sb("ada", [P, B, 6, D])
        with ExitStack() as inner:
            heads = ExitStack()
            s2 = Scope(nc, heads)
            va = s2.sb("va", [P, NT, H, HD], side="right")
            qT = s2.sb("qT", [P, H // 2, N], F16, side="right")
            kT = s2.sb("kT", [P, H // 2, N], F16, side="right")
            with ExitStack() as first:
                s3 = Scope(nc, first)
                vT = s3.sb("vT", [P, KD, N])
                ident16 = s3.sb("ident16", [P, P], F16)
                scratch = x3[:, :, :].rearrange("p i d -> p (i d)")
                sums = 4 * 3 * D
                w_qkv = s3.sb("w_qkv", [P, KD, 3 * D])
                b_qkv = s3.sb("b_qkv", [1, 3 * D])
                norm_modulate(nc, sems, "n1_", x1, ada, 0, ident, vT,
                              ((w_qkv[:, :, :], rows_of("w_qkv")), (b_qkv[:, :], A["b_qkv"]), (ident16[:, :], A["ident16"])), A)
                qkv(nc, sems, w_qkv, b_qkv, ident16, vT, qT, kT, va, scratch[:, 0:sums].rearrange("p (i n) -> p i n", i=4),
                    scratch[:, sums:sums + NT * 3 * H].rearrange("p (i h) -> p i h", h=H))
            oT = Scope(nc, inner).sb("oT", [P, 4, N])
            attention(nc, sems, qT, kT, va, oT)
            heads.close()
            aT = Scope(nc, inner).sb("aT", [P, KD, N])
            w_o = Scope(nc, inner).sb("w_o", [P, KD, D])
            b_o = Scope(nc, inner).sb("b_o", [1, D])
            heads_out(nc, sems, ident, oT, aT, x3, ((w_o[:, :, :], rows_of("w_o")), (b_o[:, :], A["b_o"])))
            project_out(nc, sems, w_o, b_o, aT, x3)
        lin = s.sb("lin", [P, NT, D])
        hyper_residual(nc, sems, "r1_", x1, x3, ada, 2, x3, ())
        with ExitStack() as inner:
            s2 = Scope(nc, inner)
            vT = s2.sb("vT2", [P, KD, N])
            weights = [s2.sb(name, shape) for name, shape in (
                ("w_f1", [P, KD, FF]), ("w_f2", [P, FF // P, D]), ("b_f1", [P, FF // P]), ("b_f2", [1, D]))]
            norm_modulate(nc, sems, "n2_", x3, ada, 3, ident, vT,
                          tuple(zip((w[:] for w in weights), (rows_of("w_f1"), rows_of("w_f2"), A["b_f1"], A["b_f2"]))))
            feed_forward(nc, sems, weights, vT, lin)
        hyper_residual(nc, sems, "r2_", x3, lin, ada, 5, x3, last_copies())


def build(nc, A, out):
    sems = Semaphores(nc)
    with ExitStack() as stack:
        s = Scope(nc, stack)
        ident = s.sb("ident", [P, P])
        x1 = s.sb("x1", [P, NT, D])
        with ExitStack() as inner:
            s2 = Scope(nc, inner)
            hist = s2.sb("hist", [P, T, KD, B])
            xw = s2.sb("xw", [P, T, G8 * B])
            wq = s2.sb("wq", [P, 2, KD, 4 * D], F16)
            gate_scale = s2.sb("gate_scale", [P, 1])
            weights = [s2.sb(name, [P] + shape) for name, shape in (
                ("w_in", [KD, 2 * DI]), ("conv_w", [CI, DCONV]), ("conv_b", [CI]), ("w_dt", [CI]), ("b_dt", [CI]),
                ("w_x", [CI, 2 * DS + 1]), ("norm_w", [KD]), ("ones", [P]),
                ("a_neg", [CI, DS]), ("d_par", [CI]), ("w_out", [CI, D]))]
            w_in, conv_w, conv_b, w_dt, b_dt, w_x, norm_w, ones, a_neg, d_par, w_out = weights
            copies = [(w[:], A[name]) for w, name in (
                (conv_w, "conv_w"), (conv_b, "conv_b"), (w_dt, "w_dt"), (b_dt, "b_dt"), (norm_w, "norm_w"),
                (a_neg, "a_log"), (d_par, "d_par"))]
            copies += [(w[:], A[name].rearrange("(k p) n -> p k n", p=P)) for w, name in (
                (w_in, "w_in"), (w_x, "w_x"), (w_out, "w_out"), (x1, "x"))]
            lstm_inputs(nc, sems, A, xw, wq, gate_scale, ident, copies)
            make_weights(nc, sems, weights)
            lstm_mamba(nc, sems, A, xw, wq, gate_scale, ident, hist, x1, weights)
        x3 = s.sb("x3", [P, NT, D])
        glu = []

        def glu_copies():
            rows_of = lambda name: A[name].rearrange("(k p) n -> p k n", p=P)
            for name, shape, src in (
                    ("g_w1", [P, KD, FF], rows_of("w1T")), ("g_w2", [P, KD, FF], rows_of("w2T")),
                    ("g_h1", [P, FF // P, FF], rows_of("h1T")), ("g_h2", [P, FF // P, FF], rows_of("h2T")),
                    ("g_w3", [P, FF // P, D], rows_of("w3T")), ("g_sc", [P, 4, FF // P], A["ffn_s"]), ("g_s3", [1, D], A["w3_s"])):
                glu.append((s.sb(name, shape, side="right"), src))
            return [(w[:], src) for w, src in glu]

        hyperbolic_block(nc, sems, A, ident, x1, x3, glu_copies)
        glu_ffn(nc, sems, [w for w, _ in glu], ident, x1, x3, out)



def kernel(**inputs):
    import concourse.bacc as bacc
    from concourse.bass_utils import run_bass_kernel_spmd

    a = {k.replace("L0_", ""): np.asarray(v) for k, v in inputs.items()}

    def chunks(v):
        v = v.reshape((-1, P) + v.shape[1:])
        return np.moveaxis(v, 0, 1)

    def gates(w):
        return np.concatenate([w[..., 0:2 * D], w[..., 3 * D:4 * D], w[..., 2 * D:3 * D]], axis=-1)

    x = a["x"].reshape(N, D)
    arrays = {
        "x": x, "xT": x.T, "condT": a["cond_1024"].T,
        "Wx": gates(a["cond_Wx"]), "Wh": gates(a["cond_Wh"]), "b": chunks(gates(a["cond_b"])),
        "ident": np.eye(P, dtype=np.float32), "ident16": np.eye(P, dtype=np.float16),
        "norm_w": chunks(a["attn_norm_w"]), "w_in": a["attn_W_in"], "conv_w": chunks(a["attn_conv_w"][:, 0, :]),
        "conv_b": chunks(a["attn_conv_b"]), "w_x": a["attn_W_x"], "w_dt": chunks(a["attn_w_dt"]),
        "b_dt": chunks(a["attn_b_dt"]), "a_log": chunks(a["attn_A_log"]), "d_par": chunks(a["attn_D_param"]),
        "w_out": a["attn_W_out"],
        "w_qkv": np.concatenate([a["cond2_w_q"], a["cond2_w_k"], a["cond2_w_v"]], axis=1),
        "b_qkv": np.concatenate([a["cond2_b_q"], a["cond2_b_k"], a["cond2_b_v"]])[None, :],
        "w_o": a["cond2_w_o"], "b_o": a["cond2_b_o"][None, :], "w_f1": a["cond2_w_f1"], "b_f1": chunks(a["cond2_b_f1"]),
        "w_f2": a["cond2_w_f2"], "b_f2": a["cond2_b_f2"][None, :], "w_ada": a["cond2_w_ada"], "b_ada": a["cond2_b_ada"][None, :],
        "w1T": a["ffn_w1_w"].T, "w2T": a["ffn_w2_w"].T, "h1T": a["ffn_h1_w"].T, "h2T": a["ffn_h2_w"].T, "w3T": a["ffn_w3_w"].T,
        "w3_s": a["ffn_w3_s"][None, :],
        "ffn_s": np.stack([chunks(a["ffn_" + n]) for n in ("w1_s", "w2_s", "h1_s", "h2_s")], axis=1),
    }
    arrays = {f"in_{k}": np.ascontiguousarray(v) for k, v in arrays.items()}
    nc = bacc.Bacc("TRN2", target_bir_lowering=False, num_devices=1)
    A = {k[3:]: nc.dram_tensor(k, v.shape, mybir.dt.from_np(v.dtype), kind="ExternalInput").ap() for k, v in arrays.items()}
    out = nc.dram_tensor("out_0_dram", (N, D), F32, kind="ExternalOutput").ap()
    build(nc, A, out)
    r = run_bass_kernel_spmd(nc, [arrays], core_ids=[0])
    return r.results[0]["out_0_dram"].reshape(B, T, D)
```
